# Optimizing a Trainium2 kernel written in Bass

```python
import numpy as np
import jax
import jax.numpy as jnp

def _softmax(x, axis=-1):
    return jax.nn.softmax(x, axis=axis)

def _gelu(x):
    return jax.nn.gelu(x, approximate=True)

def _silu(x):
    return jax.nn.silu(x)

def _sigmoid(x):
    return jax.nn.sigmoid(x)

def _layernorm(x, axis=-1, eps=1e-05):
    m = jnp.mean(x, axis=axis, keepdims=True)
    v = jnp.var(x, axis=axis, keepdims=True)
    return (x - m) / jnp.sqrt(v + eps)

def _scatter_add(tgt, idx, src, axis=0):
    return tgt.at[idx].add(src)

def _segment_sum(src, seg, n):
    return jax.ops.segment_sum(src, seg, n)
kernel_name = 'mk_flamingo_gated_d2_seqx_r4_74a497'

def setup_inputs(seed: int=0):
    np.random.seed(seed)
    _w = jnp.asarray

    def _rec_inputs():
        import jax
        import jax.numpy as jnp
        _rk = jax.random.key(seed)
        x = -0.0002928 + 1 * jax.random.normal(jax.random.fold_in(_rk, 1), (8, 100, 256), jnp.float32)
        _lenS = 100 - jax.random.randint(jax.random.fold_in(_rk, 7), (8,), 0, max(1, 100 // 4) + 1, jnp.int32)
        _lenS2 = 361 - jax.random.randint(jax.random.fold_in(_rk, 8), (8,), 0, max(1, 361 // 4) + 1, jnp.int32)
        _ctx_1024P = jax.random.normal(jax.random.fold_in(_rk, 11), (8, 16, 256), jnp.float32)
        _ctx_1024c = jax.random.dirichlet(jax.random.fold_in(_rk, 511), 0.3 * jnp.ones((16,), jnp.float32), (8, 361))
        _ctx_1024t = jnp.einsum('bsk,bkd->bsd', _ctx_1024c, _ctx_1024P)
        _ctx_1024t = _ctx_1024t * jax.lax.rsqrt(jnp.mean(jnp.square(_ctx_1024t)) + 1e-12) * 0.953939
        ctx_1024 = -1.39393e-06 + 0.999914 * (_ctx_1024t + 0.3 * jax.random.normal(jax.random.fold_in(_rk, 611), (8, 361, 256), jnp.float32))
        fside_1x1xSxS2_0 = 0.000376506 + 0.999991 * jax.random.normal(jax.random.fold_in(_rk, 12), (1, 1, 100, 361), jnp.float32)
        _validS = jnp.arange(100)[None, :] < _lenS[:, None]
        _validS2 = jnp.arange(361)[None, :] < _lenS2[:, None]
        _causal = jnp.tril(jnp.ones((100, 100), dtype=bool))
        mask_Bx1x1xS2_ik0 = jnp.where(jnp.broadcast_to(_validS2[:, None, None, :], (8, 1, 1, 361)), 0, 1).astype(jnp.int32)
        _g = jax.random.normal(jax.random.fold_in(_rk, 9001), (2, 2), jnp.float32)
        _g = jnp.sign(_g) * jnp.maximum(jnp.abs(_g), 1.0) + (_g == 0) * 1.0
        g_xattn = _g[0]
        g_ffn = _g[1]
        return (x, ctx_1024, fside_1x1xSxS2_0, mask_Bx1x1xS2_ik0, g_xattn, g_ffn)
    x, ctx_1024, fside_1x1xSxS2_0, mask_Bx1x1xS2_ik0, g_xattn, g_ffn = _rec_inputs()

    def _L0_xattn_setup():
        import jax, jax.numpy as jnp
        import numpy as np
        HIDDEN = 256
        HEADS = 16
        DEPTH = HIDDEN // HEADS
        B, F, T = (2, 512, 512)
        key = jax.random.key(seed)
        ks = jax.random.split(key, 7)
        return {'query_input': jax.random.normal(ks[0], (B, F, HIDDEN), dtype=jnp.float32), 'source_input': jax.random.normal(ks[1], (B, T, HIDDEN), dtype=jnp.float32), 'bias': jax.random.normal(ks[2], (1, 1, F, T), dtype=jnp.float32), 'wq': jax.random.normal(ks[3], (HIDDEN, HEADS, DEPTH), dtype=jnp.float32) * 0.02, 'wk': jax.random.normal(ks[4], (HIDDEN, HEADS, DEPTH), dtype=jnp.float32) * 0.02, 'wv': jax.random.normal(ks[5], (HIDDEN, HEADS, DEPTH), dtype=jnp.float32) * 0.02, 'wo': jax.random.normal(ks[6], (HEADS, DEPTH, HIDDEN), dtype=jnp.float32) * 0.02}
    _L0_xattn_all = _L0_xattn_setup()
    _L0_xattn_in = {k: v for k, v in _L0_xattn_all.items() if k in ('wq', 'wk', 'wv', 'wo')}
    del _L0_xattn_all

    def _L0_ffn_setup():
        import jax, jax.numpy as jnp
        import numpy as np
        D_MODEL = 256
        D_FF = 1024
        N_EXPERTS = 8
        D_EXPERT = D_FF // N_EXPERTS
        TOP_K = 2
        LB_WEIGHT = 0.01
        B, S = (4, 512)

        def _top_k_softmax(logits, k):
            vals, _ = jax.lax.top_k(logits, k)
            thresh = vals[..., -1:]
            masked = jnp.where(logits >= thresh, logits, -jnp.inf)
            return jax.nn.softmax(masked, axis=-1)
        key = jax.random.key(seed)
        ks = jax.random.split(key, 8)
        x = jax.random.normal(ks[0], (B, S, D_MODEL), dtype=jnp.float32)
        w1 = jax.random.normal(ks[1], (N_EXPERTS, D_MODEL, D_EXPERT), dtype=jnp.float32) * (1.0 / np.sqrt(D_MODEL))
        b1 = jnp.zeros((N_EXPERTS, D_EXPERT), dtype=jnp.float32)
        w2 = jax.random.normal(ks[2], (N_EXPERTS, D_EXPERT, D_MODEL), dtype=jnp.float32) * (1.0 / np.sqrt(D_EXPERT))
        b2 = jnp.zeros((N_EXPERTS, D_MODEL), dtype=jnp.float32)
        centroids = jax.random.normal(ks[3], (N_EXPERTS, D_MODEL), dtype=jnp.float32) * 0.02
        w_route = jax.random.normal(ks[4], (N_EXPERTS, D_MODEL), dtype=jnp.float32) * (1.0 / np.sqrt(D_MODEL))
        return {'x': x, 'w1': w1, 'b1': b1, 'w2': w2, 'b2': b2, 'centroids': centroids, 'w_route': w_route}
    _L0_ffn_all = _L0_ffn_setup()
    _L0_ffn_in = {k: v for k, v in _L0_ffn_all.items() if k in ('w1', 'b1', 'w2', 'b2', 'centroids', 'w_route')}
    del _L0_ffn_all

    def _L1_xattn_setup():
        import jax, jax.numpy as jnp
        import numpy as np
        D_MODEL = 256
        NUM_HEADS = 16
        DEPTH = D_MODEL // NUM_HEADS
        NEG_INF = -1000000000.0

        def _split_heads(x):
            B, S, _ = x.shape
            return x.reshape(B, S, NUM_HEADS, DEPTH).transpose(0, 2, 1, 3)
        key = jax.random.key(seed)
        ks = jax.random.split(key, 12)
        B, S = (4, 512)
        scale = 1.0 / np.sqrt(D_MODEL)
        inp = {'q': jax.random.normal(ks[0], (B, S, D_MODEL), jnp.float32), 'k': jax.random.normal(ks[1], (B, S, D_MODEL), jnp.float32), 'v': jax.random.normal(ks[2], (B, S, D_MODEL), jnp.float32), 'mask': jax.random.randint(ks[3], (B, 1, 1, S), 0, 2, jnp.int32), 'wq': jax.random.normal(ks[4], (D_MODEL, D_MODEL), jnp.float32) * scale, 'bq': jnp.zeros((D_MODEL,), jnp.float32), 'wk': jax.random.normal(ks[5], (D_MODEL, D_MODEL), jnp.float32) * scale, 'bk': jnp.zeros((D_MODEL,), jnp.float32), 'wv': jax.random.normal(ks[6], (D_MODEL, D_MODEL), jnp.float32) * scale, 'bv': jnp.zeros((D_MODEL,), jnp.float32), 'wo': jax.random.normal(ks[7], (D_MODEL, D_MODEL), jnp.float32) * scale, 'bo': jnp.zeros((D_MODEL,), jnp.float32)}
        return inp
    _L1_xattn_all = _L1_xattn_setup()
    _L1_xattn_in = {k: v for k, v in _L1_xattn_all.items() if k in ('wq', 'bq', 'wk', 'bk', 'wv', 'bv', 'wo', 'bo')}
    del _L1_xattn_all

    def _L1_ffn_setup():
        import jax, jax.numpy as jnp
        import numpy as np
        E, D, DFF = (8, 256, 1024)
        key = jax.random.key(seed)
        ks = jax.random.split(key, 10)
        s = 0.02
        return {'x': jax.random.normal(ks[0], (4, 512, D), dtype=jnp.float32), 'Wr': jax.random.normal(ks[1], (D, E), dtype=jnp.float32) * s, 'br': jnp.zeros((E,), dtype=jnp.float32), 'W1': jax.random.normal(ks[2], (E, D, DFF), dtype=jnp.float32) * s, 'b1': jnp.zeros((E, DFF), dtype=jnp.float32), 'W2': jax.random.normal(ks[3], (E, D, DFF), dtype=jnp.float32) * s, 'b2': jnp.zeros((E, DFF), dtype=jnp.float32), 'W3': jax.random.normal(ks[4], (E, DFF, D), dtype=jnp.float32) * s, 'b3': jnp.zeros((E, D), dtype=jnp.float32)}
    _L1_ffn_all = _L1_ffn_setup()
    _L1_ffn_in = {k: v for k, v in _L1_ffn_all.items() if k in ('Wr', 'br', 'W1', 'b1', 'W2', 'b2', 'W3', 'b3')}
    del _L1_ffn_all
    return {'x': x, 'ctx_1024': ctx_1024, 'fside_1x1xSxS2_0': fside_1x1xSxS2_0, 'mask_Bx1x1xS2_ik0': mask_Bx1x1xS2_ik0, 'g_xattn': g_xattn, 'g_ffn': g_ffn, 'L0_xattn_wq': _L0_xattn_in['wq'], 'L0_xattn_wk': _L0_xattn_in['wk'], 'L0_xattn_wv': _L0_xattn_in['wv'], 'L0_xattn_wo': _L0_xattn_in['wo'], 'L0_ffn_w1': _L0_ffn_in['w1'], 'L0_ffn_b1': _L0_ffn_in['b1'], 'L0_ffn_w2': _L0_ffn_in['w2'], 'L0_ffn_b2': _L0_ffn_in['b2'], 'L0_ffn_centroids': _L0_ffn_in['centroids'], 'L0_ffn_w_route': _L0_ffn_in['w_route'], 'L1_xattn_wq': _L1_xattn_in['wq'], 'L1_xattn_bq': _L1_xattn_in['bq'], 'L1_xattn_wk': _L1_xattn_in['wk'], 'L1_xattn_bk': _L1_xattn_in['bk'], 'L1_xattn_wv': _L1_xattn_in['wv'], 'L1_xattn_bv': _L1_xattn_in['bv'], 'L1_xattn_wo': _L1_xattn_in['wo'], 'L1_xattn_bo': _L1_xattn_in['bo'], 'L1_ffn_Wr': _L1_ffn_in['Wr'], 'L1_ffn_br': _L1_ffn_in['br'], 'L1_ffn_W1': _L1_ffn_in['W1'], 'L1_ffn_b1': _L1_ffn_in['b1'], 'L1_ffn_W2': _L1_ffn_in['W2'], 'L1_ffn_b2': _L1_ffn_in['b2'], 'L1_ffn_W3': _L1_ffn_in['W3'], 'L1_ffn_b3': _L1_ffn_in['b3']}

def reference(x, ctx_1024, fside_1x1xSxS2_0, mask_Bx1x1xS2_ik0, g_xattn, g_ffn, L0_xattn_wq, L0_xattn_wk, L0_xattn_wv, L0_xattn_wo, L0_ffn_w1, L0_ffn_b1, L0_ffn_w2, L0_ffn_b2, L0_ffn_centroids, L0_ffn_w_route, L1_xattn_wq, L1_xattn_bq, L1_xattn_wk, L1_xattn_bk, L1_xattn_wv, L1_xattn_bv, L1_xattn_wo, L1_xattn_bo, L1_ffn_Wr, L1_ffn_br, L1_ffn_W1, L1_ffn_b1, L1_ffn_W2, L1_ffn_b2, L1_ffn_W3, L1_ffn_b3):
    import jax
    import jax.numpy as jnp

    def _L0_xattn_ref(query_input, source_input, bias, wq, wk, wv, wo):
        import jax, jax.numpy as jnp
        import numpy as np
        HIDDEN = 256
        HEADS = 16
        DEPTH = HIDDEN // HEADS
        B, F, T = (2, 512, 512)
        q = jnp.einsum('bfc,cnh->bfnh', query_input, wq)
        k = jnp.einsum('btc,cnh->btnh', source_input, wk)
        v = jnp.einsum('btc,cnh->btnh', source_input, wv)
        q = q * DEPTH ** (-0.5)
        logits = jnp.einsum('btnh,bfnh->bnft', k, q)
        logits = logits + bias
        weights = jax.nn.softmax(logits, axis=3)
        attn = jnp.einsum('bnft,btnh->bfnh', weights, v)
        out = jnp.einsum('bfnh,nhe->bfe', attn, wo)
        return out

    def _L0_ffn_ref(x, w1, b1, w2, b2, centroids, w_route):
        import jax, jax.numpy as jnp
        import numpy as np
        D_MODEL = 256
        D_FF = 1024
        N_EXPERTS = 8
        D_EXPERT = D_FF // N_EXPERTS
        TOP_K = 2
        LB_WEIGHT = 0.01
        B, S = (4, 512)

        def _top_k_softmax(logits, k):
            vals, _ = jax.lax.top_k(logits, k)
            thresh = vals[..., -1:]
            masked = jnp.where(logits >= thresh, logits, -jnp.inf)
            return jax.nn.softmax(masked, axis=-1)
        eps = 1e-12
        x_norm = x / jnp.maximum(jnp.linalg.norm(x, axis=-1, keepdims=True), eps)
        c_norm = centroids / jnp.maximum(jnp.linalg.norm(centroids, axis=-1, keepdims=True), eps)
        cos_scores = jnp.einsum('bsd,ed->bse', x_norm, c_norm)
        route_scores = jnp.einsum('bsd,ed->bse', x, w_route)
        logits = cos_scores + route_scores
        gates = _top_k_softmax(logits, TOP_K)
        h = jax.nn.gelu(jnp.einsum('bsd,edh->bseh', x, w1) + b1, approximate=False)
        expert_out = jnp.einsum('bseh,ehd->bsed', h, w2) + b2
        out = jnp.einsum('bse,bsed->bsd', gates, expert_out)
        return out

    def _L1_xattn_ref(q, k, v, mask, wq, bq, wk, bk, wv, bv, wo, bo):
        import jax, jax.numpy as jnp
        import numpy as np
        D_MODEL = 256
        NUM_HEADS = 16
        DEPTH = D_MODEL // NUM_HEADS
        NEG_INF = -1000000000.0

        def _split_heads(x):
            B, S, _ = x.shape
            return x.reshape(B, S, NUM_HEADS, DEPTH).transpose(0, 2, 1, 3)
        B, S, _ = q.shape
        qh = _split_heads(q @ wq + bq)
        kh = _split_heads(k @ wk + bk)
        vh = _split_heads(v @ wv + bv)
        logits = jnp.einsum('bhqd,bhkd->bhqk', qh, kh) / jnp.sqrt(jnp.asarray(DEPTH, jnp.float32))
        logits = logits + mask.astype(jnp.float32) * NEG_INF
        weights = jax.nn.softmax(logits, axis=-1)
        attn = jnp.einsum('bhqk,bhkd->bhqd', weights, vh)
        attn = attn.transpose(0, 2, 1, 3).reshape(B, S, D_MODEL)
        return attn @ wo + bo

    def _L1_ffn_ref(x, Wr, br, W1, b1, W2, b2, W3, b3):
        import jax, jax.numpy as jnp
        import numpy as np
        E, D, DFF = (8, 256, 1024)
        b, s, d = x.shape
        xt = x.reshape(b * s, d)
        logits = xt @ Wr + br
        pr, idx = jax.lax.top_k(logits, 2)
        w = jax.nn.softmax(pr, axis=-1)
        onehot = jax.nn.one_hot(idx, W1.shape[0], dtype=x.dtype)
        cw = jnp.einsum('tk,tke->te', w, onehot)
        y = jnp.zeros_like(xt)
        for e in range(W1.shape[0]):
            h = jax.nn.silu(xt @ W1[e] + b1[e]) * (xt @ W2[e] + b2[e])
            y = y + (h @ W3[e] + b3[e]) * cw[:, e:e + 1]
        return y.reshape(b, s, d)
    x = x + jnp.tanh(g_xattn[0]) * _L0_xattn_ref(_layernorm(x, axis=-1), ctx_1024, fside_1x1xSxS2_0, L0_xattn_wq, L0_xattn_wk, L0_xattn_wv, L0_xattn_wo)
    x = x + jnp.tanh(g_ffn[0]) * _L0_ffn_ref(_layernorm(x, axis=-1), L0_ffn_w1, L0_ffn_b1, L0_ffn_w2, L0_ffn_b2, L0_ffn_centroids, L0_ffn_w_route)
    x = x + jnp.tanh(g_xattn[1]) * _L1_xattn_ref(_layernorm(x, axis=-1), ctx_1024, ctx_1024, mask_Bx1x1xS2_ik0, L1_xattn_wq, L1_xattn_bq, L1_xattn_wk, L1_xattn_bk, L1_xattn_wv, L1_xattn_bv, L1_xattn_wo, L1_xattn_bo)
    x = x + jnp.tanh(g_ffn[1]) * _L1_ffn_ref(_layernorm(x, axis=-1), L1_ffn_Wr, L1_ffn_br, L1_ffn_W1, L1_ffn_b1, L1_ffn_W2, L1_ffn_b2, L1_ffn_W3, L1_ffn_b3)
    return x

_drawn_inputs = setup_inputs


def setup_inputs(seed=0):
    import zlib

    import numpy as np

    out = dict(_drawn_inputs(seed))
    spreads = {'g_ffn': (-1.0, 0.6),
     'L0_ffn_b1': (0.0, 0.1),
     'L0_ffn_b2': (0.0, 0.1),
     'L1_xattn_bq': (0.0, 0.434),
     'L1_xattn_bk': (0.0, 0.8),
     'L1_xattn_bv': (0.0, 0.1),
     'L1_xattn_bo': (0.0, 0.1),
     'L1_ffn_br': (0.0, 0.327),
     'L1_ffn_b1': (0.0, 0.8),
     'L1_ffn_b2': (0.0, 0.8),
     'L1_ffn_b3': (0.0, 0.1)}
    factors = {'fside_1x1xSxS2_0': 3.944,
     'L0_xattn_wq': 8.0,
     'L0_xattn_wk': 8.0,
     'L1_ffn_W1': 3.233,
     'L1_ffn_W2': 3.185,
     'L1_ffn_W3': 3.036}
    for name, (base, spread) in spreads.items():
        noise = np.random.default_rng([zlib.crc32(name.encode()), seed]).standard_normal(out[name].shape)
        drawn = base * np.exp(spread * noise) if base else spread * noise
        out[name] = jnp.asarray(drawn.astype(out[name].dtype))
    for name, factor in factors.items():
        out[name] = (out[name] * factor).astype(out[name].dtype)
    return out
```

```python
from contextlib import ExitStack

import concourse.bass as bass
from concourse import mybir

ALU = mybir.AluOpType
ACT = mybir.ActivationFunctionType
F32 = mybir.dt.float32
F32R = mybir.dt.float32r
I32 = mybir.dt.int32
U32 = mybir.dt.uint32
AX = mybir.AxisListType

B, S, D = 8, 100, 256
NK = 361
KT = [128, 128, NK - 256]
H, DH = 16, 16
DT = D // 128
E = 8
HID = 128
FF = 1024
FT = FF // 128
HALF = 4 * S
LN_EPS = 1e-5
NEG_INF = -1000000000.0
UNITS = 12


def attention_order(layer):
    n0 = layer * B
    order = []

    def context(n):
        return [("CT", n, 0), ("CT", n, 1)], [("KP", n, 0), ("KP", n, 1)], [("VP", n, 0), ("VP", n, 1), ("VP", n, 2)]

    for part in context(n0):
        order += part
    order += [("SN", n0, h) for h in range(H)] + [("MT", n0)]
    for part in context(n0 + 1):
        order += part
    for b in range(B):
        n = n0 + b
        heads = [("SN", n + 1, h) for h in range(H)] if b + 1 < B else []
        for u in range(UNITS):
            order.append(("ST", n, u))
            if heads:
                order += heads[:2]
                heads = heads[2:]
            if u >= 2:
                order.append(("PV", n, u - 2))
            if b >= 1:
                order += {2: [("O1", n - 1)], 5: [("O2", n - 1)], 7: [("O3", n - 1)]}.get(u, [])
            if b + 2 < B:
                transposes, keys, values = context(n + 2)
                order += {3: transposes, 6: keys, 9: values}.get(u, [])
            if u == 8 and b + 1 < B:
                order.append(("MT", n + 1))
        order += [("PV", n, UNITS - 2), ("PV", n, UNITS - 1), ("OE", n)]
    order += [("O1", n0 + B - 1), ("O2", n0 + B - 1), ("O3", n0 + B - 1)]
    return order


def norm_order(s):
    return [("LS", s)] + [("LX", s, b) for b in range(B)]


def query_order(layer):
    return [("Q", layer, half, rt) for half in range(2) for rt in range(2)]


def ffn0_order():
    order = [("R", 0), ("GT", 0, 0), ("GT", 0, 1)] + [("GB", 0, b) for b in range(B)]
    steps = [(e, half) for e in range(E) for half in range(2)]
    for i, (e, half) in enumerate(steps):
        order.append(("H0", e, half))
        if i >= 1:
            pe, ph = steps[i - 1]
            order += [("Y0", pe, ph * 4 + j) for j in range(4)]
    order += [("Y0", E - 1, 4 + j) for j in range(4)]
    return order


def ffn1_order():
    order = [("R", 1), ("GT", 1, 0), ("GT", 1, 1)] + [("GB", 1, b) for b in range(B)]
    steps = [(e, half) for e in range(E) for half in range(2)]
    for i, (e, half) in enumerate(steps):
        for f in range(FT):
            order.append(("H1", e, half, f))
            if e + 1 < E and half == 1 and f < 6:
                order.append(("W", e + 1, f))
            if i >= 1 and f % 2 == 1:
                pe, ph = steps[i - 1]
                order.append(("Y1", pe, ph * 4 + f // 2))
    order += [("Y1", E - 1, 4 + j) for j in range(4)]
    return order


def gated_layers(nc, x, ctx, fside, mask, g_xattn, g_ffn, w0, f0, w1, f1, out):
    prep = [("PB", 0), ("PB", 1), ("PM", 0), ("PF", 0), ("PC", 0)]
    order = ([("AW", 0)] + norm_order(0) + prep + query_order(0) + attention_order(0)[:7] + [("AW", 1)]
             + attention_order(0)[7:]
             + [("V", c) for c in range(4)] + norm_order(1) + ffn0_order()
             + norm_order(2) + query_order(1) + attention_order(1)
             + [("W", 0, c) for c in range(6)] + norm_order(3) + ffn1_order())
    shared = [s for s in order if s[0] in ("PB", "PM", "PF", "PC", "LX", "Q", "CT", "KP", "VP", "MT",
                                           "O1", "O2", "O3", "R", "GT", "GB")]
    job = {s: i for i, s in enumerate(shared)}
    high_order = {s: i for i, s in enumerate([s for s in shared if s[0] in ("LX", "Q", "CT", "KP", "MT", "O2")])}

    st = ExitStack()

    def sb(name, shape, dt=F32, stack=None):
        return (stack or st).enter_context(nc.sbuf_tensor(name, shape, dt))

    def sem(name):
        return st.enter_context(nc.semaphore(name))

    bank = [st.enter_context(nc.psum_tensor(f"bank{i}", [128, 512], F32)) for i in range(8)]

    def misc(step):
        return bank[6 + job[step] % 2]

    xres = sb("xres", [S, B, D])
    xT = [sb("xT_hi", [128, DT, B * S], F32R), sb("xT_lo", [128, DT, B * S], F32R)]
    xn = sb("xn", [S, 2, D])
    stats = sb("stats", [S, B, 6])
    mv = sb("mv", [S, B, 2])
    rs = sb("rs", [S, 4, B])
    ssq = sb("ssq", [S, B])
    sqj = sb("sqj", [S, D])
    ident = sb("ident", [128, 128])
    tg = sb("tg", [128, 4])
    b12T = sb("b12T", [128, 128])
    colT = sb("colT", [128, 12])
    rows8 = sb("rows8", [E, 2, D])
    rt_raw = sb("rt_raw", [128, DT, 24])
    rtw = [sb("rt_hi", [128, DT, 24], F32R), sb("rt_lo", [128, DT, 24], F32R)]
    brb = sb("brb", [S, E])
    lg = sb("lg", [S, B, 16])
    gw = sb("gw", [S, 7, B, E])
    gate = sb("gate", [S, B, E])
    iota_i = sb("iota_i", [S, E], I32)
    iota8 = sb("iota8", [S, E])
    idx = sb("idx", [S, B, 8], U32)
    gT = sb("gT", [E, B * S])
    nat = sb("nat", [128, 128])
    nat2 = sb("nat2", [12, 128])
    cw = sb("cw", [E, 2, D])
    crs = sb("crs", [E, 6])

    at = ExitStack()
    w_raw = sb("w_raw", [128, 4, DT, D], F32, at)
    w_at = [[sb(f"w{l}_{p}", [128, 4, DT, D], F32R, at) for p in ("hi", "lo")] for l in range(2)]
    bvb = sb("bvb", [128, D], F32, at)
    bob = sb("bob", [S, D], F32, at)
    fnat = sb("fnat", [S, NK], F32, at)
    fT = sb("fT", [128, 3, S], F32, at)
    mnat_i = sb("mnat_i", [B, NK], I32, at)
    mnat = sb("mnat", [B, NK], F32, at)
    maskT = sb("maskT", [128, 3, B], F32, at)
    mrow_i = sb("mrow_i", [S, 2, NK], I32, at)
    mrow = sb("mrow", [S, 2, NK], F32, at)
    hmask = sb("hmask", [128, 8], F32, at)
    cnat = sb("cnat", [128, 2, 3, D], F32, at)
    vA = [sb(f"v{i}", [128, 3, H, 32], F32, at) for i in range(3)]
    mx = sb("mx", [S, 2, 48], F32, at)
    nm = sb("nm", [48, S], F32R, at)
    dg = [sb(f"dg{i}", [48, H, S], F32R, at) for i in range(2)]
    ones = sb("ones", [48, 128], F32R, at)
    onesf = sb("onesf", [48, 128], F32, at)
    cT = [sb("c_hi", [128, DT, NK + 1], F32R, at), sb("c_lo", [128, DT, NK + 1], F32R, at)]
    a1 = ExitStack()
    qT = [sb("q_hi", [128, 2, B * S], F32R, a1), sb("q_lo", [128, 2, B * S], F32R, a1)]
    qm = [[sb(f"qm{i}_{p}", [128, 2, 8, S], F32R, a1) for p in ("hi", "lo")] for i in range(2)]
    kT = [[sb(f"k{i}_{p}", [128, 2, NK + 1], F32R, a1) for p in ("hi", "lo")] for i in range(3)]
    junk = sb("junk", [S, 2, NK], F32, a1)
    sbias = sb("sbias", [128, 3, 4 * S], F32, a1)
    pT = sb("pT", [128, 4, 4 * S], F32, a1)
    pv = sb("pv", [128, 4, S], F32, a1)
    rden = sb("rden", [S, H], F32, a1)
    an = sb("an", [S, D], F32, a1)
    aT = [sb("a_hi", [128, 2, S], F32R, a1), sb("a_lo", [128, 2, S], F32R, a1)]
    a1.close()
    m0 = ExitStack()
    e0_raw = sb("e0_raw", [128, 2, E, 256], F32, m0)
    e0 = [sb("e0_hi", [128, 2, E, 256], F32R, m0), sb("e0_lo", [128, 2, E, 256], F32R, m0)]
    h0 = sb("h0", [128, 2, HALF], F32, m0)
    h0s = [sb("h0_hi", [128, 2, HALF], F32R, m0), sb("h0_lo", [128, 2, HALF], F32R, m0)]
    m0.close()
    at.close()
    m1 = ExitStack()
    NRAW = 4
    e1_raw = sb("e1_raw", [128, NRAW, 1024], F32, m1)
    e1 = [[sb(f"e1{i}_{p}", [128, 6, 1024], F32R, m1) for p in ("hi", "lo")] for i in range(2)]
    s1b = sb("s1b", [128, 2, HALF], F32, m1)
    h1f = sb("h1f", [128, 2, HALF], F32, m1)
    h1s = [sb("h1_hi", [128, 2, FT, HALF], F32R, m1), sb("h1_lo", [128, 2, FT, HALF], F32R, m1)]
    m1.close()

    loaded_x, loaded_small, out_done = sem("loaded_x"), sem("loaded_small"), sem("out_done")
    loaded_w = [sem("loaded_w0"), sem("loaded_w1")]
    loaded_ctx = [sem("loaded_ctx0"), sem("loaded_ctx1")]
    loaded_mask = [sem("loaded_mask0"), sem("loaded_mask1")]
    loaded_e0 = sem("loaded_e0")
    loaded_raw = [sem(f"loaded_raw{i}") for i in range(NRAW)]
    pool_const, pool_step, dve_step, dve_prep = sem("pool_const"), sem("pool_step"), sem("dve_step"), sem("dve_prep")
    tanh_done, var_ready, sqrt_done = sem("tanh_done"), sem("var_ready"), sem("sqrt_done")
    w_high, w_split, xn_ready = sem("w_high"), sem("w_split"), sem("xn_ready")
    product, high_done, split_done = sem("product"), sem("high_done"), sem("split_done")
    qm_ready, mrow_ready = sem("qm_ready"), sem("mrow_ready")
    sn_ready, max_done, max_twice, dg_ready = sem("sn_ready"), sem("max_done"), sem("max_twice"), sem("dg_ready")
    st_ready, biased, exp_done, pv_done, pv_out = (sem("st_ready"), sem("biased"), sem("exp_done"), sem("pv_done"),
                                                   sem("pv_out"))
    an_ready, attn_done, moe_done = sem("an_ready"), sem("attn_done"), sem("moe_done")
    v_high, v_split, shifted, exp_gate, gates_ready = (sem("v_high"), sem("v_split"), sem("shifted"),
                                                       sem("exp_gate"), sem("gates_ready"))
    h_ready, h_act, h_made, h_high, h_split = sem("h_ready"), sem("h_act"), sem("h_made"), sem("h_high"), sem("h_split")
    y_ready, y_added = sem("y_ready"), sem("y_added")
    r_high, r_split = sem("r_high"), sem("r_split")

    N_SMALL = 17
    w3v = f1["W3"].rearrange("e (j p) d -> e p j d", p=128)

    def piece_source(e, c):
        if c < 4:
            return f1["W1" if c < 2 else "W2"][e, 128 * (c % 2):128 * (c % 2) + 128, :]
        return w3v[e, :, 4 * (c - 4):4 * (c - 4) + 4, :]

    block = st.enter_context(nc.Block())

    @block.sync
    def _(sp):
        def load_context(n):
            b = n % B
            if n >= 2:
                sp.wait_ge(product, job[("CT", n - 2, 1)] + 1)
            sp.dma_start(cnat[:, n % 2, 0:2], ctx[b, 0:256].rearrange("(t p) d -> p t d", p=128))\
                .then_inc(loaded_ctx[n % 2], 16)
            sp.dma_start(cnat[0:KT[2], n % 2, 2], ctx[b, 256:NK]).then_inc(loaded_ctx[n % 2], 16)

        def load_mask(n):
            if n >= B + 2:
                sp.wait_ge(mrow_ready, n - B - 1)
            sp.dma_start(mrow_i[:, n % 2], mask[n % B, 0].to_broadcast((S, NK))).then_inc(loaded_mask[n % 2], 16)

        def load_weights(l, w):
            for i, name in enumerate(("wq", "wk", "wv", "wo")):
                sp.dma_start(w_raw[:, i], w[name].rearrange("(k p) n -> p k n", p=128)).then_inc(loaded_w[l], 16)

        sp.dma_start(xres[:], x.rearrange("b s d -> s b d")).then_inc(loaded_x, 16)
        load_weights(0, w0)
        load_context(0)
        small = [(nat[0:64, :], f1["b1"].rearrange("e (f p) -> (e f) p", p=128)),
                 (nat[64:128, :], f1["b2"].rearrange("e (f p) -> (e f) p", p=128)),
                 (nat2[0:8, :], f0["b1"]),
                 (nat2[8:10, :], w1["bq"].rearrange("(a p) -> a p", p=128)),
                 (nat2[10:12, :], w1["bk"].rearrange("(a p) -> a p", p=128)),
                 (rows8[:, 0, :], f0["b2"]), (rows8[:, 1, :], f1["b3"]),
                 (cw[:, 0, :], f0["centroids"]), (cw[:, 1, :], f0["w_route"]),
                 (rt_raw[:, :, 16:24], f1["Wr"].rearrange("(k p) e -> p k e", p=128)),
                 (brb[:], f1["br"].rearrange("(a e) -> a e", a=1).to_broadcast((S, E))),
                 (tg[:, 0:2], g_xattn.rearrange("(a e) -> a e", a=1).to_broadcast((128, 2))),
                 (tg[:, 2:4], g_ffn.rearrange("(a e) -> a e", a=1).to_broadcast((128, 2))),
                 (fnat[:], fside[0, 0]), (mnat_i[:], mask.rearrange("b u v k -> (b u v) k")),
                 (bvb[:], w1["bv"].rearrange("(a e) -> a e", a=1).to_broadcast((128, D))),
                 (bob[:], w1["bo"].rearrange("(a e) -> a e", a=1).to_broadcast((S, D)))]
        assert len(small) == N_SMALL
        for dst, src in small:
            sp.dma_start(dst, src).then_inc(loaded_small, 16)
        load_context(1)
        sp.wait_ge(w_split, 1)
        load_weights(1, w1)
        for n in range(2, 2 * B):
            if n == B + 2:
                sp.wait_ge(attn_done, 1)
                sp.dma_start(e0_raw[:, 0].rearrange("p e (k h) -> p (e k) h", k=2),
                             f0["w1"].rearrange("e (k p) h -> p (e k) h", p=128)).then_inc(loaded_e0, 16)
                sp.dma_start(e0_raw[:, 1], f0["w2"].rearrange("e p d -> p e d")).then_inc(loaded_e0, 16)
                load_mask(B)
                load_mask(B + 1)
            load_context(n)
            if n >= B + 2:
                load_mask(n)
        sp.wait_ge(attn_done, 2)
        for c in range(6 * E):
            if c >= NRAW:
                sp.wait_ge(r_split, c - NRAW + 1)
            dst = e1_raw[:, c % NRAW]
            if c % 6 >= 4:
                dst = dst.rearrange("p (j d) -> p j d", j=4)
            sp.dma_start(dst, piece_source(c // 6, c % 6)).then_inc(loaded_raw[c % NRAW], 16)
        sp.wait_ge(moe_done, 2)
        sp.dma_start(out.rearrange("b s d -> s b d"), xres[:]).then_inc(out_done, 16)
        sp.wait_ge(out_done, 16)

    @block.gpsimd
    def _(pool):
        steps = [0]

        def after(ins):
            steps[0] += 1
            ins.then_inc(pool_step, 1)
            pool.wait_ge(pool_step, steps[0])

        after(pool.memset(ident[:], 0.0))
        after(pool.affine_select(out=ident[:], in_=ident[:], compare_op=ALU.not_equal, fill=1.0, base=0,
                                 pattern=[[-1, 128]], channel_multiplier=1))
        after(pool.memset(hmask[:], 1.0))
        after(pool.affine_select(out=hmask[:], in_=hmask[:], compare_op=ALU.is_ge, fill=0.0, base=0,
                                 pattern=[[-DH, 8]], channel_multiplier=1))
        after(pool.affine_select(out=hmask[:], in_=hmask[:], compare_op=ALU.is_ge, fill=0.0, base=DH - 1,
                                 pattern=[[DH, 8]], channel_multiplier=-1))
        after(pool.iota(iota_i[:], pattern=[[1, E]], base=0, channel_multiplier=0))
        for i in range(3):
            after(pool.memset(vA[i][:], 0.0))
            after(pool.memset(vA[i][:, :, :, DH:DH + 1], 1.0))
        for i in range(2):
            after(pool.memset(dg[i][:].bitcast(F32), 0.0))
        for part in cT:
            after(pool.memset(part[:, :, NK:NK + 1].bitcast(F32), 0.0))
        after(pool.memset(onesf[:], 1.0))
        after(pool.tensor_copy(ones[:], onesf[:]))
        pool.memset(mx[:], 0.0).then_inc(pool_const, 1)

        def masked_queries(n, rt):
            b = n % B
            pool.wait_ge(split_done, job[("Q", n // B, b // 4, rt)] + 1)
            if n >= 2:
                pool.wait_ge(st_ready, UNITS * (n - 2) + 6 * (rt + 1))
            for p in range(2):
                last = pool.tensor_tensor(
                    qm[n % 2][p][:, rt],
                    qT[p][:, rt, b * S:(b + 1) * S].bitcast(F32).unsqueeze(1).to_broadcast((128, 8, S)),
                    hmask[:].unsqueeze(2).to_broadcast((128, 8, S)), ALU.mult)
            last.then_inc(qm_ready, 1)
            pool.wait_ge(qm_ready, 2 * n + rt + 1)

        def mask_row(n):
            pool.wait_ge(loaded_mask[n % 2], 16 * ((n - B) // 2 + 1))
            if n >= B + 2:
                pool.wait_ge(max_done, H * (n - 1))
            pool.tensor_scalar(mrow[:, n % 2], mrow_i[:, n % 2], NEG_INF, None, ALU.mult).then_inc(mrow_ready, 1)

        def diagonal(n):
            pool.wait_ge(split_done, job[("MT", n)] + 1)
            if n >= 2:
                pool.wait_ge(st_ready, UNITS * (n - 1))
            for r in (0, 32):
                ins = pool.affine_select(
                    out=dg[n % 2][r:r + H], in_=nm[r:r + H].bitcast(F32).unsqueeze(1).to_broadcast((H, H, S)),
                    compare_op=ALU.is_equal, fill=0.0, base=0, pattern=[[-1, H], [0, S]], channel_multiplier=1)
                if r == 0:
                    after(ins)
            ins.then_inc(dg_ready, 1)
            pool.wait_ge(dg_ready, n + 1)

        def split_hidden0(i):
            pool.wait_ge(h_act, i + 1)
            if i >= 2:
                pool.wait_ge(y_ready, 4 * (i - 1))
            after(pool.tensor_copy(h0s[0][:, i % 2], h0[:, i % 2]))
            pool.tensor_tensor(h0s[1][:, i % 2], h0[:, i % 2], h0s[0][:, i % 2].bitcast(F32), ALU.subtract)\
                .then_inc(h_split, 1)

        for l in range(2):
            n0 = l * B
            for n in (n0, n0 + 1):
                masked_queries(n, 0)
                masked_queries(n, 1)
                if l == 1:
                    mask_row(n)
            diagonal(n0)
            for n in range(n0 + 2, n0 + B):
                masked_queries(n, 0)
                diagonal(n - 1)
                masked_queries(n, 1)
                if l == 1:
                    mask_row(n)
            diagonal(n0 + B - 1)
            if l == 0:
                for i in range(2 * E):
                    split_hidden0(i)
        for k in range(2 * E * FT):
            pool.wait_ge(h_high, k + 1)
            step, f = k // FT, k % FT
            pool.tensor_tensor(h1s[1][:, step % 2, f], h1f[:, k % 2], h1s[0][:, step % 2, f].bitcast(F32),
                               ALU.subtract).then_inc(h_split, 1)

    Y0N = 4 * 2 * E
    R16 = 2 * E

    @block.tensor
    def _(pe):
        def begin(step):
            if job[step] >= 2:
                pe.wait_ge(split_done, job[step] - 1)
            return misc(step)

        def done(step):
            pe.wait_ge(split_done, job[step] + 1)

        def split_matmul(dst, pairs, first=True, last=True):
            for i, ((ah, al), (bh, bl)) in enumerate(pairs):
                for j, (a, b) in enumerate(((ah, bh), (ah, bl), (al, bh))):
                    ins = pe.matmul(dst, a, b, start=first and i == 0 and j == 0,
                                    stop=last and i == len(pairs) - 1 and j == 2)
            return ins

        def both(parts, *ix):
            return tuple(p[ix] for p in parts)

        A = slice(None)
        w_seen = set()

        def step_prep(s):
            dst = begin(s)
            if s == ("PB", 0):
                pe.wait_ge(loaded_small, 16 * N_SMALL)
                pe.wait_ge(pool_const, 1)
                ins = pe.transpose(dst[:, 0:128], nat[:], ident[:])
            elif s == ("PB", 1):
                ins = pe.transpose(dst[:, 0:12], nat2[:], ident[0:12, 0:12])
            elif s[0] == "PM":
                pe.wait_ge(dve_prep, 1)
                for t in range(3):
                    ins = pe.transpose(dst[0:KT[t], 8 * t:8 * t + 8], mnat[:, 128 * t:128 * t + KT[t]], ident[0:8, 0:8])
            elif s[0] == "PF":
                for t in range(3):
                    ins = pe.transpose(dst[0:KT[t], S * t:S * t + S], fnat[:, 128 * t:128 * t + KT[t]],
                                       ident[0:S, 0:S])
            else:
                pe.wait_ge(dve_prep, 2)
                for k in range(DT):
                    for j in range(2):
                        c = 16 * k + 8 * j
                        ins = pe.transpose(dst[:, c:c + 8], cw[:, j, 128 * k:128 * k + 128], ident[0:8, 0:8])
            ins.then_inc(product, 1)

        def norm_transposes(s):
            dst = begin(s)
            _, i, b = s
            pe.wait_ge(pool_const, 1)
            pe.wait_ge(xn_ready, B * i + b + 1)
            for k in range(DT):
                ins = pe.transpose(dst[:, k * S:(k + 1) * S], xn[:, b % 2, 128 * k:128 * k + 128], ident[0:S, 0:S])
            ins.then_inc(product, 1)

        def queries(s):
            dst = begin(s)
            _, l, half, rt = s
            pe.wait_ge(w_split, l + 1)
            done(("LX", 2 * l, 4 * half + 3))
            t = slice(half * HALF, (half + 1) * HALF)
            split_matmul(dst[:, 0:HALF], [(both(w_at[l], A, 0, k, slice(128 * rt, 128 * rt + 128)),
                                           both(xT, A, k, t)) for k in range(DT)]).then_inc(product, 1)

        def context_transposes(s):
            dst = begin(s)
            _, n, k = s
            pe.wait_ge(loaded_ctx[n % 2], 32 * (n // 2 + 1))
            pe.wait_ge(pool_const, 1)
            for t in range(3):
                ins = pe.transpose(dst[:, 128 * t:128 * t + KT[t]], cnat[0:KT[t], n % 2, t, 128 * k:128 * k + 128],
                                   ident[0:KT[t], 0:KT[t]])
            ins.then_inc(product, 1)

        def keys(s):
            dst = begin(s)
            _, n, rt = s
            pe.wait_ge(w_split, n // B + 1)
            done(("CT", n, 1))
            split_matmul(dst[:, 0:NK + 1], [(both(w_at[n // B], A, 1, k, slice(128 * rt, 128 * rt + 128)),
                                             both(cT, A, k, slice(0, NK + 1))) for k in range(DT)])\
                .then_inc(product, 1)

        def values(s):
            dst = begin(s)
            _, n, t = s
            pe.wait_ge(w_split, n // B + 1)
            done(("CT", n, 1))
            split_matmul(dst[0:KT[t], 0:D], [(both(cT, A, k, slice(128 * t, 128 * t + KT[t])),
                                              both(w_at[n // B], A, 2, k, A)) for k in range(DT)])\
                .then_inc(product, 1)

        def plain_scores(s):
            _, n, h = s
            x_ = H * n + h
            if x_ >= 2:
                pe.wait_ge(max_done, x_ - 1)
            pe.wait_ge(qm_ready, 2 * n + h // 8 + 1)
            done(("KP", n, h // 8))
            pe.matmul(bank[3 + x_ % 2][0:S, 0:NK + 1], qm[n % 2][0][:, h // 8, h % 8, :], kT[n % 3][0][:, h // 8, :],
                      start=True, stop=True).then_inc(sn_ready, 1)

        def max_transpose(s):
            dst = begin(s)
            n = s[1]
            pe.wait_ge(max_twice, n + 1)
            pe.transpose(dst[0:48, 0:S], mx[:, n % 2], ident[0:S, 0:S]).then_inc(product, 1)

        def scores(s):
            _, n, u = s
            g, t = u // 3, u % 3
            U = UNITS * n + u
            rt, h0_ = g // 2, 4 * (g % 2)
            if n < B and U >= 3:
                pe.wait_ge(biased, U - 2)
            if n >= B:
                pe.wait_ge(exp_done, U - 2)
            pe.wait_ge(dg_ready, n + 1)
            dst = bank[U % 3][0:KT[t], 0:HALF].rearrange("p (h q) -> p h q", h=4)
            ks = slice(128 * t, 128 * t + KT[t])
            split_matmul(dst, [(both(kT[n % 3], A, rt, ks), both(qm[n % 2], A, rt, slice(h0_, h0_ + 4), A))],
                         last=False)
            pe.matmul(dst, ones[:, 0:KT[t]], dg[n % 2][:, 4 * g:4 * g + 4, :], start=False, stop=True)\
                .then_inc(st_ready, 1)

        def weighted_values(s):
            _, n, u = s
            g, t = u // 3, u % 3
            U = UNITS * n + u
            done(("VP", n, 2))
            pe.wait_ge(exp_done, U + 1)
            if u == 0 and n >= 1:
                pe.wait_ge(pv_out, n)
            for j in range(4):
                ins = pe.matmul(bank[5][32 * j:32 * j + 32, g * S:(g + 1) * S], vA[n % 3][0:KT[t], t, 4 * g + j, :],
                                pT[0:KT[t], U % 4, j * S:(j + 1) * S], start=(t == 0), stop=(t == 2),
                                tile_position=(0, 32 * j), skip_group_check=True)
            ins.then_inc(pv_done, 1)

        def out1(s):
            dst = begin(s)
            pe.wait_ge(pv_out, s[1] + 1)
            for g in range(4):
                ins = pe.transpose(dst[0:S, 128 * g:128 * g + 128], pv[:, g, :], ident[:])
            ins.then_inc(product, 1)

        def out2(s):
            dst = begin(s)
            done(("O1", s[1]))
            for k in range(2):
                ins = pe.transpose(dst[:, k * S:(k + 1) * S], an[:, 128 * k:128 * k + 128], ident[0:S, 0:S])
            ins.then_inc(product, 1)

        def out3(s):
            dst = begin(s)
            n = s[1]
            done(("O2", n))
            split_matmul(dst[0:S, 0:D], [(both(aT, A, k, A), both(w_at[n // B], A, 3, k, A)) for k in range(2)])\
                .then_inc(product, 1)

        def router(s):
            dst = begin(s)
            l = s[1]
            done(("LX", 2 * l + 1, B - 1))
            done(("PC", 0))
            cols = slice(0, 16) if l == 0 else slice(16, 24)
            wide = 16 if l == 0 else 8
            for b in range(B):
                ins = split_matmul(dst[0:S, 16 * b:16 * b + wide],
                                   [(both(xT, A, k, slice(b * S, b * S + S)), both(rtw, A, k, cols))
                                    for k in range(DT)])
            ins.then_inc(product, 1)

        def gate_transposes(s):
            dst = begin(s)
            pe.wait_ge(gates_ready, s[1] + 1)
            for j in range(4):
                ins = pe.transpose(dst[0:E, j * S:(j + 1) * S], gate[:, 4 * s[2] + j, :], ident[0:S, 0:S])
            ins.then_inc(product, 1)

        def gate_bias(s):
            dst = begin(s)
            _, l, b = s
            done(("GT", l, b // 4))
            pe.matmul(dst[0:S, 0:D], gT[:, b * S:(b + 1) * S], rows8[:, l, :], start=True, stop=True)\
                .then_inc(product, 1)

        def hidden0(s):
            _, e, half = s
            i = 2 * e + half
            if i >= 3:
                pe.wait_ge(h_act, i - 2)
            pe.wait_ge(v_split, e // 2 + 1)
            t = slice(half * HALF, (half + 1) * HALF)
            split_matmul(bank[i % 3][:, 0:HALF], [(both(e0, A, 0, e, slice(128 * k, 128 * k + 128)),
                                                   both(xT, A, k, t)) for k in range(DT)]).then_inc(h_ready, 1)

        def output0(s):
            _, e, b = s
            i = 2 * e + b // 4
            j = 4 * i + b % 4
            if j >= 3:
                pe.wait_ge(y_added, j - 2)
            pe.wait_ge(h_split, i + 1)
            t = slice((b % 4) * S, (b % 4) * S + S)
            split_matmul(bank[3 + j % 3][0:S, 0:D], [(both(h0s, A, i % 2, t), both(e0, A, 1, e, A))])\
                .then_inc(y_ready, 1)

        def hidden1(s):
            _, e, half, f = s
            k_ = (2 * e + half) * FT + f
            if k_ == 0:
                pe.wait_ge(y_added, Y0N)
            if k_ >= 3:
                pe.wait_ge(h_made, k_ - 2)
            pe.wait_ge(r_split, 6 * e + 4)
            t = slice(half * HALF, (half + 1) * HALF)
            for m in range(2):
                ins = split_matmul(bank[2 * (k_ % 3) + m][:, 0:HALF],
                                   [(both(e1[e % 2], A, 2 * m + k, slice(128 * f, 128 * f + 128)), both(xT, A, k, t))
                                    for k in range(DT)])
            ins.then_inc(h_ready, 1)

        def output1(s):
            _, e, b = s
            step = 2 * e + b // 4
            j = 4 * step + b % 4
            if j < 2:
                pe.wait_ge(split_done, len(shared))
            if j >= 2:
                pe.wait_ge(y_added, Y0N + j - 1)
            pe.wait_ge(h_split, R16 + (step + 1) * FT)
            pe.wait_ge(r_split, 6 * (e + 1))
            t = slice((b % 4) * S, (b % 4) * S + S)
            split_matmul(bank[6 + j % 2][0:S, 0:D],
                         [(both(h1s, A, step % 2, f, t),
                           both(e1[e % 2], A, 4 + f // 4, slice(D * (f % 4), D * (f % 4) + D))) for f in range(FT)])\
                .then_inc(y_ready, 1)

        what = {"PB": step_prep, "PM": step_prep, "PF": step_prep, "PC": step_prep, "LX": norm_transposes,
                "Q": queries, "CT": context_transposes, "KP": keys, "VP": values, "SN": plain_scores,
                "MT": max_transpose, "ST": scores, "PV": weighted_values, "O1": out1, "O2": out2, "O3": out3,
                "R": router, "GT": gate_transposes, "GB": gate_bias, "H0": hidden0, "Y0": output0, "H1": hidden1,
                "Y1": output1}
        for s in order:
            if s[0] in what:
                what[s[0]](s)

    @block.scalar
    def _(act):
        n_sqrt = [0]

        def begin(step):
            act.wait_ge(product, job[step] + 1)
            return misc(step)

        def square_root(rows):
            n_sqrt[0] += 1
            act.wait_ge(var_ready, n_sqrt[0])
            act.activation(rows[1], rows[0], ACT.Sqrt).then_inc(sqrt_done, 1)

        def attention_weights(s):
            l = s[1]
            act.wait_ge(loaded_w[l], 64)
            act.activation(w_at[l][0][:, 0], w_raw[:, 0], ACT.Copy, scale=0.25)
            act.activation(w_at[l][0][:, 1:4], w_raw[:, 1:4], ACT.Copy).then_inc(w_high, 1)

        def norm_root(s):
            i = s[1]
            if i == 0:
                act.wait_ge(loaded_small, 16 * N_SMALL)
                act.activation(tg[:], tg[:], ACT.Tanh).then_inc(tanh_done, 1)
                square_root((crs[:, 0:1], crs[:, 1:2]))
            square_root((rs[:, 0], rs[:, 1]))

        def norm_high(s):
            src = begin(s)
            b = s[2]
            act.activation(xT[0][:, :, b * S:(b + 1) * S], src[:, 0:2 * S].rearrange("p (k q) -> p k q", k=2), ACT.Copy)\
                .then_inc(high_done, 1)

        def queries_high(s):
            src = begin(s)
            _, l, half, rt = s
            dst = qT[0][:, rt, half * HALF:(half + 1) * HALF]
            if l == 0:
                act.activation(dst, src[:, 0:HALF], ACT.Copy).then_inc(high_done, 1)
            else:
                act.activation(dst, src[:, 0:HALF], ACT.Identity, bias=colT[:, 8 + rt:9 + rt]).then_inc(high_done, 1)

        def context_high(s):
            src = begin(s)
            k = s[2]
            act.activation(cT[0][:, k, 0:NK], src[:, 0:NK], ACT.Copy).then_inc(high_done, 1)

        def keys_high(s):
            src = begin(s)
            _, n, rt = s
            dst = kT[n % 3][0][:, rt, :]
            if n < B:
                act.activation(dst, src[:, 0:NK + 1], ACT.Copy).then_inc(high_done, 1)
            else:
                act.activation(dst, src[:, 0:NK + 1], ACT.Identity, bias=colT[:, 10 + rt:11 + rt]).then_inc(high_done, 1)

        def max_high(s):
            src = begin(s)
            n = s[1]
            if n >= 1:
                act.wait_ge(dg_ready, n)
            act.activation(nm[:], src[0:48, 0:S], ACT.Copy, scale=-1.0).then_inc(high_done, 1)

        def exps(s):
            _, n, u = s
            t = u % 3
            U = UNITS * n + u
            if U >= 4:
                act.wait_ge(pv_done, U - 3)
            dst = pT[0:KT[t], U % 4]
            if n < B:
                act.wait_ge(biased, U + 1)
                act.activation(dst, sbias[0:KT[t], U % 3], ACT.Exp).then_inc(exp_done, 1)
            else:
                act.wait_ge(st_ready, U + 1)
                act.activation(dst, bank[U % 3][0:KT[t], 0:HALF], ACT.Exp,
                               bias=maskT[0:KT[t], t, n - B:n - B + 1]).then_inc(exp_done, 1)

        def evacuate(s):
            n = s[1]
            act.wait_ge(pv_done, UNITS * (n + 1))
            if n >= 1:
                act.wait_ge(product, job[("O1", n - 1)] + 1)
            act.activation(pv[:], bank[5][:, 0:4 * S].rearrange("p (g q) -> p g q", g=4), ACT.Copy).then_inc(pv_out, 1)

        def out_high(s):
            src = begin(s)
            act.activation(aT[0][:], src[:, 0:2 * S].rearrange("p (k q) -> p k q", k=2), ACT.Copy)\
                .then_inc(high_done, 1)

        def experts0_high(s):
            c = s[1]
            act.wait_ge(loaded_e0, 32)
            act.activation(e0[0][:, :, 2 * c:2 * c + 2], e0_raw[:, :, 2 * c:2 * c + 2], ACT.Copy).then_inc(v_high, 1)

        def router_exp(s):
            if s[1] == 0:
                square_root((rs[:, 0], rs[:, 1]))
            act.wait_ge(shifted, s[1] + 1)
            act.activation(gw[:, 3], gw[:, 2], ACT.Exp).then_inc(exp_gate, 1)

        def gelu(s):
            _, e, half = s
            i = 2 * e + half
            act.wait_ge(h_ready, i + 1)
            if i >= 2:
                act.wait_ge(h_split, i - 1)
            act.activation(h0[:, i % 2], bank[i % 3][:, 0:HALF], ACT.Gelu, bias=colT[:, e:e + 1]).then_inc(h_act, 1)

        def experts1_high(s):
            _, e, c = s
            p = 6 * e + c
            act.wait_ge(loaded_raw[p % NRAW], 16 * (p // NRAW + 1))
            if e >= 2 and c == 0:
                act.wait_ge(y_ready, Y0N + 8 * (e - 1))
            act.activation(e1[e % 2][0][:, c], e1_raw[:, p % NRAW], ACT.Copy).then_inc(r_high, 1)

        def high1(k):
            step, f = k // FT, k % FT
            act.wait_ge(h_made, k + 1)
            if step >= 2 and f == 0:
                act.wait_ge(y_ready, Y0N + 4 * (step - 1))
            act.activation(h1s[0][:, step % 2, f], h1f[:, k % 2], ACT.Copy).then_inc(h_high, 1)

        def silu(s):
            _, e, half, f = s
            k = (2 * e + half) * FT + f
            act.wait_ge(h_ready, R16 + k + 1)
            if k >= 2:
                act.wait_ge(h_made, k - 1)
            act.activation(s1b[:, k % 2], bank[2 * (k % 3)][:, 0:HALF], ACT.Silu, bias=b12T[:, 8 * e + f:8 * e + f + 1])\
                .then_inc(h_act, 1)
            if k >= 1:
                high1(k - 1)
            if k == 2 * E * FT - 1:
                high1(k)

        what = {"AW": attention_weights, "LS": norm_root, "LX": norm_high, "Q": queries_high, "CT": context_high,
                "KP": keys_high, "MT": max_high, "ST": exps, "OE": evacuate, "O2": out_high, "V": experts0_high,
                "R": router_exp, "H0": gelu, "W": experts1_high, "H1": silu}
        for s in order:
            if s[0] in what:
                what[s[0]](s)

    @block.vector
    def _(dve):
        steps = [0]

        def after(ins):
            steps[0] += 1
            ins.then_inc(dve_step, 1)
            dve.wait_ge(dve_step, steps[0])

        n_sqrt = [0]

        def inverse_root(v, y, t):
            n_sqrt[0] += 1
            dve.wait_ge(sqrt_done, n_sqrt[0])
            after(dve.reciprocal(y, y))
            after(dve.tensor_tensor(t, y, y, ALU.mult))
            after(dve.tensor_tensor(t, t, v, ALU.mult))
            after(dve.tensor_scalar(t, t, -0.5, 1.5, ALU.mult, ALU.add))
            after(dve.tensor_tensor(y, y, t, ALU.mult))

        def begin(step):
            dve.wait_ge(product, job[step] + 1)
            return misc(step)

        def high(step):
            dve.wait_ge(high_done, high_order[step] + 1)
            return begin(step)

        def attention_weights(s):
            l = s[1]
            dve.wait_ge(w_high, l + 1)
            dve.scalar_tensor_tensor(w_at[l][1][:, 0], w_raw[:, 0], 0.25, w_at[l][0][:, 0].bitcast(F32), ALU.mult,
                                     ALU.subtract)
            dve.tensor_tensor(w_at[l][1][:, 1:4], w_raw[:, 1:4], w_at[l][0][:, 1:4].bitcast(F32), ALU.subtract)\
                .then_inc(w_split, 1)

        def prepare():
            dve.wait_ge(pool_const, 1)
            dve.wait_ge(loaded_small, 16 * N_SMALL)
            dve.tensor_scalar(mnat[:], mnat_i[:], NEG_INF, None, ALU.mult).then_inc(dve_prep, 1)
            dve.tensor_copy(iota8[:], iota_i[:])
            dve.tensor_tensor_reduce(sqj[0:E], cw[:, 0], cw[:, 0], 1.0, 0.0, ALU.mult, ALU.add, crs[:, 4:5])\
                .then_inc(dve_step, 1)
            steps[0] += 1
            dve.wait_ge(dve_step, steps[0])
            dve.tensor_scalar(crs[:, 0:1], crs[:, 4:5], 1e-24, None, ALU.max).then_inc(var_ready, 1)
            inverse_root(crs[:, 0:1], crs[:, 1:2], crs[:, 2:3])
            dve.tensor_scalar(cw[:, 0], cw[:, 0], crs[:, 1:2], None, ALU.mult).then_inc(dve_prep, 1)
            dve.wait_ge(tanh_done, 1)
            dve.tensor_scalar(bob[:], bob[:], tg[0:S, 1:2], None, ALU.mult)

        def norm_stats(s):
            i = s[1]
            if i == 0:
                prepare()
                dve.wait_ge(loaded_x, 16)
            for b in range(B):
                last = dve.bn_stats(stats[:, b], xres[:, b])
            after(last)
            for b in range(B):
                last = dve.bn_aggr(mv[:, b], stats[:, b])
            after(last)
            dve.tensor_scalar(rs[:, 0], mv[:, :, 1], LN_EPS, None, ALU.add).then_inc(var_ready, 1)
            inverse_root(rs[:, 0], rs[:, 1], rs[:, 2])

        def norm_low(s):
            _, i, b = s

            def normalise(c):
                if c >= 2:
                    dve.wait_ge(product, job[("LX", i, c - 2)] + 1)
                ins = dve.tensor_scalar(xn[:, c % 2], xres[:, c], mv[:, c, 0:1], rs[:, 1, c:c + 1], ALU.subtract, ALU.mult)
                ins.then_inc(xn_ready, 1)
                if i == 1:
                    dve.wait_ge(xn_ready, B * i + c + 1)
                    after(dve.tensor_tensor_reduce(sqj[:], xn[:, c % 2], xn[:, c % 2], 1.0, 0.0, ALU.mult, ALU.add,
                                                   ssq[:, c:c + 1]))

            if b == 0:
                normalise(0)
            if b + 1 < B:
                normalise(b + 1)
            src = high(s)
            t = slice(b * S, (b + 1) * S)
            dve.tensor_tensor(xT[1][:, :, t], src[:, 0:2 * S].rearrange("p (k q) -> p k q", k=2),
                              xT[0][:, :, t].bitcast(F32), ALU.subtract).then_inc(split_done, 1)

        def queries_low(s):
            src = high(s)
            _, l, half, rt = s
            t = slice(half * HALF, (half + 1) * HALF)
            if l == 0:
                dve.tensor_tensor(qT[1][:, rt, t], src[:, 0:HALF], qT[0][:, rt, t].bitcast(F32), ALU.subtract)\
                    .then_inc(split_done, 1)
            else:
                dve.scalar_tensor_tensor(qT[1][:, rt, t], src[:, 0:HALF], colT[:, 8 + rt:9 + rt],
                                         qT[0][:, rt, t].bitcast(F32), ALU.add, ALU.subtract).then_inc(split_done, 1)

        def context_low(s):
            src = high(s)
            k = s[2]
            dve.tensor_tensor(cT[1][:, k, 0:NK], src[:, 0:NK], cT[0][:, k, 0:NK].bitcast(F32), ALU.subtract)\
                .then_inc(split_done, 1)

        def keys_low(s):
            src = high(s)
            _, n, rt = s
            hi, lo = kT[n % 3][0][:, rt, 0:NK].bitcast(F32), kT[n % 3][1][:, rt, 0:NK]
            if n < B:
                dve.tensor_tensor(lo, src[:, 0:NK], hi, ALU.subtract).then_inc(split_done, 1)
            else:
                dve.scalar_tensor_tensor(lo, src[:, 0:NK], colT[:, 10 + rt:11 + rt], hi, ALU.add, ALU.subtract)\
                    .then_inc(split_done, 1)

        def values_out(s):
            src = begin(s)
            _, n, t = s
            dst = vA[n % 3][0:KT[t], t, :, 0:DH]
            v = src[0:KT[t], 0:D].rearrange("p (h d) -> p h d", h=H)
            if n < B:
                dve.tensor_copy(dst, v).then_inc(split_done, 1)
            else:
                dve.tensor_tensor(dst, v, bvb[0:KT[t], :].rearrange("p (h d) -> p h d", h=H), ALU.add)\
                    .then_inc(split_done, 1)

        def maxima(s):
            _, n, h = s
            x_ = H * n + h
            dve.wait_ge(sn_ready, x_ + 1)
            if n >= B and h == 0:
                dve.wait_ge(mrow_ready, n - B + 1)
            if x_ >= 2:
                dve.wait_ge(max_done, x_ - 1)
            add = fnat[:] if n < B else mrow[:, n % 2]
            dve.tensor_tensor_reduce(junk[:, x_ % 2], bank[3 + x_ % 2][0:S, 0:NK], add, 1.0, -3.0e38, ALU.add, ALU.max,
                                     mx[:, n % 2, h:h + 1]).then_inc(max_done, 1)
            if h == H - 1:
                dve.wait_ge(max_done, x_ + 1)
                dve.tensor_copy(mx[:, n % 2, 32:48], mx[:, n % 2, 0:16]).then_inc(max_twice, 1)

        def max_low(s):
            src = high(s)
            dve.scalar_tensor_tensor(nm[32:48], src[32:48, 0:S], -1.0, nm[32:48].bitcast(F32), ALU.mult, ALU.subtract)\
                .then_inc(split_done, 1)

        def bias_scores(s):
            _, n, u = s
            if n >= B:
                return
            t = u % 3
            U = UNITS * n + u
            dve.wait_ge(st_ready, U + 1)
            if U >= 3:
                dve.wait_ge(exp_done, U - 2)
            dve.tensor_tensor(sbias[0:KT[t], U % 3].rearrange("p (h q) -> p h q", h=4),
                              bank[U % 3][0:KT[t], 0:HALF].rearrange("p (h q) -> p h q", h=4),
                              fT[0:KT[t], t].unsqueeze(1).to_broadcast((KT[t], 4, S)), ALU.add).then_inc(biased, 1)

        def normalise_heads(s):
            src = begin(s)
            v = src[0:S, 0:512].rearrange("p (h c) -> p h c", c=32)
            after(dve.reciprocal(rden[:], v[:, :, DH]))
            dve.tensor_tensor(an[:].rearrange("p (h d) -> p h d", h=H), v[:, :, 0:DH],
                              rden[:].unsqueeze(2).to_broadcast((S, H, DH)), ALU.mult).then_inc(split_done, 1)

        def out_low(s):
            src = high(s)
            dve.tensor_tensor(aT[1][:], src[:, 0:2 * S].rearrange("p (k q) -> p k q", k=2), aT[0][:].bitcast(F32),
                              ALU.subtract).then_inc(split_done, 1)

        def add_attention(s):
            src = begin(s)
            n = s[1]
            l, b = n // B, n % B
            dve.scalar_tensor_tensor(xres[:, b], src[0:S, 0:D], tg[0:S, l:l + 1], xres[:, b], ALU.mult, ALU.add)\
                .then_inc(split_done, 1)
            dve.wait_ge(split_done, job[s] + 1)
            if l == 1:
                after(dve.tensor_tensor(xres[:, b], xres[:, b], bob[:], ALU.add))
            if b == B - 1:
                dve.tensor_copy(rs[:, 3], rs[:, 2]).then_inc(attn_done, 1)

        def prep_out(s):
            src = begin(s)
            if s == ("PB", 0):
                ins = dve.tensor_copy(b12T[:], src[:, 0:128])
            elif s == ("PB", 1):
                after(dve.tensor_copy(colT[:], src[:, 0:12]))
                ins = dve.tensor_scalar(colT[:, 8:10], colT[:, 8:10], 0.25, None, ALU.mult)
            elif s[0] == "PM":
                for t in range(3):
                    ins = dve.tensor_copy(maskT[0:KT[t], t], src[0:KT[t], 8 * t:8 * t + 8])
            elif s[0] == "PF":
                for t in range(3):
                    ins = dve.tensor_copy(fT[0:KT[t], t], src[0:KT[t], S * t:S * t + S])
            else:
                after(dve.tensor_copy(rt_raw[:, :, 0:16], src[:, 0:32].rearrange("p (k c) -> p k c", k=2)))
                after(dve.tensor_copy(rtw[0][:], rt_raw[:]))
                ins = dve.tensor_tensor(rtw[1][:], rt_raw[:], rtw[0][:].bitcast(F32), ALU.subtract)
            ins.then_inc(split_done, 1)

        def experts0_low(s):
            c = s[1]
            p = slice(2 * c, 2 * c + 2)
            dve.wait_ge(v_high, c + 1)
            dve.tensor_tensor(e0[1][:, :, p], e0_raw[:, :, p], e0[0][:, :, p].bitcast(F32), ALU.subtract).then_inc(v_split, 1)

        def gates(s):
            l = s[1]
            src = begin(s)
            wide = 16 if l == 0 else 8
            dve.tensor_copy(lg[:, :, 0:wide], src[0:S, 0:16 * B].rearrange("p (b c) -> p b c", b=B)[:, :, 0:wide])\
                .then_inc(split_done, 1)
            dve.wait_ge(split_done, job[s] + 1)
            z, top, low, ex, pick, pick2, pr = (gw[:, i] for i in range(7))

            def wide_of(a):
                return a.to_broadcast((S, B, E))

            if l == 0:
                dve.tensor_scalar(rs[:, 0], ssq[:], 1e-24, None, ALU.max).then_inc(var_ready, 1)
                inverse_root(rs[:, 0], rs[:, 1], rs[:, 2])
                after(dve.tensor_tensor(z, lg[:, :, 0:8], wide_of(rs[:, 1].unsqueeze(2)), ALU.mult))
                after(dve.tensor_tensor(z, z, lg[:, :, 8:16], ALU.add))
            else:
                after(dve.tensor_tensor(z, lg[:, :, 0:8], wide_of(brb[:].unsqueeze(1)), ALU.add))
            for b in range(B):
                last = dve.max(top[:, b], z[:, b])
            after(last)
            dve.tensor_tensor(low, z, wide_of(top[:, :, 0:1]), ALU.subtract).then_inc(shifted, 1)
            if l == 0:
                after(dve.tensor_tensor(pick, z, wide_of(top[:, :, 1:2]), ALU.is_ge))
            else:
                for b in range(B):
                    last = dve.max_index(idx[:, b], top[:, b], z[:, b])
                after(last)
                after(dve.tensor_copy(pr, idx[:]))
                dve.tensor_tensor(pick, wide_of(iota8[:].unsqueeze(1)), wide_of(pr[:, :, 0:1]), ALU.is_equal)
                after(dve.tensor_tensor(pick2, wide_of(iota8[:].unsqueeze(1)), wide_of(pr[:, :, 1:2]), ALU.is_equal))
                after(dve.tensor_tensor(pick, pick, pick2, ALU.add))
            dve.wait_ge(exp_gate, l + 1)
            after(dve.tensor_tensor(pick2, ex, pick, ALU.mult))
            after(dve.tensor_reduce(rs[:, 0], pick2, AX.X, ALU.add))
            after(dve.reciprocal(rs[:, 1], rs[:, 0]))
            after(dve.tensor_tensor(gate[:], pick2, wide_of(rs[:, 1].unsqueeze(2)), ALU.mult))
            dve.tensor_scalar(gate[:], gate[:], tg[0:S, 2 + l:3 + l], None, ALU.mult).then_inc(gates_ready, 1)
            dve.wait_ge(gates_ready, l + 1)

        def gates_turned(s):
            src = begin(s)
            dve.tensor_copy(gT[:, s[2] * HALF:(s[2] + 1) * HALF], src[0:E, 0:HALF]).then_inc(split_done, 1)

        def add_bias(s):
            src = begin(s)
            b = s[2]
            dve.tensor_tensor(xres[:, b], src[0:S, 0:D], xres[:, b], ALU.add).then_inc(split_done, 1)
            if b == B - 1:
                dve.wait_ge(split_done, job[s] + 1)

        def add_expert(j, src, e, b):
            dve.wait_ge(y_ready, j + 1)
            if j >= 1:
                dve.wait_ge(y_added, j)
            dve.scalar_tensor_tensor(xres[:, b], src[0:S, 0:D], gate[:, b, e:e + 1], xres[:, b], ALU.mult, ALU.add)\
                .then_inc(y_added, 1)

        def output0(s):
            _, e, b = s
            j = 4 * (2 * e + b // 4) + b % 4
            add_expert(j, bank[3 + j % 3], e, b)
            if j == Y0N - 1:
                dve.wait_ge(y_added, Y0N)

        def output1(s):
            _, e, b = s
            j = 4 * (2 * e + b // 4) + b % 4
            add_expert(Y0N + j, bank[6 + j % 2], e, b)
            if j == 8 * E - 1:
                dve.wait_ge(y_added, Y0N + 8 * E)
                dve.tensor_copy(rs[:, 3], rs[:, 2]).then_inc(moe_done, 2)

        def experts1_low(s):
            _, e, c = s
            p = 6 * e + c
            dve.wait_ge(r_high, p + 1)
            dve.tensor_tensor(e1[e % 2][1][:, c], e1_raw[:, p % NRAW], e1[e % 2][0][:, c].bitcast(F32), ALU.subtract)\
                .then_inc(r_split, 1)

        def hidden1(s):
            _, e, half, f = s
            k = (2 * e + half) * FT + f
            dve.wait_ge(h_act, R16 + k + 1)
            if k >= 2:
                dve.wait_ge(h_split, R16 + k - 1)
            dve.scalar_tensor_tensor(h1f[:, k % 2], bank[2 * (k % 3) + 1][:, 0:HALF],
                                     b12T[:, 64 + 8 * e + f:65 + 8 * e + f], s1b[:, k % 2], ALU.add, ALU.mult)\
                .then_inc(h_made, 1)

        what = {"AW": attention_weights, "PB": prep_out, "PM": prep_out, "PF": prep_out, "PC": prep_out,
                "LS": norm_stats, "LX": norm_low, "Q": queries_low, "CT": context_low, "KP": keys_low,
                "VP": values_out, "SN": maxima, "MT": max_low, "ST": bias_scores, "O1": normalise_heads,
                "O2": out_low, "O3": add_attention, "V": experts0_low, "R": gates, "GT": gates_turned,
                "GB": add_bias, "Y0": output0, "Y1": output1, "W": experts1_low, "H1": hidden1}
        for s in order:
            if s[0] in what:
                what[s[0]](s)

    st.close()


_INS = ["x", "ctx_1024", "fside_1x1xSxS2_0", "mask_Bx1x1xS2_ik0", "g_xattn", "g_ffn",
        "L0_xattn_wq", "L0_xattn_wk", "L0_xattn_wv", "L0_xattn_wo",
        "L0_ffn_w1", "L0_ffn_b1", "L0_ffn_w2", "L0_ffn_b2", "L0_ffn_centroids", "L0_ffn_w_route",
        "L1_xattn_wq", "L1_xattn_bq", "L1_xattn_wk", "L1_xattn_bk", "L1_xattn_wv", "L1_xattn_bv",
        "L1_xattn_wo", "L1_xattn_bo",
        "L1_ffn_Wr", "L1_ffn_br", "L1_ffn_W1", "L1_ffn_b1", "L1_ffn_W2", "L1_ffn_b2", "L1_ffn_W3", "L1_ffn_b3"]


def kernel(**inputs):
    import numpy as _np
    import concourse.bacc as _bacc
    from concourse import mybir as _mybir
    from concourse.bass_utils import run_bass_kernel_spmd as _run

    nc = _bacc.Bacc("TRN2", target_bir_lowering=False, num_devices=1)
    arrays, aps = {}, {}
    for name in _INS:
        a = _np.ascontiguousarray(inputs[name])
        if name in ("L0_xattn_wq", "L0_xattn_wk", "L0_xattn_wv", "L0_xattn_wo"):
            a = a.reshape(D, D)
        arrays[f"in_{name}_dram"] = a
        aps[name] = nc.dram_tensor(f"in_{name}_dram", a.shape, _mybir.dt.from_np(a.dtype), kind="ExternalInput").ap()
    out = nc.dram_tensor("out_0_dram", (B, S, D), F32, kind="ExternalOutput").ap()

    def part(prefix):
        return {name[len(prefix):]: ap for name, ap in aps.items() if name.startswith(prefix)}

    gated_layers(nc, aps["x"], aps["ctx_1024"], aps["fside_1x1xSxS2_0"], aps["mask_Bx1x1xS2_ik0"], aps["g_xattn"],
                 aps["g_ffn"], part("L0_xattn_"), part("L0_ffn_"), part("L1_xattn_"), part("L1_ffn_"), out)
    r = _run(nc, [arrays], core_ids=[0])
    return r.results[0]["out_0_dram"]
```

```python
from contextlib import ExitStack

import concourse.bass as bass
from concourse import mybir

ALU = mybir.AluOpType
ACT = mybir.ActivationFunctionType
F32 = mybir.dt.float32
F32R = mybir.dt.float32r
I32 = mybir.dt.int32
U32 = mybir.dt.uint32
AX = mybir.AxisListType

B, S, D = 8, 100, 256
NK = 361
KT = [128, 128, NK - 256]
H, DH = 16, 16
DT = D // 128
E = 8
HID = 128
FF = 1024
FT = FF // 128
HALF = 4 * S
LN_EPS = 1e-5
NEG_INF = -1000000000.0
TOP = 2
TILES = (TOP * B * S + E * 127) // 128
UNITS = 12


def attention_order(layer):
    n0 = layer * B
    order = []

    def context(n):
        return [("CT", n, 0), ("CT", n, 1)], [("KP", n, 0), ("KP", n, 1)], [("VP", n, 0), ("VP", n, 1), ("VP", n, 2)]

    for part in context(n0):
        order += part
    order += [("SN", n0, h) for h in range(H)] + [("MT", n0)]
    for part in context(n0 + 1):
        order += part
    for b in range(B):
        n = n0 + b
        heads = [("SN", n + 1, h) for h in range(H)] if b + 1 < B else []
        for u in range(UNITS):
            order.append(("ST", n, u))
            if heads:
                order += heads[:2]
                heads = heads[2:]
            if u >= 2:
                order.append(("PV", n, u - 2))
            if b >= 1:
                order += {2: [("O1", n - 1)], 5: [("O2", n - 1)], 7: [("O3", n - 1)]}.get(u, [])
            if b + 2 < B:
                transposes, keys, values = context(n + 2)
                order += {3: transposes, 6: keys, 9: values}.get(u, [])
            if u == 8 and b + 1 < B:
                order.append(("MT", n + 1))
        order += [("PV", n, UNITS - 2), ("PV", n, UNITS - 1), ("OE", n)]
    order += [("O1", n0 + B - 1), ("O2", n0 + B - 1), ("O3", n0 + B - 1)]
    return order


def norm_order(s):
    return [("LS", s)] + [("LX", s, b) for b in range(B)]


def query_order(layer):
    return [("Q", layer, half, rt) for half in range(2) for rt in range(2)]


def ffn0_order():
    order = [("R", 0), ("GT", 0, 0), ("GT", 0, 1)] + [("GB", 0, b) for b in range(B)]
    steps = [(e, half) for e in range(E) for half in range(2)]
    for i, (e, half) in enumerate(steps):
        order.append(("H0", e, half))
        if i >= 1:
            pe, ph = steps[i - 1]
            order += [("Y0", pe, ph * 4 + j) for j in range(4)]
    order += [("Y0", E - 1, 4 + j) for j in range(4)]
    return order


def ffn1_order():
    order = [("BB",), ("R", 1), ("PS",)] + [("W", 0, c) for c in range(6)] + [("GT", 1, 0), ("GT", 1, 1)] + [("GB", 1, b) for b in range(B)]
    order += [("XT", 0), ("XT", 1)]
    for j in range(TILES + 1):
        if j < TILES:
            order.append(("HP", j, 0))
        if j >= 1:
            order.append(("HT", j - 1, 1))
        if j + 1 < TILES:
            order += [("W", j + 1, c) for c in (0, 1)]
        if j < TILES:
            order += [("HP", j, 1), ("HT", j, 0)]
        if j + 1 < TILES:
            order += [("W", j + 1, c) for c in (2, 3)]
        if j >= 1:
            order.append(("Y1", j - 1))
        if j + 1 < TILES:
            order += [("W", j + 1, c) for c in (4, 5)]
        if j + 2 < TILES:
            order.append(("XT", j + 2))
    return order + [("GA",)]


def gated_layers(nc, x, ctx, fside, mask, g_xattn, g_ffn, w0, f0, w1, f1, out):
    prep = [("PB", 0), ("PM", 0), ("PF", 0), ("PC", 0)]
    order = ([("AW", 0)] + norm_order(0) + prep + query_order(0) + attention_order(0)[:7] + [("AW", 1)]
             + attention_order(0)[7:]
             + [("V", c) for c in range(4)] + norm_order(1) + ffn0_order()
             + norm_order(2) + query_order(1) + attention_order(1)
             + norm_order(3) + ffn1_order())
    shared = [s for s in order if s[0] in ("PB", "PM", "PF", "PC", "LX", "Q", "CT", "KP", "VP", "MT",
                                           "O1", "O2", "O3", "R", "GT", "GB", "PS", "XT", "Y1")]
    job = {s: i for i, s in enumerate(shared)}
    high_order = {s: i for i, s in enumerate([s for s in shared if s[0] in ("LX", "Q", "CT", "KP", "MT", "O2", "XT")])}

    st = ExitStack()

    def sb(name, shape, dt=F32, stack=None):
        return (stack or st).enter_context(nc.sbuf_tensor(name, shape, dt))

    def sem(name):
        return st.enter_context(nc.semaphore(name))

    bank = [st.enter_context(nc.psum_tensor(f"bank{i}", [128, 512], F32)) for i in range(8)]

    def misc(step):
        return bank[6 + job[step] % 2]

    xres = sb("xres", [S, B, D])
    xT = [sb("xT_hi", [128, DT, B * S], F32R), sb("xT_lo", [128, DT, B * S], F32R)]
    xn = sb("xn", [S, 2, D])
    stats = sb("stats", [S, B, 6])
    mv = sb("mv", [S, B, 2])
    rs = sb("rs", [S, 4, B])
    ssq = sb("ssq", [S, B])
    sqj = sb("sqj", [S, D])
    ident = sb("ident", [128, 128])
    ones = sb("ones", [48, 128], F32R)
    onesf = sb("onesf", [48, 128])
    tg = sb("tg", [128, 4])
    colT = sb("colT", [128, 12])
    rows8 = sb("rows8", [E, 2, D])
    rt_raw = sb("rt_raw", [128, DT, 24])
    rtw = [sb("rt_hi", [128, DT, 24], F32R), sb("rt_lo", [128, DT, 24], F32R)]
    brb = sb("brb", [S, E])
    lg = sb("lg", [S, B, 16])
    gw = sb("gw", [S, 7, B, E])
    gate = sb("gate", [S, B, E])
    iota_i = sb("iota_i", [S, E], I32)
    iota8 = sb("iota8", [S, E])
    tri = [sb("tri", [S, S], F32R), sb("all_ones", [S, S], F32R)]
    trif = sb("trif", [S, S])
    mult_i = sb("mult_i", [S, 7], I32)
    mult128 = sb("mult128", [S, 7])
    tri8 = sb("tri8", [S, E, E])
    tile_i = sb("tile_i", [1, TILES], I32)
    tile_no = sb("tile_no", [1, TILES])
    gT = sb("gT", [E, B * S])
    nat2 = sb("nat2", [12, 128])
    cw = sb("cw", [E, 2, D])
    crs = sb("crs", [E, 6])

    at = ExitStack()
    w_raw = sb("w_raw", [128, 4, DT, D], F32, at)
    w_at = [[sb(f"w{l}_{p}", [128, 4, DT, D], F32R, at) for p in ("hi", "lo")] for l in range(2)]
    bvb = sb("bvb", [128, D], F32, at)
    bob = sb("bob", [S, D], F32, at)
    fnat = sb("fnat", [S, NK], F32, at)
    fT = sb("fT", [128, 3, S], F32, at)
    mnat_i = sb("mnat_i", [B, NK], I32, at)
    mnat = sb("mnat", [B, NK], F32, at)
    maskT = sb("maskT", [128, 3, B], F32, at)
    mrow_i = sb("mrow_i", [S, 2, NK], I32, at)
    mrow = sb("mrow", [S, 2, NK], F32, at)
    hmask = sb("hmask", [128, 8], F32, at)
    cnat = sb("cnat", [128, 2, 3, D], F32, at)
    vA = [sb(f"v{i}", [128, 3, H, 32], F32, at) for i in range(3)]
    mx = sb("mx", [S, 2, 48], F32, at)
    nm = sb("nm", [48, S], F32R, at)
    dg = [sb(f"dg{i}", [48, H, S], F32R, at) for i in range(2)]
    cT = [sb("c_hi", [128, DT, NK + 1], F32R, at), sb("c_lo", [128, DT, NK + 1], F32R, at)]
    a1 = ExitStack()
    qT = [sb("q_hi", [128, 2, B * S], F32R, a1), sb("q_lo", [128, 2, B * S], F32R, a1)]
    qm = [[sb(f"qm{i}_{p}", [128, 2, 8, S], F32R, a1) for p in ("hi", "lo")] for i in range(2)]
    kT = [[sb(f"k{i}_{p}", [128, 2, NK + 1], F32R, a1) for p in ("hi", "lo")] for i in range(3)]
    junk = sb("junk", [S, 2, NK], F32, a1)
    sbias = sb("sbias", [128, 3, 4 * S], F32, a1)
    pT = sb("pT", [128, 4, 4 * S], F32, a1)
    pv = sb("pv", [128, 4, S], F32, a1)
    rden = sb("rden", [S, H], F32, a1)
    an = sb("an", [S, D], F32, a1)
    aT = [sb("a_hi", [128, 2, S], F32R, a1), sb("a_lo", [128, 2, S], F32R, a1)]
    a1.close()
    m0 = ExitStack()
    e0_raw = sb("e0_raw", [128, 2, E, 256], F32, m0)
    e0 = [sb("e0_hi", [128, 2, E, 256], F32R, m0), sb("e0_lo", [128, 2, E, 256], F32R, m0)]
    h0 = sb("h0", [128, 2, HALF], F32, m0)
    h0s = [sb("h0_hi", [128, 2, HALF], F32R, m0), sb("h0_lo", [128, 2, HALF], F32R, m0)]
    m0.close()
    at.close()
    m1 = ExitStack()
    e1_raw = sb("e1_raw", [128, 6, 1024], F32, m1)
    e1 = [[sb(f"e1{i}_{p}", [128, 6, 1024], F32R, m1) for p in ("hi", "lo")] for i in range(2)]
    bt = [sb(f"bt{i}", [34, FF], F32R, m1) for i in range(2)]
    xna = sb("xna", [S, B, D], F32, m1)
    idx = sb("idx", [S, B, 8], U32, m1)
    pk = sb("pk", [S, TOP, B, E], F32, m1)
    pkr = sb("pkr", [S, B * E], F32R, m1)
    cnt = sb("cnt", [S, 2, B, E], F32, m1)
    off = sb("off", [S, B + 1, E], F32, m1)
    pos = sb("pos", [S, B, E], F32, m1)
    posk = sb("posk", [S, TOP, B], F32, m1)
    slot = sb("slot", [S, TOP, B], U32, m1)
    gk = sb("gk", [S, TOP, B], F32, m1)
    tl = sb("tl", [S, 4, E], F32, m1)
    cmp7 = sb("cmp7", [S, E, 7], F32, m1)
    tri8m = sb("tri8m", [S, E, E], F32, m1)
    cmpt = sb("cmpt", [1, TILES, E - 1], F32, m1)
    tex = sb("tex", [1, 2, TILES], F32, m1)
    texi = sb("texi", [1, 2, TILES], I32, m1)
    mb = ExitStack()
    bnat = sb("bnat", [E, 2, FF], F32, mb)
    bsp = [sb("b_hi", [E, 2, FF], F32R, mb), sb("b_lo", [E, 2, FF], F32R, mb)]
    mb.close()
    m2 = ExitStack()
    xs = sb("xs", [128, 3, D], F32, m2)
    xst = [[sb(f"xst{i}_{p}", [128, DT, 128], F32R, m2) for p in ("hi", "lo")] for i in range(2)]
    h1f = sb("h1f", [128, 2, 512], F32, m2)
    h1s = [[sb(f"h1{i}_{p}", [128, FT, 128], F32R, m2) for p in ("hi", "lo")] for i in range(2)]
    yo = sb("yo", [128, 2, D], F32, m2)
    m2.close()
    yk = sb("yk", [S, TOP, B, D], F32, m1)
    m1.close()

    loaded_x, loaded_small, out_done = sem("loaded_x"), sem("loaded_small"), sem("out_done")
    loaded_w = [sem("loaded_w0"), sem("loaded_w1")]
    loaded_ctx = [sem("loaded_ctx0"), sem("loaded_ctx1")]
    loaded_mask = [sem("loaded_mask0"), sem("loaded_mask1")]
    loaded_e0 = sem("loaded_e0")
    loaded_raw = [sem(f"loaded_raw{i}") for i in range(6)]
    loaded_xs = [sem(f"loaded_xs{i}") for i in range(3)]
    loaded_bt = [sem(f"loaded_bt{i}") for i in range(2)]
    loaded_b, b_split, b_stored = sem("loaded_b"), sem("b_split"), sem("b_stored")
    slots_zeroed, zeros_ready, slots_ready, scattered = (sem("slots_zeroed"), sem("zeros_ready"), sem("slots_ready"),
                                                         [sem(f"scattered{b}") for b in range(B)])
    experts_known, counts_in, y_stored, gathered = (sem("experts_known"), sem("counts_in"),
                                                    [sem("y_stored0"), sem("y_stored1")],
                                                    [sem(f"gathered{b}") for b in range(B)])
    h_turned = sem("h_turned")
    pool_const, pool_step, dve_step, dve_prep = sem("pool_const"), sem("pool_step"), sem("dve_step"), sem("dve_prep")
    tanh_done, var_ready, sqrt_done = sem("tanh_done"), sem("var_ready"), sem("sqrt_done")
    w_high, w_split, xn_ready = sem("w_high"), sem("w_split"), sem("xn_ready")
    product, high_done, split_done = sem("product"), sem("high_done"), sem("split_done")
    qm_ready, mrow_ready = sem("qm_ready"), sem("mrow_ready")
    sn_ready, max_done, max_twice, dg_ready = sem("sn_ready"), sem("max_done"), sem("max_twice"), sem("dg_ready")
    st_ready, biased, exp_done, pv_done, pv_out = (sem("st_ready"), sem("biased"), sem("exp_done"), sem("pv_done"),
                                                   sem("pv_out"))
    an_ready, attn_done, moe_done = sem("an_ready"), sem("attn_done"), sem("moe_done")
    b_high = sem("b_high")
    v_high, v_split, shifted, exp_gate, gates_ready = (sem("v_high"), sem("v_split"), sem("shifted"),
                                                       sem("exp_gate"), sem("gates_ready"))
    h_ready, h_act, h_made, h_high, h_split = sem("h_ready"), sem("h_act"), sem("h_made"), sem("h_high"), sem("h_split")
    y_ready, y_added = sem("y_ready"), sem("y_added")
    r_high, r_split = sem("r_high"), sem("r_split")

    x_slots = nc.dram_tensor("x_slots", (TILES * 128, D), F32).ap()
    y_slots = nc.dram_tensor("y_slots", (TILES * 128, D), F32).ap()
    b_parts = nc.dram_tensor("b_parts", (2, E, 2, FF), F32).ap()

    N_SMALL = 15
    w3v = f1["W3"].rearrange("e (j p) d -> e p j d", p=128)

    Y0N = 4 * 2 * E
    R16 = 2 * E

    block = st.enter_context(nc.Block())

    def load_rows(sp, j):
        if j >= 3:
            sp.wait_ge(product, job[("XT", j - 3)] + 1)
        sp.dma_start(xs[:, j % 3], x_slots[128 * j:128 * j + 128]).then_inc(loaded_xs[j % 3], 16)

    @block.sync
    def _(sp):
        def load_context(n):
            b = n % B
            if n >= 2:
                sp.wait_ge(product, job[("CT", n - 2, 1)] + 1)
            sp.dma_start(cnat[:, n % 2, 0:2], ctx[b, 0:256].rearrange("(t p) d -> p t d", p=128))\
                .then_inc(loaded_ctx[n % 2], 16)
            sp.dma_start(cnat[0:KT[2], n % 2, 2], ctx[b, 256:NK]).then_inc(loaded_ctx[n % 2], 16)

        def load_mask(n):
            if n >= B + 2:
                sp.wait_ge(mrow_ready, n - B - 1)
            sp.dma_start(mrow_i[:, n % 2], mask[n % B, 0].to_broadcast((S, NK))).then_inc(loaded_mask[n % 2], 16)

        def load_weights(l, w):
            for i, name in enumerate(("wq", "wk", "wv", "wo")):
                sp.dma_start(w_raw[:, i], w[name].rearrange("(k p) n -> p k n", p=128)).then_inc(loaded_w[l], 16)

        sp.dma_start(xres[:], x.rearrange("b s d -> s b d")).then_inc(loaded_x, 16)
        load_weights(0, w0)
        load_context(0)
        small = [(nat2[0:8, :], f0["b1"]),
                 (nat2[8:10, :], w1["bq"].rearrange("(a p) -> a p", p=128)),
                 (nat2[10:12, :], w1["bk"].rearrange("(a p) -> a p", p=128)),
                 (rows8[:, 0, :], f0["b2"]), (rows8[:, 1, :], f1["b3"]),
                 (cw[:, 0, :], f0["centroids"]), (cw[:, 1, :], f0["w_route"]),
                 (rt_raw[:, :, 16:24], f1["Wr"].rearrange("(k p) e -> p k e", p=128)),
                 (brb[:], f1["br"].rearrange("(a e) -> a e", a=1).to_broadcast((S, E))),
                 (tg[:, 0:2], g_xattn.rearrange("(a e) -> a e", a=1).to_broadcast((128, 2))),
                 (tg[:, 2:4], g_ffn.rearrange("(a e) -> a e", a=1).to_broadcast((128, 2))),
                 (fnat[:], fside[0, 0]), (mnat_i[:], mask.rearrange("b u v k -> (b u v) k")),
                 (bvb[:], w1["bv"].rearrange("(a e) -> a e", a=1).to_broadcast((128, D))),
                 (bob[:], w1["bo"].rearrange("(a e) -> a e", a=1).to_broadcast((S, D)))]
        assert len(small) == N_SMALL
        for dst, src in small:
            sp.dma_start(dst, src).then_inc(loaded_small, 16)
        load_context(1)
        sp.wait_ge(w_split, 1)
        load_weights(1, w1)
        for n in range(2, 2 * B):
            if n == B + 2:
                sp.wait_ge(attn_done, 1)
                sp.dma_start(e0_raw[:, 0].rearrange("p e (k h) -> p (e k) h", k=2),
                             f0["w1"].rearrange("e (k p) h -> p (e k) h", p=128)).then_inc(loaded_e0, 16)
                sp.dma_start(e0_raw[:, 1], f0["w2"].rearrange("e p d -> p e d")).then_inc(loaded_e0, 16)
                load_mask(B)
                load_mask(B + 1)
                sp.wait_ge(zeros_ready, 1)
                sp.dma_start(x_slots.rearrange("(r p) d -> p r d", p=128),
                             w_raw[:, 0, 0].unsqueeze(1).to_broadcast((128, TILES, D))).then_inc(slots_zeroed, 16)
            load_context(n)
            if n >= B + 2:
                load_mask(n)
        sp.wait_ge(attn_done, 2)
        sp.dma_start(bnat[:, 0], f1["b1"]).then_inc(loaded_b, 16)
        sp.dma_start(bnat[:, 1], f1["b2"]).then_inc(loaded_b, 16)
        sp.wait_ge(b_split, 1)
        for p in range(2):
            sp.dma_start(b_parts[:, :, p].rearrange("w e f -> e w f"), bsp[p][:].bitcast(F32)).then_inc(b_stored, 16)
        sp.wait_ge(b_stored, 32)

        def store_rows(j):
            sp.wait_ge(split_done, job[("Y1", j)] + 1)
            sp.dma_start(y_slots[128 * j:128 * j + 128], yo[:, j % 2]).then_inc(y_stored[j % 2], 16)

        sp.wait_ge(experts_known, 1)
        for j in range(TILES):
            if j >= 3:
                store_rows(j - 3)
            expert = sp.value_load(texi[0:1, 0, j:j + 1], min_val=0, max_val=E - 1)
            differs = sp.value_load(texi[0:1, 1, j:j + 1], min_val=0, max_val=1)
            if j >= 2:
                sp.wait_ge(h_ready, R16 + 2 * (j - 1))
            for w in range(2):
                sp.dma_start(bt[j % 2][32 * w:32 * w + 2].bitcast(F32),
                             b_parts[w][bass.ds(expert, 1)].rearrange("o p f -> (o p) f")).then_inc(loaded_bt[j % 2], 16)
            for c in range(6):
                if j >= 1:
                    sp.wait_ge(r_split, 6 * (j - 1) + c + 1)
                if c < 4:
                    src = f1["W1" if c < 2 else "W2"][bass.ds(expert, 1), 128 * (c % 2):128 * (c % 2) + 128, :]
                    src, dst = src.rearrange("o p f -> p (o f)"), e1_raw[:, c]
                else:
                    src = w3v[bass.ds(expert, 1), :, 4 * (c - 4):4 * (c - 4) + 4, :]
                    src, dst = src.rearrange("o p j d -> p (o j) d"), e1_raw[:, c].rearrange("p (j d) -> p j d", j=4)
                sp.dma_start(dst, src, cond=differs).then_inc(loaded_raw[c], 16)
            if j == 0:
                for b in range(B):
                    sp.wait_ge(scattered[b], 16 * TOP)
                load_rows(sp, 0)
                load_rows(sp, 1)
            if j + 2 < TILES:
                load_rows(sp, j + 2)
        for j in range(TILES - 3, TILES):
            store_rows(j)
        sp.wait_ge(moe_done, B)
        sp.dma_start(out.rearrange("b s d -> s b d"), xres[:]).then_inc(out_done, 16)
        sp.wait_ge(out_done, 16)

    @block.gpsimd
    def _(pool):
        steps = [0]

        def after(ins):
            steps[0] += 1
            ins.then_inc(pool_step, 1)
            pool.wait_ge(pool_step, steps[0])

        after(pool.memset(ident[:], 0.0))
        after(pool.affine_select(out=ident[:], in_=ident[:], compare_op=ALU.not_equal, fill=1.0, base=0,
                                 pattern=[[-1, 128]], channel_multiplier=1))
        after(pool.memset(hmask[:], 1.0))
        after(pool.affine_select(out=hmask[:], in_=hmask[:], compare_op=ALU.is_ge, fill=0.0, base=0,
                                 pattern=[[-DH, 8]], channel_multiplier=1))
        after(pool.affine_select(out=hmask[:], in_=hmask[:], compare_op=ALU.is_ge, fill=0.0, base=DH - 1,
                                 pattern=[[DH, 8]], channel_multiplier=-1))
        after(pool.iota(iota_i[:], pattern=[[1, E]], base=0, channel_multiplier=0))
        after(pool.iota(mult_i[:], pattern=[[128, 7]], base=0, channel_multiplier=0))
        after(pool.iota(tile_i[:], pattern=[[1, TILES]], base=0, channel_multiplier=0))
        after(pool.memset(tri8[:], 1.0))
        after(pool.affine_select(out=tri8[:], in_=tri8[:], compare_op=ALU.is_ge, fill=0.0, base=0,
                                 pattern=[[1, E], [-1, E]], channel_multiplier=0))
        after(pool.memset(trif[:], 1.0))
        after(pool.tensor_copy(tri[1][:], trif[:]))
        after(pool.affine_select(out=trif[:], in_=trif[:], compare_op=ALU.is_gt, fill=0.0, base=0,
                                 pattern=[[1, S]], channel_multiplier=-1))
        after(pool.tensor_copy(tri[0][:], trif[:]))
        for i in range(3):
            after(pool.memset(vA[i][:], 0.0))
            after(pool.memset(vA[i][:, :, :, DH:DH + 1], 1.0))
        for i in range(2):
            after(pool.memset(dg[i][:].bitcast(F32), 0.0))
        for part in cT:
            after(pool.memset(part[:, :, NK:NK + 1].bitcast(F32), 0.0))
        after(pool.memset(onesf[:], 1.0))
        after(pool.tensor_copy(ones[:], onesf[:]))
        pool.memset(mx[:], 0.0).then_inc(pool_const, 1)

        def masked_queries(n, rt):
            b = n % B
            pool.wait_ge(split_done, job[("Q", n // B, b // 4, rt)] + 1)
            if n >= 2:
                pool.wait_ge(st_ready, UNITS * (n - 2) + 6 * (rt + 1))
            for p in range(2):
                last = pool.tensor_tensor(
                    qm[n % 2][p][:, rt],
                    qT[p][:, rt, b * S:(b + 1) * S].bitcast(F32).unsqueeze(1).to_broadcast((128, 8, S)),
                    hmask[:].unsqueeze(2).to_broadcast((128, 8, S)), ALU.mult)
            last.then_inc(qm_ready, 1)
            pool.wait_ge(qm_ready, 2 * n + rt + 1)

        def mask_row(n):
            pool.wait_ge(loaded_mask[n % 2], 16 * ((n - B) // 2 + 1))
            if n >= B + 2:
                pool.wait_ge(max_done, H * (n - 1))
            pool.tensor_scalar(mrow[:, n % 2], mrow_i[:, n % 2], NEG_INF, None, ALU.mult).then_inc(mrow_ready, 1)

        def diagonal(n):
            pool.wait_ge(split_done, job[("MT", n)] + 1)
            if n >= 2:
                pool.wait_ge(st_ready, UNITS * (n - 1))
            for r in (0, 32):
                ins = pool.affine_select(
                    out=dg[n % 2][r:r + H], in_=nm[r:r + H].bitcast(F32).unsqueeze(1).to_broadcast((H, H, S)),
                    compare_op=ALU.is_equal, fill=0.0, base=0, pattern=[[-1, H], [0, S]], channel_multiplier=1)
                if r == 0:
                    after(ins)
            ins.then_inc(dg_ready, 1)
            pool.wait_ge(dg_ready, n + 1)

        def split_hidden0(i):
            pool.wait_ge(h_act, i + 1)
            if i >= 2:
                pool.wait_ge(y_ready, 4 * (i - 1))
            after(pool.tensor_copy(h0s[0][:, i % 2], h0[:, i % 2]))
            pool.tensor_tensor(h0s[1][:, i % 2], h0[:, i % 2], h0s[0][:, i % 2].bitcast(F32), ALU.subtract)\
                .then_inc(h_split, 1)

        for l in range(2):
            n0 = l * B
            if l == 1:
                pool.wait_ge(w_split, 2)
                pool.memset(w_raw[:, 0, 0], 0.0).then_inc(zeros_ready, 1)
            for n in (n0, n0 + 1):
                masked_queries(n, 0)
                masked_queries(n, 1)
                if l == 1:
                    mask_row(n)
            diagonal(n0)
            for n in range(n0 + 2, n0 + B):
                masked_queries(n, 0)
                diagonal(n - 1)
                masked_queries(n, 1)
                if l == 1:
                    mask_row(n)
            diagonal(n0 + B - 1)
            if l == 0:
                for i in range(2 * E):
                    split_hidden0(i)
        pool.wait_ge(attn_done, 2)
        pool.wait_ge(slots_zeroed, 16)
        pool.wait_ge(slots_ready, 1)
        for b in range(B):
            for c in range(TOP):
                pool.indirect_dma_start(out=x_slots, in_=xna[:, b], in_offset=None,
                                        out_offset=bass.IndirectOffsetOnAxis(ap=slot[:, c, b:b + 1], axis=0))\
                    .then_inc(scattered[b], 16)
        for i in range(2):
            pool.wait_ge(y_stored[i], 16 * (TILES // 2))
        for b in range(B):
            for c in range(TOP):
                pool.indirect_dma_start(out=yk[:, c, b], out_offset=None, in_=y_slots,
                                        in_offset=bass.IndirectOffsetOnAxis(ap=slot[:, c, b:b + 1], axis=0))\
                    .then_inc(gathered[b], 16)
        for b in range(B):
            pool.wait_ge(gathered[b], 16 * TOP)

    @block.tensor
    def _(pe):
        def begin(step):
            if job[step] >= 2:
                pe.wait_ge(split_done, job[step] - 1)
            return misc(step)

        def done(step):
            pe.wait_ge(split_done, job[step] + 1)

        def split_matmul(dst, pairs, first=True, last=True):
            for i, ((ah, al), (bh, bl)) in enumerate(pairs):
                for j, (a, b) in enumerate(((ah, bh), (ah, bl), (al, bh))):
                    ins = pe.matmul(dst, a, b, start=first and i == 0 and j == 0,
                                    stop=last and i == len(pairs) - 1 and j == 2)
            return ins

        def both(parts, *ix):
            return tuple(p[ix] for p in parts)

        A = slice(None)
        w_seen = set()

        def step_prep(s):
            dst = begin(s)
            if s[0] == "PB":
                pe.wait_ge(loaded_small, 16 * N_SMALL)
                pe.wait_ge(pool_const, 1)
                ins = pe.transpose(dst[:, 0:12], nat2[:], ident[0:12, 0:12])
            elif s[0] == "PM":
                pe.wait_ge(dve_prep, 1)
                for t in range(3):
                    ins = pe.transpose(dst[0:KT[t], 8 * t:8 * t + 8], mnat[:, 128 * t:128 * t + KT[t]], ident[0:8, 0:8])
            elif s[0] == "PF":
                for t in range(3):
                    ins = pe.transpose(dst[0:KT[t], S * t:S * t + S], fnat[:, 128 * t:128 * t + KT[t]],
                                       ident[0:S, 0:S])
            else:
                pe.wait_ge(dve_prep, 2)
                for k in range(DT):
                    for j in range(2):
                        c = 16 * k + 8 * j
                        ins = pe.transpose(dst[:, c:c + 8], cw[:, j, 128 * k:128 * k + 128], ident[0:8, 0:8])
            ins.then_inc(product, 1)

        def norm_transposes(s):
            dst = begin(s)
            _, i, b = s
            pe.wait_ge(pool_const, 1)
            pe.wait_ge(xn_ready, B * i + b + 1)
            for k in range(DT):
                src = xna[:, b] if i == 3 else xn[:, b % 2]
                ins = pe.transpose(dst[:, k * S:(k + 1) * S], src[:, 128 * k:128 * k + 128], ident[0:S, 0:S])
            ins.then_inc(product, 1)

        def queries(s):
            dst = begin(s)
            _, l, half, rt = s
            pe.wait_ge(w_split, l + 1)
            done(("LX", 2 * l, 4 * half + 3))
            t = slice(half * HALF, (half + 1) * HALF)
            split_matmul(dst[:, 0:HALF], [(both(w_at[l], A, 0, k, slice(128 * rt, 128 * rt + 128)),
                                           both(xT, A, k, t)) for k in range(DT)]).then_inc(product, 1)

        def context_transposes(s):
            dst = begin(s)
            _, n, k = s
            pe.wait_ge(loaded_ctx[n % 2], 32 * (n // 2 + 1))
            pe.wait_ge(pool_const, 1)
            for t in range(3):
                ins = pe.transpose(dst[:, 128 * t:128 * t + KT[t]], cnat[0:KT[t], n % 2, t, 128 * k:128 * k + 128],
                                   ident[0:KT[t], 0:KT[t]])
            ins.then_inc(product, 1)

        def keys(s):
            dst = begin(s)
            _, n, rt = s
            pe.wait_ge(w_split, n // B + 1)
            done(("CT", n, 1))
            split_matmul(dst[:, 0:NK + 1], [(both(w_at[n // B], A, 1, k, slice(128 * rt, 128 * rt + 128)),
                                             both(cT, A, k, slice(0, NK + 1))) for k in range(DT)])\
                .then_inc(product, 1)

        def values(s):
            dst = begin(s)
            _, n, t = s
            pe.wait_ge(w_split, n // B + 1)
            done(("CT", n, 1))
            split_matmul(dst[0:KT[t], 0:D], [(both(cT, A, k, slice(128 * t, 128 * t + KT[t])),
                                              both(w_at[n // B], A, 2, k, A)) for k in range(DT)])\
                .then_inc(product, 1)

        def plain_scores(s):
            _, n, h = s
            x_ = H * n + h
            if x_ >= 2:
                pe.wait_ge(max_done, x_ - 1)
            pe.wait_ge(qm_ready, 2 * n + h // 8 + 1)
            done(("KP", n, h // 8))
            pe.matmul(bank[3 + x_ % 2][0:S, 0:NK + 1], qm[n % 2][0][:, h // 8, h % 8, :], kT[n % 3][0][:, h // 8, :],
                      start=True, stop=True).then_inc(sn_ready, 1)

        def max_transpose(s):
            dst = begin(s)
            n = s[1]
            pe.wait_ge(max_twice, n + 1)
            pe.transpose(dst[0:48, 0:S], mx[:, n % 2], ident[0:S, 0:S]).then_inc(product, 1)

        def scores(s):
            _, n, u = s
            g, t = u // 3, u % 3
            U = UNITS * n + u
            rt, h0_ = g // 2, 4 * (g % 2)
            if n < B and U >= 3:
                pe.wait_ge(biased, U - 2)
            if n >= B:
                pe.wait_ge(exp_done, U - 2)
            pe.wait_ge(dg_ready, n + 1)
            dst = bank[U % 3][0:KT[t], 0:HALF].rearrange("p (h q) -> p h q", h=4)
            ks = slice(128 * t, 128 * t + KT[t])
            split_matmul(dst, [(both(kT[n % 3], A, rt, ks), both(qm[n % 2], A, rt, slice(h0_, h0_ + 4), A))],
                         last=False)
            pe.matmul(dst, ones[:, 0:KT[t]], dg[n % 2][:, 4 * g:4 * g + 4, :], start=False, stop=True)\
                .then_inc(st_ready, 1)

        def weighted_values(s):
            _, n, u = s
            g, t = u // 3, u % 3
            U = UNITS * n + u
            done(("VP", n, 2))
            pe.wait_ge(exp_done, U + 1)
            if u == 0 and n >= 1:
                pe.wait_ge(pv_out, n)
            for j in range(4):
                ins = pe.matmul(bank[5][32 * j:32 * j + 32, g * S:(g + 1) * S], vA[n % 3][0:KT[t], t, 4 * g + j, :],
                                pT[0:KT[t], U % 4, j * S:(j + 1) * S], start=(t == 0), stop=(t == 2),
                                tile_position=(0, 32 * j), skip_group_check=True)
            ins.then_inc(pv_done, 1)

        def out1(s):
            dst = begin(s)
            pe.wait_ge(pv_out, s[1] + 1)
            for g in range(4):
                ins = pe.transpose(dst[0:S, 128 * g:128 * g + 128], pv[:, g, :], ident[:])
            ins.then_inc(product, 1)

        def out2(s):
            dst = begin(s)
            done(("O1", s[1]))
            for k in range(2):
                ins = pe.transpose(dst[:, k * S:(k + 1) * S], an[:, 128 * k:128 * k + 128], ident[0:S, 0:S])
            ins.then_inc(product, 1)

        def out3(s):
            dst = begin(s)
            n = s[1]
            done(("O2", n))
            split_matmul(dst[0:S, 0:D], [(both(aT, A, k, A), both(w_at[n // B], A, 3, k, A)) for k in range(2)])\
                .then_inc(product, 1)

        def router(s):
            dst = begin(s)
            l = s[1]
            done(("LX", 2 * l + 1, B - 1))
            done(("PC", 0))
            cols = slice(0, 16) if l == 0 else slice(16, 24)
            wide = 16 if l == 0 else 8
            for b in range(B):
                ins = split_matmul(dst[0:S, 16 * b:16 * b + wide],
                                   [(both(xT, A, k, slice(b * S, b * S + S)), both(rtw, A, k, cols))
                                    for k in range(DT)])
            ins.then_inc(product, 1)

        def gate_transposes(s):
            dst = begin(s)
            pe.wait_ge(gates_ready, s[1] + 1)
            for j in range(4):
                ins = pe.transpose(dst[0:E, j * S:(j + 1) * S], gate[:, 4 * s[2] + j, :], ident[0:S, 0:S])
            ins.then_inc(product, 1)

        def gate_bias(s):
            dst = begin(s)
            _, l, b = s
            done(("GT", l, b // 4))
            pe.matmul(dst[0:S, 0:D], gT[:, b * S:(b + 1) * S], rows8[:, l, :], start=True, stop=True)\
                .then_inc(product, 1)

        def hidden0(s):
            _, e, half = s
            i = 2 * e + half
            if i >= 3:
                pe.wait_ge(h_act, i - 2)
            pe.wait_ge(v_split, e // 2 + 1)
            t = slice(half * HALF, (half + 1) * HALF)
            split_matmul(bank[i % 3][:, 0:HALF], [(both(e0, A, 0, e, slice(128 * k, 128 * k + 128)),
                                                   both(xT, A, k, t)) for k in range(DT)]).then_inc(h_ready, 1)

        def output0(s):
            _, e, b = s
            i = 2 * e + b // 4
            j = 4 * i + b % 4
            if j >= 3:
                pe.wait_ge(y_added, j - 2)
            pe.wait_ge(h_split, i + 1)
            t = slice((b % 4) * S, (b % 4) * S + S)
            split_matmul(bank[3 + j % 3][0:S, 0:D], [(both(h0s, A, i % 2, t), both(e0, A, 1, e, A))])\
                .then_inc(y_ready, 1)

        def count_choices(s):
            dst = begin(s)
            pe.wait_ge(counts_in, 1)
            for m in range(2):
                ins = pe.matmul(dst[0:S, 64 * m:64 * m + 64], tri[m][:], pkr[:], start=True, stop=True)
            ins.then_inc(product, 1)

        def rows_turned(s):
            dst = begin(s)
            j = s[1]
            pe.wait_ge(loaded_xs[j % 3], 16 * (j // 3 + 1))
            for k in range(DT):
                ins = pe.transpose(dst[:, 128 * k:128 * k + 128], xs[:, j % 3, 128 * k:128 * k + 128], ident[:])
            ins.then_inc(product, 1)

        def hidden1(s):
            _, j, m = s
            if j == 0:
                pe.wait_ge(y_added, Y0N)
            if j >= 1:
                pe.wait_ge(h_made, 2 * (j - 1) + m + 1)
            done(("XT", j))
            pe.wait_ge(r_split, 6 * j + 4)
            pe.wait_ge(loaded_bt[j % 2], 32 * (j // 2 + 1))
            f = slice(512 * m, 512 * m + 512)
            for w in range(2):
                dst = bank[2 * m + w][:]
                split_matmul(dst, [(both(xst[j % 2], A, k, A), both(e1[j % 2], A, 2 * w + k, f)) for k in range(DT)],
                             last=False)
                ins = pe.matmul(dst, ones[32 * w:32 * w + 2, :], bt[j % 2][32 * w:32 * w + 2, f], start=False, stop=True)
            ins.then_inc(h_ready, 1)

        def hidden_turned(s):
            _, j, m = s
            pe.wait_ge(h_made, 2 * j + m + 1)
            if j >= 1:
                pe.wait_ge(h_split, R16 + 2 * (j - 1) + m + 1)
            for f in range(4):
                ins = pe.transpose(bank[4 + m][:, 128 * f:128 * f + 128], h1f[:, m, 128 * f:128 * f + 128], ident[:])
            ins.then_inc(h_turned, 1)

        def output1(s):
            dst = begin(s)
            j = s[1]
            pe.wait_ge(h_split, R16 + 2 * j + 2)
            pe.wait_ge(r_split, 6 * j + 6)
            split_matmul(dst[:, 0:D],
                         [(both(h1s[j % 2], A, f, A),
                           both(e1[j % 2], A, 4 + f // 4, slice(D * (f % 4), D * (f % 4) + D))) for f in range(FT)])\
                .then_inc(product, 1)

        what = {"PB": step_prep, "PM": step_prep, "PF": step_prep, "PC": step_prep, "LX": norm_transposes,
                "Q": queries, "CT": context_transposes, "KP": keys, "VP": values, "SN": plain_scores,
                "MT": max_transpose, "ST": scores, "PV": weighted_values, "O1": out1, "O2": out2, "O3": out3,
                "R": router, "GT": gate_transposes, "GB": gate_bias, "H0": hidden0, "Y0": output0, "HP": hidden1,
                "HT": hidden_turned, "Y1": output1, "PS": count_choices, "XT": rows_turned}
        for s in order:
            if s[0] in what:
                what[s[0]](s)

    @block.scalar
    def _(act):
        n_sqrt = [0]

        def begin(step):
            act.wait_ge(product, job[step] + 1)
            return misc(step)

        def square_root(rows):
            n_sqrt[0] += 1
            act.wait_ge(var_ready, n_sqrt[0])
            act.activation(rows[1], rows[0], ACT.Sqrt).then_inc(sqrt_done, 1)

        def attention_weights(s):
            l = s[1]
            act.wait_ge(loaded_w[l], 64)
            act.activation(w_at[l][0][:, 0], w_raw[:, 0], ACT.Copy, scale=0.25)
            act.activation(w_at[l][0][:, 1:4], w_raw[:, 1:4], ACT.Copy).then_inc(w_high, 1)

        def norm_root(s):
            i = s[1]
            if i == 0:
                act.wait_ge(loaded_small, 16 * N_SMALL)
                act.activation(tg[:], tg[:], ACT.Tanh).then_inc(tanh_done, 1)
                square_root((crs[:, 0:1], crs[:, 1:2]))
            square_root((rs[:, 0], rs[:, 1]))

        def norm_high(s):
            src = begin(s)
            b = s[2]
            act.activation(xT[0][:, :, b * S:(b + 1) * S], src[:, 0:2 * S].rearrange("p (k q) -> p k q", k=2), ACT.Copy)\
                .then_inc(high_done, 1)

        def queries_high(s):
            src = begin(s)
            _, l, half, rt = s
            dst = qT[0][:, rt, half * HALF:(half + 1) * HALF]
            if l == 0:
                act.activation(dst, src[:, 0:HALF], ACT.Copy).then_inc(high_done, 1)
            else:
                act.activation(dst, src[:, 0:HALF], ACT.Identity, bias=colT[:, 8 + rt:9 + rt]).then_inc(high_done, 1)

        def context_high(s):
            src = begin(s)
            k = s[2]
            act.activation(cT[0][:, k, 0:NK], src[:, 0:NK], ACT.Copy).then_inc(high_done, 1)

        def keys_high(s):
            src = begin(s)
            _, n, rt = s
            dst = kT[n % 3][0][:, rt, :]
            if n < B:
                act.activation(dst, src[:, 0:NK + 1], ACT.Copy).then_inc(high_done, 1)
            else:
                act.activation(dst, src[:, 0:NK + 1], ACT.Identity, bias=colT[:, 10 + rt:11 + rt]).then_inc(high_done, 1)

        def max_high(s):
            src = begin(s)
            n = s[1]
            if n >= 1:
                act.wait_ge(dg_ready, n)
            act.activation(nm[:], src[0:48, 0:S], ACT.Copy, scale=-1.0).then_inc(high_done, 1)

        def exps(s):
            _, n, u = s
            t = u % 3
            U = UNITS * n + u
            if U >= 4:
                act.wait_ge(pv_done, U - 3)
            dst = pT[0:KT[t], U % 4]
            if n < B:
                act.wait_ge(biased, U + 1)
                act.activation(dst, sbias[0:KT[t], U % 3], ACT.Exp).then_inc(exp_done, 1)
            else:
                act.wait_ge(st_ready, U + 1)
                act.activation(dst, bank[U % 3][0:KT[t], 0:HALF], ACT.Exp,
                               bias=maskT[0:KT[t], t, n - B:n - B + 1]).then_inc(exp_done, 1)

        def evacuate(s):
            n = s[1]
            act.wait_ge(pv_done, UNITS * (n + 1))
            if n >= 1:
                act.wait_ge(product, job[("O1", n - 1)] + 1)
            act.activation(pv[:], bank[5][:, 0:4 * S].rearrange("p (g q) -> p g q", g=4), ACT.Copy).then_inc(pv_out, 1)

        def out_high(s):
            src = begin(s)
            act.activation(aT[0][:], src[:, 0:2 * S].rearrange("p (k q) -> p k q", k=2), ACT.Copy)\
                .then_inc(high_done, 1)

        def experts0_high(s):
            c = s[1]
            act.wait_ge(loaded_e0, 32)
            act.activation(e0[0][:, :, 2 * c:2 * c + 2], e0_raw[:, :, 2 * c:2 * c + 2], ACT.Copy).then_inc(v_high, 1)

        def router_exp(s):
            if s[1] == 0:
                square_root((rs[:, 0], rs[:, 1]))
            act.wait_ge(shifted, s[1] + 1)
            act.activation(gw[:, 3], gw[:, 2], ACT.Exp).then_inc(exp_gate, 1)

        def gelu(s):
            _, e, half = s
            i = 2 * e + half
            act.wait_ge(h_ready, i + 1)
            if i >= 2:
                act.wait_ge(h_split, i - 1)
            act.activation(h0[:, i % 2], bank[i % 3][:, 0:HALF], ACT.Gelu, bias=colT[:, e:e + 1]).then_inc(h_act, 1)

        def experts1_high(s):
            _, j, c = s
            act.wait_ge(loaded_raw[c], 16 * (j + 1))
            if j >= 2 and c == 0:
                act.wait_ge(h_ready, R16 + 2 * (j - 1))
            if j >= 2 and c == 4:
                act.wait_ge(product, job[("Y1", j - 2)] + 1)
            act.activation(e1[j % 2][0][:, c], e1_raw[:, c], ACT.Copy).then_inc(r_high, 1)

        def biases1_high(s):
            act.wait_ge(loaded_b, 32)
            act.activation(bsp[0][:], bnat[:], ACT.Copy).then_inc(b_high, 1)

        def rows_high(s):
            src = begin(s)
            j = s[1]
            act.activation(xst[j % 2][0][:], src[:, 0:D].rearrange("p (k q) -> p k q", k=2), ACT.Copy)\
                .then_inc(high_done, 1)

        def silu(s):
            _, j, m = s
            i = 2 * j + m
            act.wait_ge(h_ready, R16 + i + 1)
            if j >= 1:
                act.wait_ge(h_turned, 2 * (j - 1) + m + 1)
            act.activation(h1f[:, m], bank[2 * m][:], ACT.Silu).then_inc(h_act, 1)

        def hidden_high(s):
            _, j, m = s
            act.wait_ge(h_turned, 2 * j + m + 1)
            act.activation(h1s[j % 2][0][:, 4 * m:4 * m + 4], bank[4 + m][:].rearrange("p (f q) -> p f q", f=4),
                           ACT.Copy).then_inc(h_high, 1)

        what = {"AW": attention_weights, "LS": norm_root, "LX": norm_high, "Q": queries_high, "CT": context_high,
                "KP": keys_high, "MT": max_high, "ST": exps, "OE": evacuate, "O2": out_high, "V": experts0_high,
                "R": router_exp, "H0": gelu, "W": experts1_high, "BB": biases1_high, "XT": rows_high,
                "HP": silu, "HT": hidden_high}
        for s in order:
            if s[0] in what:
                what[s[0]](s)

    @block.vector
    def _(dve):
        steps = [0]

        def after(ins):
            steps[0] += 1
            ins.then_inc(dve_step, 1)
            dve.wait_ge(dve_step, steps[0])

        n_sqrt = [0]

        def inverse_root(v, y, t):
            n_sqrt[0] += 1
            dve.wait_ge(sqrt_done, n_sqrt[0])
            after(dve.reciprocal(y, y))
            after(dve.tensor_tensor(t, y, y, ALU.mult))
            after(dve.tensor_tensor(t, t, v, ALU.mult))
            after(dve.tensor_scalar(t, t, -0.5, 1.5, ALU.mult, ALU.add))
            after(dve.tensor_tensor(y, y, t, ALU.mult))

        def begin(step):
            dve.wait_ge(product, job[step] + 1)
            return misc(step)

        def high(step):
            dve.wait_ge(high_done, high_order[step] + 1)
            return begin(step)

        def attention_weights(s):
            l = s[1]
            dve.wait_ge(w_high, l + 1)
            dve.scalar_tensor_tensor(w_at[l][1][:, 0], w_raw[:, 0], 0.25, w_at[l][0][:, 0].bitcast(F32), ALU.mult,
                                     ALU.subtract)
            dve.tensor_tensor(w_at[l][1][:, 1:4], w_raw[:, 1:4], w_at[l][0][:, 1:4].bitcast(F32), ALU.subtract)\
                .then_inc(w_split, 1)

        def prepare():
            dve.wait_ge(pool_const, 1)
            dve.wait_ge(loaded_small, 16 * N_SMALL)
            dve.tensor_scalar(mnat[:], mnat_i[:], NEG_INF, None, ALU.mult).then_inc(dve_prep, 1)
            dve.tensor_copy(iota8[:], iota_i[:])
            dve.tensor_copy(mult128[:], mult_i[:])
            dve.tensor_copy(tile_no[:], tile_i[:])
            dve.tensor_tensor_reduce(sqj[0:E], cw[:, 0], cw[:, 0], 1.0, 0.0, ALU.mult, ALU.add, crs[:, 4:5])\
                .then_inc(dve_step, 1)
            steps[0] += 1
            dve.wait_ge(dve_step, steps[0])
            dve.tensor_scalar(crs[:, 0:1], crs[:, 4:5], 1e-24, None, ALU.max).then_inc(var_ready, 1)
            inverse_root(crs[:, 0:1], crs[:, 1:2], crs[:, 2:3])
            dve.tensor_scalar(cw[:, 0], cw[:, 0], crs[:, 1:2], None, ALU.mult).then_inc(dve_prep, 1)
            dve.wait_ge(tanh_done, 1)
            dve.tensor_scalar(bob[:], bob[:], tg[0:S, 1:2], None, ALU.mult)

        def norm_stats(s):
            i = s[1]
            if i == 0:
                prepare()
                dve.wait_ge(loaded_x, 16)
            for b in range(B):
                last = dve.bn_stats(stats[:, b], xres[:, b])
            after(last)
            for b in range(B):
                last = dve.bn_aggr(mv[:, b], stats[:, b])
            after(last)
            dve.tensor_scalar(rs[:, 0], mv[:, :, 1], LN_EPS, None, ALU.add).then_inc(var_ready, 1)
            inverse_root(rs[:, 0], rs[:, 1], rs[:, 2])

        def norm_low(s):
            _, i, b = s

            def normalise(c):
                if c >= 2:
                    dve.wait_ge(product, job[("LX", i, c - 2)] + 1)
                dst = xna[:, c] if i == 3 else xn[:, c % 2]
                ins = dve.tensor_scalar(dst, xres[:, c], mv[:, c, 0:1], rs[:, 1, c:c + 1], ALU.subtract, ALU.mult)
                ins.then_inc(xn_ready, 1)
                if i == 1:
                    dve.wait_ge(xn_ready, B * i + c + 1)
                    after(dve.tensor_tensor_reduce(sqj[:], xn[:, c % 2], xn[:, c % 2], 1.0, 0.0, ALU.mult, ALU.add,
                                                   ssq[:, c:c + 1]))

            if b == 0:
                normalise(0)
            if b + 1 < B:
                normalise(b + 1)
            src = high(s)
            t = slice(b * S, (b + 1) * S)
            dve.tensor_tensor(xT[1][:, :, t], src[:, 0:2 * S].rearrange("p (k q) -> p k q", k=2),
                              xT[0][:, :, t].bitcast(F32), ALU.subtract).then_inc(split_done, 1)

        def queries_low(s):
            src = high(s)
            _, l, half, rt = s
            t = slice(half * HALF, (half + 1) * HALF)
            if l == 0:
                dve.tensor_tensor(qT[1][:, rt, t], src[:, 0:HALF], qT[0][:, rt, t].bitcast(F32), ALU.subtract)\
                    .then_inc(split_done, 1)
            else:
                dve.scalar_tensor_tensor(qT[1][:, rt, t], src[:, 0:HALF], colT[:, 8 + rt:9 + rt],
                                         qT[0][:, rt, t].bitcast(F32), ALU.add, ALU.subtract).then_inc(split_done, 1)

        def context_low(s):
            src = high(s)
            k = s[2]
            dve.tensor_tensor(cT[1][:, k, 0:NK], src[:, 0:NK], cT[0][:, k, 0:NK].bitcast(F32), ALU.subtract)\
                .then_inc(split_done, 1)

        def keys_low(s):
            src = high(s)
            _, n, rt = s
            hi, lo = kT[n % 3][0][:, rt, 0:NK].bitcast(F32), kT[n % 3][1][:, rt, 0:NK]
            if n < B:
                dve.tensor_tensor(lo, src[:, 0:NK], hi, ALU.subtract).then_inc(split_done, 1)
            else:
                dve.scalar_tensor_tensor(lo, src[:, 0:NK], colT[:, 10 + rt:11 + rt], hi, ALU.add, ALU.subtract)\
                    .then_inc(split_done, 1)

        def values_out(s):
            src = begin(s)
            _, n, t = s
            dst = vA[n % 3][0:KT[t], t, :, 0:DH]
            v = src[0:KT[t], 0:D].rearrange("p (h d) -> p h d", h=H)
            if n < B:
                dve.tensor_copy(dst, v).then_inc(split_done, 1)
            else:
                dve.tensor_tensor(dst, v, bvb[0:KT[t], :].rearrange("p (h d) -> p h d", h=H), ALU.add)\
                    .then_inc(split_done, 1)

        def maxima(s):
            _, n, h = s
            x_ = H * n + h
            dve.wait_ge(sn_ready, x_ + 1)
            if n >= B and h == 0:
                dve.wait_ge(mrow_ready, n - B + 1)
            if x_ >= 2:
                dve.wait_ge(max_done, x_ - 1)
            add = fnat[:] if n < B else mrow[:, n % 2]
            dve.tensor_tensor_reduce(junk[:, x_ % 2], bank[3 + x_ % 2][0:S, 0:NK], add, 1.0, -3.0e38, ALU.add, ALU.max,
                                     mx[:, n % 2, h:h + 1]).then_inc(max_done, 1)
            if h == H - 1:
                dve.wait_ge(max_done, x_ + 1)
                dve.tensor_copy(mx[:, n % 2, 32:48], mx[:, n % 2, 0:16]).then_inc(max_twice, 1)

        def max_low(s):
            src = high(s)
            dve.scalar_tensor_tensor(nm[32:48], src[32:48, 0:S], -1.0, nm[32:48].bitcast(F32), ALU.mult, ALU.subtract)\
                .then_inc(split_done, 1)

        def bias_scores(s):
            _, n, u = s
            if n >= B:
                return
            t = u % 3
            U = UNITS * n + u
            dve.wait_ge(st_ready, U + 1)
            if U >= 3:
                dve.wait_ge(exp_done, U - 2)
            dve.tensor_tensor(sbias[0:KT[t], U % 3].rearrange("p (h q) -> p h q", h=4),
                              bank[U % 3][0:KT[t], 0:HALF].rearrange("p (h q) -> p h q", h=4),
                              fT[0:KT[t], t].unsqueeze(1).to_broadcast((KT[t], 4, S)), ALU.add).then_inc(biased, 1)

        def normalise_heads(s):
            src = begin(s)
            v = src[0:S, 0:512].rearrange("p (h c) -> p h c", c=32)
            after(dve.reciprocal(rden[:], v[:, :, DH]))
            dve.tensor_tensor(an[:].rearrange("p (h d) -> p h d", h=H), v[:, :, 0:DH],
                              rden[:].unsqueeze(2).to_broadcast((S, H, DH)), ALU.mult).then_inc(split_done, 1)

        def out_low(s):
            src = high(s)
            dve.tensor_tensor(aT[1][:], src[:, 0:2 * S].rearrange("p (k q) -> p k q", k=2), aT[0][:].bitcast(F32),
                              ALU.subtract).then_inc(split_done, 1)

        def add_attention(s):
            src = begin(s)
            n = s[1]
            l, b = n // B, n % B
            dve.scalar_tensor_tensor(xres[:, b], src[0:S, 0:D], tg[0:S, l:l + 1], xres[:, b], ALU.mult, ALU.add)\
                .then_inc(split_done, 1)
            dve.wait_ge(split_done, job[s] + 1)
            if l == 1:
                after(dve.tensor_tensor(xres[:, b], xres[:, b], bob[:], ALU.add))
            if b == B - 1:
                dve.tensor_copy(rs[:, 3], rs[:, 2]).then_inc(attn_done, 1)

        def prep_out(s):
            src = begin(s)
            if s[0] == "PB":
                after(dve.tensor_copy(colT[:], src[:, 0:12]))
                ins = dve.tensor_scalar(colT[:, 8:10], colT[:, 8:10], 0.25, None, ALU.mult)
            elif s[0] == "PM":
                for t in range(3):
                    ins = dve.tensor_copy(maskT[0:KT[t], t], src[0:KT[t], 8 * t:8 * t + 8])
            elif s[0] == "PF":
                for t in range(3):
                    ins = dve.tensor_copy(fT[0:KT[t], t], src[0:KT[t], S * t:S * t + S])
            else:
                after(dve.tensor_copy(rt_raw[:, :, 0:16], src[:, 0:32].rearrange("p (k c) -> p k c", k=2)))
                after(dve.tensor_copy(rtw[0][:], rt_raw[:]))
                ins = dve.tensor_tensor(rtw[1][:], rt_raw[:], rtw[0][:].bitcast(F32), ALU.subtract)
            ins.then_inc(split_done, 1)

        def experts0_low(s):
            c = s[1]
            p = slice(2 * c, 2 * c + 2)
            dve.wait_ge(v_high, c + 1)
            dve.tensor_tensor(e0[1][:, :, p], e0_raw[:, :, p], e0[0][:, :, p].bitcast(F32), ALU.subtract).then_inc(v_split, 1)

        def gates(s):
            l = s[1]
            src = begin(s)
            wide = 16 if l == 0 else 8
            dve.tensor_copy(lg[:, :, 0:wide], src[0:S, 0:16 * B].rearrange("p (b c) -> p b c", b=B)[:, :, 0:wide])\
                .then_inc(split_done, 1)
            dve.wait_ge(split_done, job[s] + 1)
            z, top, low, ex, pick, pick2, pr = (gw[:, i] for i in range(7))

            def wide_of(a):
                return a.to_broadcast((S, B, E))

            if l == 0:
                dve.tensor_scalar(rs[:, 0], ssq[:], 1e-24, None, ALU.max).then_inc(var_ready, 1)
                inverse_root(rs[:, 0], rs[:, 1], rs[:, 2])
                after(dve.tensor_tensor(z, lg[:, :, 0:8], wide_of(rs[:, 1].unsqueeze(2)), ALU.mult))
                after(dve.tensor_tensor(z, z, lg[:, :, 8:16], ALU.add))
            else:
                after(dve.tensor_tensor(z, lg[:, :, 0:8], wide_of(brb[:].unsqueeze(1)), ALU.add))
            for b in range(B):
                last = dve.max(top[:, b], z[:, b])
            after(last)
            dve.tensor_tensor(low, z, wide_of(top[:, :, 0:1]), ALU.subtract).then_inc(shifted, 1)
            if l == 0:
                after(dve.tensor_tensor(pick, z, wide_of(top[:, :, 1:2]), ALU.is_ge))
            else:
                for b in range(B):
                    last = dve.max_index(idx[:, b], top[:, b], z[:, b])
                after(last)
                after(dve.tensor_copy(pr, idx[:]))
                for c in range(TOP):
                    last = dve.tensor_tensor(pk[:, c], wide_of(iota8[:].unsqueeze(1)), wide_of(pr[:, :, c:c + 1]),
                                             ALU.is_equal)
                after(last)
                after(dve.tensor_tensor(pick, pk[:, 0], pk[:, 1], ALU.add))
                dve.tensor_copy(pkr[:], pick.rearrange("p b e -> p (b e)")).then_inc(counts_in, 1)
            dve.wait_ge(exp_gate, l + 1)
            after(dve.tensor_tensor(pick2, ex, pick, ALU.mult))
            after(dve.tensor_reduce(rs[:, 0], pick2, AX.X, ALU.add))
            after(dve.reciprocal(rs[:, 1], rs[:, 0]))
            after(dve.tensor_tensor(gate[:], pick2, wide_of(rs[:, 1].unsqueeze(2)), ALU.mult))
            dve.tensor_scalar(gate[:], gate[:], tg[0:S, 2 + l:3 + l], None, ALU.mult).then_inc(gates_ready, 1)
            dve.wait_ge(gates_ready, l + 1)

        def gates_turned(s):
            src = begin(s)
            dve.tensor_copy(gT[:, s[2] * HALF:(s[2] + 1) * HALF], src[0:E, 0:HALF]).then_inc(split_done, 1)

        def add_bias(s):
            src = begin(s)
            b = s[2]
            dve.tensor_tensor(xres[:, b], src[0:S, 0:D], xres[:, b], ALU.add).then_inc(split_done, 1)
            if b == B - 1:
                dve.wait_ge(split_done, job[s] + 1)

        def add_expert(j, src, e, b):
            dve.wait_ge(y_ready, j + 1)
            if j >= 1:
                dve.wait_ge(y_added, j)
            dve.scalar_tensor_tensor(xres[:, b], src[0:S, 0:D], gate[:, b, e:e + 1], xres[:, b], ALU.mult, ALU.add)\
                .then_inc(y_added, 1)

        def output0(s):
            _, e, b = s
            j = 4 * (2 * e + b // 4) + b % 4
            add_expert(j, bank[3 + j % 3], e, b)
            if j == Y0N - 1:
                dve.wait_ge(y_added, Y0N)

        def biases1_low(s):
            dve.wait_ge(b_high, 1)
            dve.tensor_tensor(bsp[1][:], bnat[:], bsp[0][:].bitcast(F32), ALU.subtract).then_inc(b_split, 1)

        def experts1_low(s):
            _, j, c = s
            dve.wait_ge(r_high, 6 * j + c + 1)
            dve.tensor_tensor(e1[j % 2][1][:, c], e1_raw[:, c], e1[j % 2][0][:, c].bitcast(F32), ALU.subtract)\
                .then_inc(r_split, 1)

        def place_choices(s):
            src = begin(s)
            dve.tensor_copy(cnt[:].rearrange("p m b e -> p (m b e)"), src[0:S, 0:2 * B * E]).then_inc(split_done, 1)
            dve.memset(off[:, 0], 0.0)
            dve.wait_ge(split_done, job[s] + 1)
            after(dve.tensor_copy(off[:, 1], cnt[:, 1, 0]))
            for b in range(1, B):
                after(dve.tensor_tensor(off[:, b + 1], off[:, b], cnt[:, 1, b], ALU.add))
            after(dve.tensor_tensor(cmp7[:], off[:, B].unsqueeze(2).to_broadcast((S, E, 7)),
                                    mult128[:].unsqueeze(1).to_broadcast((S, E, 7)), ALU.is_gt))
            after(dve.tensor_reduce(tl[:, 0], cmp7[:], AX.X, ALU.add))
            after(dve.tensor_tensor(tri8m[:], tl[:, 0].unsqueeze(1).to_broadcast((S, E, E)), tri8[:], ALU.mult))
            after(dve.tensor_reduce(tl[:, 1], tri8m[:], AX.X, ALU.add))
            after(dve.tensor_tensor(cmpt[:], tl[0:1, 1, 0:E - 1].unsqueeze(1).to_broadcast((1, TILES, E - 1)),
                                    tile_no[:].unsqueeze(2).to_broadcast((1, TILES, E - 1)), ALU.is_le))
            dve.memset(tex[:, 1], 1.0)
            after(dve.tensor_reduce(tex[:, 0], cmpt[:], AX.X, ALU.add))
            after(dve.tensor_tensor(tex[:, 1, 1:TILES], tex[:, 0, 1:TILES], tex[:, 0, 0:TILES - 1], ALU.not_equal))
            dve.tensor_copy(texi[:], tex[:]).then_inc(experts_known, 1)
            after(dve.tensor_tensor(tl[:, 2], tl[:, 1], tl[:, 0], ALU.subtract))
            after(dve.tensor_scalar(tl[:, 3], tl[:, 2], 128.0, None, ALU.mult))
            after(dve.tensor_tensor(pos[:], cnt[:, 0], off[:, 0:B], ALU.add))
            after(dve.tensor_tensor(pos[:], pos[:], tl[:, 3].unsqueeze(1).to_broadcast((S, B, E)), ALU.add))
            scratch = gw[:, 1:3]
            for c in range(TOP):
                last = dve.tensor_tensor(scratch[:, c], pk[:, c], pos[:], ALU.mult)
            after(last)
            after(dve.tensor_reduce(posk[:], scratch, AX.X, ALU.add))
            after(dve.tensor_copy(slot[:], posk[:]))
            for c in range(TOP):
                last = dve.tensor_tensor(scratch[:, c], pk[:, c], gate[:], ALU.mult)
            after(last)
            dve.tensor_reduce(gk[:], scratch, AX.X, ALU.add).then_inc(slots_ready, 1)
            dve.wait_ge(slots_ready, 1)

        def rows_low(s):
            src = high(s)
            j = s[1]
            dve.tensor_tensor(xst[j % 2][1][:], src[:, 0:D].rearrange("p (k q) -> p k q", k=2),
                              xst[j % 2][0][:].bitcast(F32), ALU.subtract).then_inc(split_done, 1)

        def hidden1(s):
            _, j, m = s
            i = 2 * j + m
            dve.wait_ge(h_act, R16 + i + 1)
            dve.tensor_tensor(h1f[:, m], bank[2 * m + 1][:], h1f[:, m], ALU.mult).then_inc(h_made, 1)

        def hidden_low(s):
            _, j, m = s
            dve.wait_ge(h_high, 2 * j + m + 1)
            f = slice(4 * m, 4 * m + 4)
            dve.tensor_tensor(h1s[j % 2][1][:, f], bank[4 + m][:].rearrange("p (f q) -> p f q", f=4),
                              h1s[j % 2][0][:, f].bitcast(F32), ALU.subtract).then_inc(h_split, 1)

        def output1(s):
            src = begin(s)
            j = s[1]
            if j >= 2:
                dve.wait_ge(y_stored[j % 2], 16 * (j // 2))
            dve.tensor_copy(yo[:, j % 2], src[:, 0:D]).then_inc(split_done, 1)

        def combine(s):
            for b in range(B):
                dve.wait_ge(gathered[b], 16 * TOP)
                for c in range(TOP):
                    ins = dve.scalar_tensor_tensor(xres[:, b], yk[:, c, b], gk[:, c, b:b + 1], xres[:, b], ALU.mult,
                                                   ALU.add)
                    if c == 0:
                        after(ins)
                ins.then_inc(moe_done, 1)

        what = {"AW": attention_weights, "PB": prep_out, "PM": prep_out, "PF": prep_out, "PC": prep_out,
                "LS": norm_stats, "LX": norm_low, "Q": queries_low, "CT": context_low, "KP": keys_low,
                "VP": values_out, "SN": maxima, "MT": max_low, "ST": bias_scores, "O1": normalise_heads,
                "O2": out_low, "O3": add_attention, "V": experts0_low, "R": gates, "GT": gates_turned,
                "GB": add_bias, "Y0": output0, "Y1": output1, "W": experts1_low, "HP": hidden1,
                "BB": biases1_low, "PS": place_choices, "XT": rows_low, "HT": hidden_low, "GA": combine}
        for s in order:
            if s[0] in what:
                what[s[0]](s)

    st.close()


_INS = ["x", "ctx_1024", "fside_1x1xSxS2_0", "mask_Bx1x1xS2_ik0", "g_xattn", "g_ffn",
        "L0_xattn_wq", "L0_xattn_wk", "L0_xattn_wv", "L0_xattn_wo",
        "L0_ffn_w1", "L0_ffn_b1", "L0_ffn_w2", "L0_ffn_b2", "L0_ffn_centroids", "L0_ffn_w_route",
        "L1_xattn_wq", "L1_xattn_bq", "L1_xattn_wk", "L1_xattn_bk", "L1_xattn_wv", "L1_xattn_bv",
        "L1_xattn_wo", "L1_xattn_bo",
        "L1_ffn_Wr", "L1_ffn_br", "L1_ffn_W1", "L1_ffn_b1", "L1_ffn_W2", "L1_ffn_b2", "L1_ffn_W3", "L1_ffn_b3"]


def kernel(**inputs):
    import numpy as _np
    import concourse.bacc as _bacc
    from concourse import mybir as _mybir
    from concourse.bass_utils import run_bass_kernel_spmd as _run

    nc = _bacc.Bacc("TRN2", target_bir_lowering=False, num_devices=1)
    arrays, aps = {}, {}
    for name in _INS:
        a = _np.ascontiguousarray(inputs[name])
        if name in ("L0_xattn_wq", "L0_xattn_wk", "L0_xattn_wv", "L0_xattn_wo"):
            a = a.reshape(D, D)
        arrays[f"in_{name}_dram"] = a
        aps[name] = nc.dram_tensor(f"in_{name}_dram", a.shape, _mybir.dt.from_np(a.dtype), kind="ExternalInput").ap()
    out = nc.dram_tensor("out_0_dram", (B, S, D), F32, kind="ExternalOutput").ap()

    def part(prefix):
        return {name[len(prefix):]: ap for name, ap in aps.items() if name.startswith(prefix)}

    gated_layers(nc, aps["x"], aps["ctx_1024"], aps["fside_1x1xSxS2_0"], aps["mask_Bx1x1xS2_ik0"], aps["g_xattn"],
                 aps["g_ffn"], part("L0_xattn_"), part("L0_ffn_"), part("L1_xattn_"), part("L1_ffn_"), out)
    r = _run(nc, [arrays], core_ids=[0])
    return r.results[0]["out_0_dram"]
```

```python
from contextlib import ExitStack

import concourse.bass as bass
from concourse import mybir

ALU = mybir.AluOpType
ACT = mybir.ActivationFunctionType
F32 = mybir.dt.float32
F32R = mybir.dt.float32r
I32 = mybir.dt.int32
U32 = mybir.dt.uint32
AX = mybir.AxisListType

B, S, D = 8, 100, 256
NK = 361
KT = [128, 128, NK - 256]
H, DH = 16, 16
DT = D // 128
E = 8
HID = 128
FF = 1024
FT = FF // 128
HALF = 4 * S
LN_EPS = 1e-5
NEG_INF = -1000000000.0
TOP = 2
TILES = (TOP * B * S + E * 127) // 128
SCORE_ROWS = 98
UNITS = 12


def context(n):
    return [("CT", n, 0), ("CT", n, 1)], [("KP", n, 0), ("KP", n, 1)], [("VP", n, 0), ("VP", n, 1), ("VP", n, 2)]


def attention_order(layer):
    n0 = layer * B
    order = [("SN", n0, h) for h in range(H)] + [("MT", n0)] + [("SN", n0 + 1, h) for h in range(4)]
    for b in range(B):
        n = n0 + b
        heads = [("SN", n + 1, h) for h in range(4 if b == 0 else 0, H)] if b + 1 < B else []
        for u in range(UNITS):
            order.append(("ST", n, u))
            order += heads[:1]
            if u >= 2:
                order.append(("PV", n, u - 2))
            order += heads[1:2]
            heads = heads[2:]
            if b >= 1:
                order += {2: [("O1", n - 1)], 6: [("O2", n - 1)], 9: [("O3", n - 1)]}.get(u, [])
            if b + 2 < B:
                transposes, keys, values = context(n + 2)
                order += {1: transposes, 3: keys, 10: values}.get(u, [])
            if u == 8 and b + 1 < B:
                order.append(("MT", n + 1))
        order += [("PV", n, UNITS - 2), ("PV", n, UNITS - 1), ("OE", n)]
    order += [("O1", n0 + B - 1), ("O2", n0 + B - 1), ("O3", n0 + B - 1)]
    return order


def norm_order(s):
    order = [("LS", s)] + [("LX", s, b) for b in range(B)]
    if s % 2:
        order = order[:6] + [("RL", s // 2, 0)] + order[6:] + [("RL", s // 2, 1)]
    return order


def query_order(layer):
    return [("Q", layer, half, rt) for half in range(2) for rt in range(2)]


def ffn0_order():
    order = [("V", 0), ("R", 0), ("G", 0)] + [("V", c) for c in range(1, 4)]
    steps = [(e, half) for e in range(E) for half in range(2)]
    for i, (e, half) in enumerate(steps):
        order.append(("H0", e, half))
        if i >= 1:
            pe, ph = steps[i - 1]
            order += [("Y0", pe, ph * 4 + j) for j in range(4)]
        order.append(("HS", e, half))
        if i == 1:
            order += [("GT", 0, 0), ("GT", 0, 1)]
        if 2 <= i < 2 + B:
            order.append(("GB", 0, i - 2))
        if i < 4:
            order.append(("AW", 1, i))
        if i in (6, 8, 10):
            order += context(B)[i // 2 - 3]
    order += [("Y0", E - 1, 4 + j) for j in range(4)]
    return order


def ffn1_order():
    order = [("R", 1), ("PS",), ("BB",), ("G", 1)]
    order += [("W", 0, c) for c in range(6)]
    order += [("GT", 1, 0), ("GT", 1, 1)] + [("GB", 1, b) for b in range(B)] + [("XT", 0), ("XT", 1)]
    for j in range(TILES + 1):
        if j + 1 < TILES:
            order += [("W", j + 1, 0), ("W", j + 1, 1)]
        if j < TILES:
            order.append(("HP", j, 0))
        if j >= 1:
            order.append(("HT", j - 1, 1))
        if j + 1 < TILES:
            order.append(("W", j + 1, 2))
        if j < TILES:
            order.append(("HP", j, 1))
        if j + 1 < TILES:
            order.append(("W", j + 1, 3))
        if j < TILES:
            order.append(("HT", j, 0))
        if j >= 1:
            order.append(("Y1", j - 1))
        if j + 1 < TILES:
            order += [("W", j + 1, c) for c in (4, 5)]
        if j + 2 < TILES:
            order.append(("XT", j + 2))
    return order + [("GA",)]


def gated_layers(nc, x, ctx, fside, mask, g_xattn, g_ffn, w0, f0, w1, f1, out):
    prep = [("PB", 0), ("PM", 0), ("PC", 0)]
    order = (norm_order(0) + [("AW", 0, c) for c in range(4)] + query_order(0) + sum(context(0), [])
             + [("PR", 0)] + prep + sum(context(1), []) + attention_order(0)
             + norm_order(1) + ffn0_order()
             + norm_order(2) + query_order(1) + sum(context(B + 1), []) + attention_order(1)
             + norm_order(3) + ffn1_order())
    shared = [s for s in order if s[0] in ("PB", "PM", "PF", "PC", "LX", "Q", "CT", "KP", "VP", "MT",
                                           "O1", "O2", "O3", "RL", "R", "GT", "GB", "PS", "XT", "Y1")]
    job = {s: i for i, s in enumerate(shared)}
    high_order = {s: i for i, s in enumerate([s for s in shared if s[0] in ("LX", "Q", "CT", "KP", "MT", "O2", "XT")])}

    st = ExitStack()

    def sb(name, shape, dt=F32, stack=None):
        return (stack or st).enter_context(nc.sbuf_tensor(name, shape, dt))

    def sem(name):
        return st.enter_context(nc.semaphore(name))

    bank = [st.enter_context(nc.psum_tensor(f"bank{i}", [128, 512], F32)) for i in range(8)]

    def misc(step):
        return bank[6 + job[step] % 2]

    xres = sb("xres", [S, B, D])
    xT = [sb("xT_hi", [128, DT, B * S], F32R), sb("xT_lo", [128, DT, B * S], F32R)]
    xn = sb("xn", [S, 3, D])
    stats = sb("stats", [S, B, 6])
    mv = sb("mv", [S, B, 2])
    rs = sb("rs", [S, 4, B])
    ssq = sb("ssq", [S, B])
    sqj = sb("sqj", [S, D])
    ident = sb("ident", [128, 128])
    ones = sb("ones", [48, 128], F32R)
    onesf = sb("onesf", [48, 128])
    tg = sb("tg", [128, 4])
    colT = sb("colT", [128, 12])
    rows8 = sb("rows8", [E, 2, D])
    rt_raw = sb("rt_raw", [128, DT, 24])
    rtw = [sb("rt_hi", [128, DT, 24], F32R), sb("rt_lo", [128, DT, 24], F32R)]
    brb = sb("brb", [S, E])
    lg = sb("lg", [S, B, 16])
    gw = sb("gw", [S, 7, B, E])
    gate = sb("gate", [S, B, E])
    iota_i = sb("iota_i", [S, E], I32)
    iota8 = sb("iota8", [S, E])
    tri = [sb("tri", [S, S], F32R), sb("all_ones", [S, S], F32R)]
    trif = sb("trif", [S, S])
    mult_i = sb("mult_i", [S, 7], I32)
    mult128 = sb("mult128", [S, 7])
    tri8 = sb("tri8", [S, E, E])
    tile_i = sb("tile_i", [1, TILES], I32)
    tile_no = sb("tile_no", [1, TILES])
    gT = sb("gT", [2 * E, B * S])
    nat2 = sb("nat2", [12, 128])
    cw = sb("cw", [E, 2, D])
    crs = sb("crs", [E, 6])

    at = ExitStack()
    w_raw = sb("w_raw", [128, 4, DT, D], F32, at)
    w_at = [sb(f"w_{p}", [128, 4, DT, D], F32R, at) for p in ("hi", "lo")]
    bvb = sb("bvb", [128, D], F32, at)
    bob = sb("bob", [S, D], F32, at)
    fnat = sb("fnat", [S, NK], F32, at)
    fr = [sb("f_hi", [S, NK], F32R, at), sb("f_lo", [S, NK], F32R, at)]
    ident4 = sb("ident4", [S, 4, S], F32R, at)
    mnat_i = sb("mnat_i", [B, NK], I32, at)
    mnat = sb("mnat", [B, NK], F32, at)
    maskT = sb("maskT", [128, 3, B], F32, at)
    mrow_i = sb("mrow_i", [S, 2, NK], I32, at)
    mrow = sb("mrow", [S, 2, NK], F32, at)
    hmask = sb("hmask", [96, 2], F32, at)
    cnat = sb("cnat", [128, 2, 3, D], F32, at)
    vA = [sb(f"v{i}", [128, 3, H, 32], F32, at) for i in range(3)]
    mx = sb("mx", [S, 2, 48], F32, at)
    nm = sb("nm", [48, S], F32R, at)
    ks = [sb(f"ks{i}", [SCORE_ROWS, H // 2, NK + 1], F32R, at) for i in range(3)]
    cT = [sb("c_hi", [128, DT, NK + 1], F32R, at), sb("c_lo", [128, DT, NK + 1], F32R, at)]
    kT = [sb(f"k_{p}", [128, 2, NK + 1], F32R, at) for p in ("hi", "lo")]
    a1 = ExitStack()
    qT = [sb("q_hi", [128, 2, B * S], F32R, a1), sb("q_lo", [128, 2, B * S], F32R, a1)]
    qs = sb("qs", [96, H // 2, HALF], F32R, a1)
    qm = [sb(f"qm{i}", [SCORE_ROWS, H, S], F32R, a1) for i in range(3)]
    junk = sb("junk", [S, 2, NK], F32, a1)
    pT = sb("pT", [128, 4, 4 * S], F32, a1)
    pv = sb("pv", [128, 4, S], F32, a1)
    rden = sb("rden", [S, H], F32, a1)
    an = sb("an", [S, D], F32, a1)
    aT = [sb("a_hi", [128, 2, S], F32R, a1), sb("a_lo", [128, 2, S], F32R, a1)]
    a1.close()
    m0 = ExitStack()
    e0_raw = sb("e0_raw", [128, 2, E, 256], F32, m0)
    e0 = [sb("e0_hi", [128, 2, E, 256], F32R, m0), sb("e0_lo", [128, 2, E, 256], F32R, m0)]
    h0 = sb("h0", [128, 2, HALF], F32, m0)
    h0s = [sb("h0_hi", [128, 2, HALF], F32R, m0), sb("h0_lo", [128, 2, HALF], F32R, m0)]
    m0.close()
    at.close()
    m1 = ExitStack()
    e1_raw = sb("e1_raw", [128, 6, 1024], F32, m1)
    e1 = [[sb(f"e1{i}_{p}", [128, 6, 1024], F32R, m1) for p in ("hi", "lo")] for i in range(2)]
    bt = [sb(f"bt{i}", [34, FF], F32R, m1) for i in range(2)]
    xna = sb("xna", [S, B, D], F32, m1)
    idx = sb("idx", [S, B, 8], U32, m1)
    pk = sb("pk", [S, TOP, B, E], F32, m1)
    pkr = sb("pkr", [S, B * E], F32R, m1)
    cnt = sb("cnt", [S, 2, B, E], F32, m1)
    off = sb("off", [S, B + 1, E], F32, m1)
    pos = sb("pos", [S, B, E], F32, m1)
    posk = sb("posk", [S, TOP, B], F32, m1)
    slot = sb("slot", [S, TOP, B], U32, m1)
    gk = sb("gk", [S, TOP, B], F32, m1)
    tl = sb("tl", [S, 4, E], F32, m1)
    cmp7 = sb("cmp7", [S, E, 7], F32, m1)
    tri8m = sb("tri8m", [S, E, E], F32, m1)
    cmpt = sb("cmpt", [1, TILES, E - 1], F32, m1)
    tex = sb("tex", [1, 2, TILES], F32, m1)
    texi = sb("texi", [1, 2, TILES], I32, m1)
    mb = ExitStack()
    bnat = sb("bnat", [E, 2, FF], F32, mb)
    bsp = [sb("b_hi", [E, 2, FF], F32R, mb), sb("b_lo", [E, 2, FF], F32R, mb)]
    mb.close()
    m2 = ExitStack()
    xs = sb("xs", [128, 3, D], F32, m2)
    xst = [[sb(f"xst{i}_{p}", [128, DT, 128], F32R, m2) for p in ("hi", "lo")] for i in range(2)]
    h1f = sb("h1f", [128, 2, 512], F32, m2)
    h1s = [[sb(f"h1{i}_{p}", [128, FT, 128], F32R, m2) for p in ("hi", "lo")] for i in range(2)]
    yo = sb("yo", [128, 2, D], F32, m2)
    m2.close()
    yk = sb("yk", [S, TOP, B, D], F32, m1)
    m1.close()

    loaded_x, loaded_small, out_done = sem("loaded_x"), sem("loaded_small"), sem("out_done")
    loaded_w = [sem("loaded_w0"), sem("loaded_w1")]
    loaded_ctx = [sem("loaded_ctx0"), sem("loaded_ctx1")]
    loaded_mask = [sem("loaded_mask0"), sem("loaded_mask1")]
    loaded_e0 = sem("loaded_e0")
    loaded_raw = [sem(f"loaded_raw{i}") for i in range(6)]
    loaded_xs = [sem(f"loaded_xs{i}") for i in range(3)]
    loaded_bt = [sem(f"loaded_bt{i}") for i in range(2)]
    loaded_b, b_split, b_stored = sem("loaded_b"), sem("b_split"), sem("b_stored")
    slots_zeroed, zeros_ready, slots_ready, scattered = (sem("slots_zeroed"), sem("zeros_ready"), sem("slots_ready"),
                                                         [sem(f"scattered{b}") for b in range(B)])
    experts_known, counts_in, y_stored, gathered = (sem("experts_known"), sem("counts_in"),
                                                    [sem("y_stored0"), sem("y_stored1")],
                                                    [sem(f"gathered{b}") for b in range(B)])
    h_turned = sem("h_turned")
    first_const = sem("first_const")
    pool_const, pool_step, dve_step, dve_prep = sem("pool_const"), sem("pool_step"), sem("dve_step"), sem("dve_prep")
    tanh_done, var_ready, sqrt_done = sem("tanh_done"), sem("var_ready"), sem("sqrt_done")
    w_high, w_split, xn_ready = sem("w_high"), sem("w_split"), sem("xn_ready")
    product, high_done, split_done = sem("product"), sem("high_done"), sem("split_done")
    qm_ready, mrow_ready = sem("qm_ready"), sem("mrow_ready")
    ks_loaded, qs_loaded, max_loaded = ([sem(f"ks_loaded{i}") for i in range(3)], sem("qs_loaded"),
                                        [sem(f"max_loaded{i}") for i in range(2)])
    sn_ready, max_done, max_twice = sem("sn_ready"), sem("max_done"), sem("max_twice")
    st_ready, f_split, exp_done, pv_done, pv_out = (sem("st_ready"), sem("f_split"), sem("exp_done"), sem("pv_done"),
                                                   sem("pv_out"))
    attn_done, moe_done = sem("attn_done"), sem("moe_done")
    b_high = sem("b_high")
    v_high, v_split, shifted, exp_gate, gates_ready = (sem("v_high"), sem("v_split"), sem("shifted"),
                                                       sem("exp_gate"), sem("gates_ready"))
    h_ready, h_act, h_made, h_high, h_split = sem("h_ready"), sem("h_act"), sem("h_made"), sem("h_high"), sem("h_split")
    y_ready, y_added = sem("y_ready"), sem("y_added")
    r_high, r_split, r_split_pool = sem("r_high"), sem("r_split"), sem("r_split_pool")

    x_slots = nc.dram_tensor("x_slots", (TILES * 128, D), F32).ap()
    y_slots = nc.dram_tensor("y_slots", (TILES * 128, D), F32).ap()
    b_parts = nc.dram_tensor("b_parts", (2, E, 2, FF), F32).ap()

    N_SMALL = 15
    POOL_PIECES = (4, 5)
    w3v = f1["W3"].rearrange("e (j p) d -> e p j d", p=128)

    Y0N = 4 * 2 * E
    R16 = 2 * E

    block = st.enter_context(nc.Block())

    def piece_split(engine, j, c):
        if c in POOL_PIECES:
            engine.wait_ge(r_split_pool, len(POOL_PIECES) * j + POOL_PIECES.index(c) + 1)
        else:
            engine.wait_ge(r_split, (6 - len(POOL_PIECES)) * j + c + 1 - sum(p < c for p in POOL_PIECES))

    def load_rows(sp, j):
        if j >= 3:
            sp.wait_ge(product, job[("XT", j - 3)] + 1)
        sp.dma_start(xs[:, j % 3], x_slots[128 * j:128 * j + 128]).then_inc(loaded_xs[j % 3], 16)

    @block.sync
    def _(sp):
        def load_context(n):
            b = n % B
            if n >= 2:
                sp.wait_ge(product, job[("CT", n - 2, 1)] + 1)
            sp.dma_start(cnat[:, n % 2, 0:2], ctx[b, 0:256].rearrange("(t p) d -> p t d", p=128))\
                .then_inc(loaded_ctx[n % 2], 16)
            sp.dma_start(cnat[0:KT[2], n % 2, 2], ctx[b, 256:NK]).then_inc(loaded_ctx[n % 2], 16)

        def load_mask(n):
            if n >= B + 2:
                sp.wait_ge(mrow_ready, n - B - 1)
            sp.dma_start(mrow_i[:, n % 2], mask[n % B, 0].to_broadcast((S, NK))).then_inc(loaded_mask[n % 2], 16)

        def load_weights(l, w):
            for i, name in enumerate(("wq", "wk", "wv", "wo")):
                sp.dma_start(w_raw[:, i], w[name].rearrange("(k p) n -> p k n", p=128)).then_inc(loaded_w[l], 16)

        sp.dma_start(xres[:], x.rearrange("b s d -> s b d")).then_inc(loaded_x, 16)
        load_weights(0, w0)
        load_context(0)
        small = [(nat2[0:8, :], f0["b1"]),
                 (nat2[8:10, :], w1["bq"].rearrange("(a p) -> a p", p=128)),
                 (nat2[10:12, :], w1["bk"].rearrange("(a p) -> a p", p=128)),
                 (rows8[:, 0, :], f0["b2"]), (rows8[:, 1, :], f1["b3"]),
                 (cw[:, 0, :], f0["centroids"]), (cw[:, 1, :], f0["w_route"]),
                 (rt_raw[:, :, 16:24], f1["Wr"].rearrange("(k p) e -> p k e", p=128)),
                 (brb[:], f1["br"].rearrange("(a e) -> a e", a=1).to_broadcast((S, E))),
                 (tg[:, 0:2], g_xattn.rearrange("(a e) -> a e", a=1).to_broadcast((128, 2))),
                 (tg[:, 2:4], g_ffn.rearrange("(a e) -> a e", a=1).to_broadcast((128, 2))),
                 (fnat[:], fside[0, 0]), (mnat_i[:], mask.rearrange("b u v k -> (b u v) k")),
                 (bvb[:], w1["bv"].rearrange("(a e) -> a e", a=1).to_broadcast((128, D))),
                 (bob[:], w1["bo"].rearrange("(a e) -> a e", a=1).to_broadcast((S, D)))]
        assert len(small) == N_SMALL
        for dst, src in small:
            sp.dma_start(dst, src).then_inc(loaded_small, 16)
        load_context(1)
        def store_strips(dst, parts, cols, loaded):
            for strip, part in enumerate(parts):
                for i in range(4):
                    sp.dma_start(
                        dst[32 * strip:32 * strip + 32].rearrange("p (rt i) n -> p rt i n", i=4)[:, :, i, :].bitcast(F32),
                        part[32 * i:32 * i + 32, :, cols].bitcast(F32)).then_inc(loaded, 16)

        def key_strips(n):
            sp.wait_ge(split_done, job[("KP", n, 1)] + 1)
            if n >= 3:
                sp.wait_ge(st_ready, UNITS * (n - 2))
            store_strips(ks[n % 3], (kT[0], kT[1], kT[0]), slice(0, NK + 1), ks_loaded[n % 3])

        def query_strips(l, half):
            sp.wait_ge(split_done, job[("Q", l, half, 1)] + 1)
            if l or half:
                sp.wait_ge(qm_ready, B * l + 4 * half)
            store_strips(qs, (qT[0], qT[0], qT[1]), slice(half * HALF, half * HALF + HALF), qs_loaded)

        sp.wait_ge(w_split, 4)
        load_weights(1, w1)
        for s in order:
            if s[0] == "Q" and s[2:] == (0, 1):
                query_strips(s[1], 0)
            elif s[0] == "CT" and s[2] == 1 and s[1] + 2 < 2 * B:
                load_context(s[1] + 2)
            elif s[0] == "KP" and s[2] == 1:
                n = s[1]
                key_strips(n)
                if n % B == 3:
                    query_strips(n // B, 1)
            elif s[0] == "SN" and s[2] == 0 and B < s[1] < 2 * B - 1:
                load_mask(s[1] + 1)
            elif s == ("LS", 1):
                sp.wait_ge(attn_done, 1)
                sp.dma_start(e0_raw[:, 0].rearrange("p e (k h) -> p (e k) h", k=2),
                             f0["w1"].rearrange("e (k p) h -> p (e k) h", p=128)).then_inc(loaded_e0, 16)
                sp.dma_start(e0_raw[:, 1], f0["w2"].rearrange("e p d -> p e d")).then_inc(loaded_e0, 16)
                load_mask(B)
                load_mask(B + 1)
            elif s == ("MT", B):
                sp.wait_ge(zeros_ready, 1)
                sp.dma_start(x_slots.rearrange("(r p) d -> p r d", p=128),
                             w_raw[:, 0, 0].unsqueeze(1).to_broadcast((128, TILES, D))).then_inc(slots_zeroed, 16)
        sp.wait_ge(attn_done, 2)
        sp.dma_start(bnat[:, 0], f1["b1"]).then_inc(loaded_b, 16)
        sp.dma_start(bnat[:, 1], f1["b2"]).then_inc(loaded_b, 16)

        def store_rows(j):
            sp.wait_ge(split_done, job[("Y1", j)] + 1)
            sp.dma_start(y_slots[128 * j:128 * j + 128], yo[:, j % 2]).then_inc(y_stored[j % 2], 16)

        def load_pieces(j, expert, differs, pieces):
            for c in pieces:
                if j >= 1:
                    piece_split(sp, j - 1, c)
                if c < 4:
                    src = f1["W1" if c < 2 else "W2"][bass.ds(expert, 1), 128 * (c % 2):128 * (c % 2) + 128, :]
                    src, dst = src.rearrange("o p f -> p (o f)"), e1_raw[:, c]
                else:
                    src = w3v[bass.ds(expert, 1), :, 4 * (c - 4):4 * (c - 4) + 4, :]
                    src, dst = src.rearrange("o p j d -> p (o j) d"), e1_raw[:, c].rearrange("p (j d) -> p j d", j=4)
                sp.dma_start(dst, src, cond=differs).then_inc(loaded_raw[c], 16)

        sp.wait_ge(experts_known, 1)
        for j in range(TILES):
            if j >= 2:
                load_pieces(j - 1, *last, range(4, 6))
            expert = sp.value_load(texi[0:1, 0, j:j + 1], min_val=0, max_val=E - 1)
            differs = sp.value_load(texi[0:1, 1, j:j + 1], min_val=0, max_val=1)
            load_pieces(j, expert, differs, range(4) if j else range(6))
            last = (expert, differs)
            if j == 0:
                sp.wait_ge(b_split, 1)
                for p in range(2):
                    sp.dma_start(b_parts[:, :, p].rearrange("w e f -> e w f"), bsp[p][:].bitcast(F32)).then_inc(b_stored, 16)
                sp.wait_ge(b_stored, 32)
            if j >= 2:
                sp.wait_ge(h_ready, R16 + 2 * (j - 1))
            for w in range(2):
                sp.dma_start(bt[j % 2][32 * w:32 * w + 2].bitcast(F32),
                             b_parts[w][bass.ds(expert, 1)].rearrange("o p f -> (o p) f")).then_inc(loaded_bt[j % 2], 16)
            if j == 0:
                for b in range(B):
                    sp.wait_ge(scattered[b], 16 * TOP)
                load_rows(sp, 0)
                load_rows(sp, 1)
            if j + 2 < TILES:
                load_rows(sp, j + 2)
            if j >= 3:
                store_rows(j - 3)
        load_pieces(TILES - 1, *last, range(4, 6))
        for j in range(TILES - 3, TILES):
            store_rows(j)
        for b in range(0, B, 2):
            sp.wait_ge(moe_done, b + 2)
            sp.dma_start(out[b:b + 2].rearrange("b s d -> s b d"), xres[:, b:b + 2]).then_inc(out_done, 16)
        sp.wait_ge(out_done, 16 * (B // 2))

    @block.gpsimd
    def _(pool):
        steps = [0]

        def after(ins):
            steps[0] += 1
            ins.then_inc(pool_step, 1)
            pool.wait_ge(pool_step, steps[0])

        after(pool.memset(ident[:], 0.0))
        after(pool.affine_select(out=ident[:], in_=ident[:], compare_op=ALU.not_equal, fill=1.0, base=0,
                                 pattern=[[-1, 128]], channel_multiplier=1))
        after(pool.iota(iota_i[:], pattern=[[1, E]], base=0, channel_multiplier=0))
        after(pool.iota(mult_i[:], pattern=[[128, 7]], base=0, channel_multiplier=0))
        after(pool.iota(tile_i[:], pattern=[[1, TILES]], base=0, channel_multiplier=0))
        after(pool.tensor_copy(ident4[:], ident[0:S, 0:S].unsqueeze(1).to_broadcast((S, 4, S))))
        for part in cT:
            after(pool.memset(part[:, :, NK:NK + 1].bitcast(F32), 0.0))
        pool.memset(trif[:], 1.0).then_inc(first_const, 1)
        pool.wait_ge(first_const, 1)
        for i in range(3):
            strip = hmask[32 * i:32 * i + 32]
            after(pool.memset(strip, 1.0))
            after(pool.affine_select(out=strip, in_=strip, compare_op=ALU.is_ge, fill=0.0, base=0,
                                     pattern=[[-DH, 2]], channel_multiplier=1))
            after(pool.affine_select(out=strip, in_=strip, compare_op=ALU.is_ge, fill=0.0, base=DH - 1,
                                     pattern=[[DH, 2]], channel_multiplier=-1))
            after(pool.memset(ks[i][96:SCORE_ROWS].bitcast(F32), 1.0))
        after(pool.memset(tri8[:], 1.0))
        after(pool.affine_select(out=tri8[:], in_=tri8[:], compare_op=ALU.is_ge, fill=0.0, base=0,
                                 pattern=[[1, E], [-1, E]], channel_multiplier=0))
        after(pool.tensor_copy(tri[1][:], trif[:]))
        after(pool.affine_select(out=trif[:], in_=trif[:], compare_op=ALU.is_gt, fill=0.0, base=0,
                                 pattern=[[1, S]], channel_multiplier=-1))
        after(pool.tensor_copy(tri[0][:], trif[:]))
        for i in range(3):
            after(pool.memset(vA[i][:], 0.0))
            after(pool.memset(vA[i][:, :, :, DH:DH + 1], 1.0))
        after(pool.memset(onesf[:], 1.0))
        after(pool.tensor_copy(ones[:], onesf[:]))
        pool.memset(mx[:], 0.0).then_inc(pool_const, 1)

        def masked_queries(n):
            b = n % B
            pool.wait_ge(qs_loaded, 16 * 12 * (n // 4 + 1))
            if n >= 3:
                pool.wait_ge(st_ready, UNITS * (n - 2))
            pool.tensor_tensor(
                qm[n % 3][0:96].rearrange("p (g h) q -> p g h q", h=2),
                qs[:, :, b % 4 * S:b % 4 * S + S].bitcast(F32).unsqueeze(2).to_broadcast((96, H // 2, 2, S)),
                hmask[:].unsqueeze(1).unsqueeze(3).to_broadcast((96, H // 2, 2, S)), ALU.mult).then_inc(qm_ready, 1)
            pool.wait_ge(qm_ready, n + 1)

        def mask_row(n):
            pool.wait_ge(loaded_mask[n % 2], 16 * ((n - B) // 2 + 1))
            if n >= B + 2:
                pool.wait_ge(max_done, H * (n - 1))
            pool.tensor_scalar(mrow[:, n % 2], mrow_i[:, n % 2], NEG_INF, None, ALU.mult).then_inc(mrow_ready, 1)

        def max_rows(n):
            pool.wait_ge(split_done, job[("MT", n)] + 1)
            for r in range(2):
                pool.dma_start(qm[n % 3][96 + r:97 + r].bitcast(F32), nm[32 * r:32 * r + H].bitcast(F32))\
                    .then_inc(max_loaded[n % 2], 16)

        for l in range(2):
            n0 = l * B
            if l == 1:
                pool.wait_ge(w_split, 8)
                pool.memset(w_raw[:, 0, 0], 0.0).then_inc(zeros_ready, 1)
            for n in (n0, n0 + 1):
                masked_queries(n)
                if l == 1:
                    mask_row(n)
            max_rows(n0)
            for n in range(n0 + 2, n0 + B):
                masked_queries(n)
                max_rows(n - 1)
                if l == 1:
                    mask_row(n)
            max_rows(n0 + B - 1)
        pool.wait_ge(attn_done, 2)
        def split_pieces(j):
            for c in POOL_PIECES:
                pool.wait_ge(r_high, 6 * j + c + 1)
                pool.tensor_tensor(e1[j % 2][1][:, c], e1_raw[:, c], e1[j % 2][0][:, c].bitcast(F32), ALU.subtract)\
                    .then_inc(r_split_pool, 1)

        pool.wait_ge(slots_zeroed, 16)
        pool.wait_ge(slots_ready, 1)
        for b in range(B):
            for c in range(TOP):
                pool.indirect_dma_start(out=x_slots, in_=xna[:, b], in_offset=None,
                                        out_offset=bass.IndirectOffsetOnAxis(ap=slot[:, c, b:b + 1], axis=0))\
                    .then_inc(scattered[b], 16)
        for j in range(TILES):
            split_pieces(j)
        for i in range(2):
            pool.wait_ge(y_stored[i], 16 * (TILES // 2))
        for b in range(B):
            for c in range(TOP):
                pool.indirect_dma_start(out=yk[:, c, b], out_offset=None, in_=y_slots,
                                        in_offset=bass.IndirectOffsetOnAxis(ap=slot[:, c, b:b + 1], axis=0))\
                    .then_inc(gathered[b], 16)
        for b in range(B):
            pool.wait_ge(gathered[b], 16 * TOP)

    @block.tensor
    def _(pe):
        def begin(step):
            if job[step] >= 2:
                pe.wait_ge(split_done, job[step] - 1)
            return misc(step)

        def done(step):
            pe.wait_ge(split_done, job[step] + 1)

        def split_matmul(dst, pairs, first=True, last=True):
            for i, ((ah, al), (bh, bl)) in enumerate(pairs):
                for j, (a, b) in enumerate(((ah, bh), (ah, bl), (al, bh))):
                    ins = pe.matmul(dst, a, b, start=first and i == 0 and j == 0,
                                    stop=last and i == len(pairs) - 1 and j == 2)
            return ins

        def both(parts, *ix):
            return tuple(p[ix] for p in parts)

        A = slice(None)
        w_seen = set()

        def step_prep(s):
            dst = begin(s)
            if s[0] == "PB":
                pe.wait_ge(loaded_small, 16 * N_SMALL)
                pe.wait_ge(first_const, 1)
                ins = pe.transpose(dst[:, 0:12], nat2[:], ident[0:12, 0:12])
            elif s[0] == "PM":
                pe.wait_ge(dve_prep, 1)
                for t in range(3):
                    ins = pe.transpose(dst[0:KT[t], 8 * t:8 * t + 8], mnat[:, 128 * t:128 * t + KT[t]], ident[0:8, 0:8])
            else:
                pe.wait_ge(dve_prep, 2)
                for k in range(DT):
                    for j in range(2):
                        c = 16 * k + 8 * j
                        ins = pe.transpose(dst[:, c:c + 8], cw[:, j, 128 * k:128 * k + 128], ident[0:8, 0:8])
            ins.then_inc(product, 1)

        def norm_transposes(s):
            dst = begin(s)
            _, i, b = s
            pe.wait_ge(first_const, 1)
            pe.wait_ge(xn_ready, B * i + b + 1)
            for k in range(DT):
                src = xna[:, b] if i == 3 else xn[:, b % 3]
                ins = pe.transpose(dst[:, k * S:(k + 1) * S], src[:, 128 * k:128 * k + 128], ident[0:S, 0:S])
            ins.then_inc(product, 1)

        def queries(s):
            dst = begin(s)
            _, l, half, rt = s
            pe.wait_ge(w_split, 4 * (l + 1))
            done(("LX", 2 * l, 4 * half + 3))
            t = slice(half * HALF, (half + 1) * HALF)
            split_matmul(dst[:, 0:HALF], [(both(w_at, A, 0, k, slice(128 * rt, 128 * rt + 128)),
                                           both(xT, A, k, t)) for k in range(DT)]).then_inc(product, 1)

        def context_transposes(s):
            dst = begin(s)
            _, n, k = s
            pe.wait_ge(loaded_ctx[n % 2], 32 * (n // 2 + 1))
            pe.wait_ge(first_const, 1)
            for t in range(3):
                ins = pe.transpose(dst[:, 128 * t:128 * t + KT[t]], cnat[0:KT[t], n % 2, t, 128 * k:128 * k + 128],
                                   ident[0:KT[t], 0:KT[t]])
            ins.then_inc(product, 1)

        def keys(s):
            dst = begin(s)
            _, n, rt = s
            pe.wait_ge(w_split, 4 * (n // B + 1))
            done(("CT", n, 1))
            split_matmul(dst[:, 0:NK + 1], [(both(w_at, A, 1, k, slice(128 * rt, 128 * rt + 128)),
                                             both(cT, A, k, slice(0, NK + 1))) for k in range(DT)])\
                .then_inc(product, 1)

        def values(s):
            dst = begin(s)
            _, n, t = s
            pe.wait_ge(w_split, 4 * (n // B + 1))
            done(("CT", n, 1))
            split_matmul(dst[0:KT[t], 0:D], [(both(cT, A, k, slice(128 * t, 128 * t + KT[t])),
                                              both(w_at, A, 2, k, A)) for k in range(DT)])\
                .then_inc(product, 1)

        def plain_scores(s):
            _, n, h = s
            x_ = H * n + h
            if x_ >= 3:
                pe.wait_ge(max_done, x_ - 2)
            pe.wait_ge(qm_ready, n + 1)
            pe.wait_ge(ks_loaded[n % 3], 16 * 12 * (n // 3 + 1))
            pe.matmul(bank[2 + x_ % 3][0:S, 0:NK + 1], qm[n % 3][0:96, h, :], ks[n % 3][0:96, h // 2, :],
                      start=True, stop=True).then_inc(sn_ready, 1)

        def max_transpose(s):
            dst = begin(s)
            n = s[1]
            pe.wait_ge(max_twice, n + 1)
            pe.transpose(dst[0:48, 0:S], mx[:, n % 2], ident[0:S, 0:S]).then_inc(product, 1)

        def scores(s):
            _, n, u = s
            g, t = u // 3, u % 3
            U = UNITS * n + u
            if U >= 2:
                pe.wait_ge(exp_done, U - 1)
            if n < B:
                pe.wait_ge(f_split, 1)
                for i, part in enumerate(fr):
                    pe.matmul(bank[U % 2][0:KT[t], 0:HALF], part[:, 128 * t:128 * t + KT[t]], ident4[:],
                              start=(i == 0), stop=False)
            if U == 0:
                pe.wait_ge(pool_const, 1)
            pe.wait_ge(max_loaded[n % 2], 32 * (n // 2 + 1))
            for g2 in (2 * g, 2 * g + 1):
                c = 2 * S * (g2 % 2)
                ins = pe.matmul(bank[U % 2][0:KT[t], c:c + 2 * S], ks[n % 3][:, g2, 128 * t:128 * t + KT[t]],
                                qm[n % 3][:, 2 * g2:2 * g2 + 2, :], start=(n >= B), stop=(n >= B or g2 % 2 == 1))
            ins.then_inc(st_ready, 1)

        def weighted_values(s):
            _, n, u = s
            g, t = u // 3, u % 3
            U = UNITS * n + u
            done(("VP", n, 2))
            pe.wait_ge(exp_done, U + 1)
            if u == 0 and n >= 1:
                pe.wait_ge(pv_out, n)
            for j in range(4):
                ins = pe.matmul(bank[5][32 * j:32 * j + 32, g * S:(g + 1) * S], vA[n % 3][0:KT[t], t, 4 * g + j, :],
                                pT[0:KT[t], U % 4, j * S:(j + 1) * S], start=(t == 0), stop=(t == 2),
                                tile_position=(0, 32 * j), skip_group_check=True)
            ins.then_inc(pv_done, 1)

        def out1(s):
            dst = begin(s)
            pe.wait_ge(pv_out, s[1] + 1)
            for g in range(4):
                ins = pe.transpose(dst[0:S, 128 * g:128 * g + 128], pv[:, g, :], ident[:])
            ins.then_inc(product, 1)

        def out2(s):
            dst = begin(s)
            done(("O1", s[1]))
            for k in range(2):
                ins = pe.transpose(dst[:, k * S:(k + 1) * S], an[:, 128 * k:128 * k + 128], ident[0:S, 0:S])
            ins.then_inc(product, 1)

        def out3(s):
            dst = begin(s)
            n = s[1]
            done(("O2", n))
            split_matmul(dst[0:S, 0:D], [(both(aT, A, k, A), both(w_at, A, 3, k, A)) for k in range(2)])\
                .then_inc(product, 1)

        def router_products(s):
            dst = begin(s)
            _, l, half = s
            done(("LX", 2 * l + 1, 4 * half + 3))
            done(("PC", 0))
            cols = slice(0, 16) if l == 0 else slice(16, 24)
            wide = 16 if l == 0 else 8
            split_matmul(dst[0:wide, 0:HALF], [(both(rtw, A, k, cols),
                                                both(xT, A, k, slice(half * HALF, half * HALF + HALF)))
                                               for k in range(DT)]).then_inc(product, 1)

        def router(s):
            dst = begin(s)
            l = s[1]
            done(("RL", l, 1))
            wide = 16 if l == 0 else 8
            for b in range(B):
                ins = pe.transpose(dst[0:S, 16 * b:16 * b + wide], gT[0:wide, b * S:(b + 1) * S], ident[0:wide, 0:wide])
            ins.then_inc(product, 1)

        def gate_transposes(s):
            dst = begin(s)
            pe.wait_ge(gates_ready, s[1] + 1)
            for j in range(4):
                ins = pe.transpose(dst[0:E, j * S:(j + 1) * S], gate[:, 4 * s[2] + j, :], ident[0:S, 0:S])
            ins.then_inc(product, 1)

        def gate_bias(s):
            dst = begin(s)
            _, l, b = s
            done(("GT", l, b // 4))
            pe.matmul(dst[0:S, 0:D], gT[0:E, b * S:(b + 1) * S], rows8[:, l, :], start=True, stop=True)\
                .then_inc(product, 1)

        def hidden0(s):
            _, e, half = s
            i = 2 * e + half
            if i >= 3:
                pe.wait_ge(h_act, i - 2)
            pe.wait_ge(v_split, e // 2 + 1)
            t = slice(half * HALF, (half + 1) * HALF)
            split_matmul(bank[i % 3][:, 0:HALF], [(both(e0, A, 0, e, slice(128 * k, 128 * k + 128)),
                                                   both(xT, A, k, t)) for k in range(DT)]).then_inc(h_ready, 1)

        def output0(s):
            _, e, b = s
            i = 2 * e + b // 4
            j = 4 * i + b % 4
            if j >= 3:
                pe.wait_ge(y_added, j - 2)
            pe.wait_ge(h_split, i + 1)
            t = slice((b % 4) * S, (b % 4) * S + S)
            split_matmul(bank[3 + j % 3][0:S, 0:D], [(both(h0s, A, i % 2, t), both(e0, A, 1, e, A))])\
                .then_inc(y_ready, 1)

        def count_choices(s):
            dst = begin(s)
            pe.wait_ge(counts_in, 1)
            for m in range(2):
                ins = pe.matmul(dst[0:S, 64 * m:64 * m + 64], tri[m][:], pkr[:], start=True, stop=True)
            ins.then_inc(product, 1)

        def rows_turned(s):
            dst = begin(s)
            j = s[1]
            pe.wait_ge(loaded_xs[j % 3], 16 * (j // 3 + 1))
            for k in range(DT):
                ins = pe.transpose(dst[:, 128 * k:128 * k + 128], xs[:, j % 3, 128 * k:128 * k + 128], ident[:])
            ins.then_inc(product, 1)

        def hidden1(s):
            _, j, m = s
            if j == 0:
                pe.wait_ge(y_added, Y0N)
            if j >= 1:
                pe.wait_ge(h_made, 2 * (j - 1) + m + 1)
            done(("XT", j))
            for c in (2, 3):
                piece_split(pe, j, c)
            pe.wait_ge(loaded_bt[j % 2], 32 * (j // 2 + 1))
            f = slice(512 * m, 512 * m + 512)
            for w in range(2):
                dst = bank[2 * m + w][:]
                split_matmul(dst, [(both(xst[j % 2], A, k, A), both(e1[j % 2], A, 2 * w + k, f)) for k in range(DT)],
                             last=False)
                ins = pe.matmul(dst, ones[32 * w:32 * w + 2, :], bt[j % 2][32 * w:32 * w + 2, f], start=False, stop=True)
            ins.then_inc(h_ready, 1)

        def hidden_turned(s):
            _, j, m = s
            pe.wait_ge(h_made, 2 * j + m + 1)
            if j >= 1:
                pe.wait_ge(h_split, R16 + 2 * (j - 1) + m + 1)
            for f in range(4):
                ins = pe.transpose(bank[4 + m][:, 128 * f:128 * f + 128], h1f[:, m, 128 * f:128 * f + 128], ident[:])
            ins.then_inc(h_turned, 1)

        def output1(s):
            dst = begin(s)
            j = s[1]
            pe.wait_ge(h_split, R16 + 2 * j + 2)
            for c in (4, 5):
                piece_split(pe, j, c)
            split_matmul(dst[:, 0:D],
                         [(both(h1s[j % 2], A, f, A),
                           both(e1[j % 2], A, 4 + f // 4, slice(D * (f % 4), D * (f % 4) + D))) for f in range(FT)])\
                .then_inc(product, 1)

        what = {"PB": step_prep, "PM": step_prep, "PF": step_prep, "PC": step_prep, "LX": norm_transposes,
                "Q": queries, "CT": context_transposes, "KP": keys, "VP": values, "SN": plain_scores,
                "MT": max_transpose, "ST": scores, "PV": weighted_values, "O1": out1, "O2": out2, "O3": out3,
                "RL": router_products, "R": router, "GT": gate_transposes, "GB": gate_bias, "H0": hidden0, "Y0": output0, "HP": hidden1,
                "HT": hidden_turned, "Y1": output1, "PS": count_choices, "XT": rows_turned}
        for s in order:
            if s[0] in what:
                what[s[0]](s)

    @block.scalar
    def _(act):
        n_sqrt = [0]

        def begin(step):
            act.wait_ge(product, job[step] + 1)
            return misc(step)

        def square_root(rows):
            n_sqrt[0] += 1
            act.wait_ge(var_ready, n_sqrt[0])
            act.activation(rows[1], rows[0], ACT.Sqrt).then_inc(sqrt_done, 1)

        def attention_weights(s):
            _, l, c = s
            act.wait_ge(loaded_w[l], 64)
            if l == 1:
                act.wait_ge(product, job[("O3", B - 1)] + 1)
            act.activation(w_at[0][:, c], w_raw[:, c], ACT.Copy, scale=0.25 if c == 0 else 1.0).then_inc(w_high, 1)

        def norm_root(s):
            i = s[1]
            square_root((rs[:, 0], rs[:, 1]))

        def prepare(s):
            act.wait_ge(loaded_small, 16 * N_SMALL)
            square_root((crs[:, 0:1], crs[:, 1:2]))
            act.activation(tg[:], tg[:], ACT.Tanh).then_inc(tanh_done, 1)

        def norm_high(s):
            src = begin(s)
            b = s[2]
            act.activation(xT[0][:, :, b * S:(b + 1) * S], src[:, 0:2 * S].rearrange("p (k q) -> p k q", k=2), ACT.Copy)\
                .then_inc(high_done, 1)

        def queries_high(s):
            src = begin(s)
            _, l, half, rt = s
            dst = qT[0][:, rt, half * HALF:(half + 1) * HALF]
            if l == 1:
                act.wait_ge(qs_loaded, 2 * 16 * 12)
            if l == 0:
                act.activation(dst, src[:, 0:HALF], ACT.Copy).then_inc(high_done, 1)
            else:
                act.activation(dst, src[:, 0:HALF], ACT.Identity, bias=colT[:, 8 + rt:9 + rt]).then_inc(high_done, 1)

        def context_high(s):
            src = begin(s)
            k = s[2]
            act.activation(cT[0][:, k, 0:NK], src[:, 0:NK], ACT.Copy).then_inc(high_done, 1)

        def keys_high(s):
            src = begin(s)
            _, n, rt = s
            dst = kT[0][:, rt, :]
            if n >= 1:
                act.wait_ge(ks_loaded[(n - 1) % 3], 16 * 12 * ((n - 1) // 3 + 1))
            if n < B:
                act.activation(dst, src[:, 0:NK + 1], ACT.Copy).then_inc(high_done, 1)
            else:
                act.activation(dst, src[:, 0:NK + 1], ACT.Identity, bias=colT[:, 10 + rt:11 + rt]).then_inc(high_done, 1)

        def max_high(s):
            src = begin(s)
            n = s[1]
            if n >= 1:
                act.wait_ge(max_loaded[(n - 1) % 2], 32 * ((n - 1) // 2 + 1))
            act.activation(nm[:], src[0:48, 0:S], ACT.Copy, scale=-1.0).then_inc(high_done, 1)

        def exps(s):
            _, n, u = s
            t = u % 3
            U = UNITS * n + u
            if U >= 4:
                act.wait_ge(pv_done, U - 3)
            dst = pT[0:KT[t], U % 4]
            act.wait_ge(st_ready, U + 1)
            if n < B:
                act.activation(dst, bank[U % 2][0:KT[t], 0:HALF], ACT.Exp).then_inc(exp_done, 1)
            else:
                act.activation(dst, bank[U % 2][0:KT[t], 0:HALF], ACT.Exp,
                               bias=maskT[0:KT[t], t, n - B:n - B + 1]).then_inc(exp_done, 1)

        def evacuate(s):
            n = s[1]
            act.wait_ge(pv_done, UNITS * (n + 1))
            if n >= 1:
                act.wait_ge(product, job[("O1", n - 1)] + 1)
            act.activation(pv[:], bank[5][:, 0:4 * S].rearrange("p (g q) -> p g q", g=4), ACT.Copy).then_inc(pv_out, 1)

        def out_high(s):
            src = begin(s)
            act.activation(aT[0][:], src[:, 0:2 * S].rearrange("p (k q) -> p k q", k=2), ACT.Copy)\
                .then_inc(high_done, 1)

        def experts0_high(s):
            c = s[1]
            act.wait_ge(loaded_e0, 32)
            act.activation(e0[0][:, :, 2 * c:2 * c + 2], e0_raw[:, :, 2 * c:2 * c + 2], ACT.Copy).then_inc(v_high, 1)

        def router_exp(s):
            if s[1] == 0:
                square_root((rs[:, 0], rs[:, 1]))
            act.wait_ge(shifted, s[1] + 1)
            act.activation(gw[:, 3], gw[:, 2], ACT.Exp).then_inc(exp_gate, 1)

        def gelu(s):
            _, e, half = s
            i = 2 * e + half
            act.wait_ge(h_ready, i + 1)
            if i >= 2:
                act.wait_ge(h_split, i - 1)
            act.activation(h0[:, i % 2], bank[i % 3][:, 0:HALF], ACT.Gelu, bias=colT[:, e:e + 1]).then_inc(h_act, 1)
            if i >= 2:
                act.wait_ge(y_ready, 4 * (i - 1))
            act.wait_ge(h_act, i + 1)
            act.activation(h0s[0][:, i % 2], h0[:, i % 2], ACT.Copy).then_inc(h_high, 1)

        def experts1_high(s):
            _, j, c = s
            act.wait_ge(loaded_raw[c], 16 * (j + 1))
            if j >= 2 and c == 0:
                act.wait_ge(h_ready, R16 + 2 * (j - 1))
            if j >= 2 and c == 4:
                act.wait_ge(product, job[("Y1", j - 2)] + 1)
            act.activation(e1[j % 2][0][:, c], e1_raw[:, c], ACT.Copy).then_inc(r_high, 1)

        def biases1_high(s):
            act.wait_ge(loaded_b, 32)
            act.activation(bsp[0][:], bnat[:], ACT.Copy).then_inc(b_high, 1)

        def rows_high(s):
            src = begin(s)
            j = s[1]
            act.activation(xst[j % 2][0][:], src[:, 0:D].rearrange("p (k q) -> p k q", k=2), ACT.Copy)\
                .then_inc(high_done, 1)

        def silu(s):
            _, j, m = s
            i = 2 * j + m
            act.wait_ge(h_ready, R16 + i + 1)
            if j >= 1:
                act.wait_ge(h_turned, 2 * (j - 1) + m + 1)
            act.activation(h1f[:, m], bank[2 * m][:], ACT.Silu).then_inc(h_act, 1)

        def hidden_high(s):
            _, j, m = s
            act.wait_ge(h_turned, 2 * j + m + 1)
            act.activation(h1s[j % 2][0][:, 4 * m:4 * m + 4], bank[4 + m][:].rearrange("p (f q) -> p f q", f=4),
                           ACT.Copy).then_inc(h_high, 1)

        what = {"AW": attention_weights, "PR": prepare, "LS": norm_root, "LX": norm_high, "Q": queries_high, "CT": context_high,
                "KP": keys_high, "MT": max_high, "ST": exps, "OE": evacuate, "O2": out_high, "V": experts0_high,
                "R": router_exp, "H0": gelu, "W": experts1_high, "BB": biases1_high, "XT": rows_high,
                "HP": silu, "HT": hidden_high}
        for s in order:
            if s[0] in what:
                what[s[0]](s)

    @block.vector
    def _(dve):
        steps = [0]

        def after(ins):
            steps[0] += 1
            ins.then_inc(dve_step, 1)
            dve.wait_ge(dve_step, steps[0])

        n_sqrt = [0]

        def inverse_root(v, y, t):
            n_sqrt[0] += 1
            dve.wait_ge(sqrt_done, n_sqrt[0])
            after(dve.reciprocal(y, y))
            after(dve.tensor_tensor(t, y, y, ALU.mult))
            after(dve.tensor_tensor(t, t, v, ALU.mult))
            after(dve.tensor_scalar(t, t, -0.5, 1.5, ALU.mult, ALU.add))
            after(dve.tensor_tensor(y, y, t, ALU.mult))

        def begin(step):
            dve.wait_ge(product, job[step] + 1)
            return misc(step)

        def high(step):
            dve.wait_ge(high_done, high_order[step] + 1)
            return begin(step)

        def attention_weights(s):
            _, l, c = s
            dve.wait_ge(w_high, 4 * l + c + 1)
            hi, lo = w_at[0][:, c].bitcast(F32), w_at[1][:, c]
            if c == 0:
                dve.scalar_tensor_tensor(lo, w_raw[:, c], 0.25, hi, ALU.mult, ALU.subtract).then_inc(w_split, 1)
            else:
                dve.tensor_tensor(lo, w_raw[:, c], hi, ALU.subtract).then_inc(w_split, 1)

        def prepare(s):
            dve.wait_ge(first_const, 1)
            dve.wait_ge(loaded_small, 16 * N_SMALL)
            dve.tensor_scalar(mnat[:], mnat_i[:], NEG_INF, None, ALU.mult).then_inc(dve_prep, 1)
            dve.tensor_copy(iota8[:], iota_i[:])
            dve.tensor_copy(mult128[:], mult_i[:])
            dve.tensor_copy(tile_no[:], tile_i[:])
            dve.tensor_tensor_reduce(sqj[0:E], cw[:, 0], cw[:, 0], 1.0, 0.0, ALU.mult, ALU.add, crs[:, 4:5])\
                .then_inc(dve_step, 1)
            steps[0] += 1
            dve.wait_ge(dve_step, steps[0])
            dve.tensor_scalar(crs[:, 0:1], crs[:, 4:5], 1e-24, None, ALU.max).then_inc(var_ready, 1)
            inverse_root(crs[:, 0:1], crs[:, 1:2], crs[:, 2:3])
            dve.tensor_scalar(cw[:, 0], cw[:, 0], crs[:, 1:2], None, ALU.mult).then_inc(dve_prep, 1)
            dve.wait_ge(tanh_done, 1)
            dve.tensor_scalar(bob[:], bob[:], tg[0:S, 1:2], None, ALU.mult)
            after(dve.tensor_copy(fr[0][:], fnat[:]))
            dve.tensor_tensor(fr[1][:], fnat[:], fr[0][:].bitcast(F32), ALU.subtract).then_inc(f_split, 1)

        def norm_stats(s):
            i = s[1]
            if i == 0:
                dve.wait_ge(loaded_x, 16)
            if i % 2 == 0:
                for b in range(B):
                    last = dve.bn_stats(stats[:, b], xres[:, b])
                after(last)
                for b in range(B):
                    last = dve.bn_aggr(mv[:, b], stats[:, b])
                after(last)
            dve.tensor_scalar(rs[:, 0], mv[:, :, 1], LN_EPS, None, ALU.add).then_inc(var_ready, 1)
            inverse_root(rs[:, 0], rs[:, 1], rs[:, 2])

        def norm_low(s):
            _, i, b = s

            def normalise(c):
                if c >= 3:
                    dve.wait_ge(product, job[("LX", i, c - 3)] + 1)
                dst = xna[:, c] if i == 3 else xn[:, c % 3]
                ins = dve.tensor_scalar(dst, xres[:, c], mv[:, c, 0:1], rs[:, 1, c:c + 1], ALU.subtract, ALU.mult)
                ins.then_inc(xn_ready, 1)
                if i == 1:
                    dve.wait_ge(xn_ready, B * i + c + 1)
                    after(dve.tensor_tensor_reduce(sqj[:], xn[:, c % 3], xn[:, c % 3], 1.0, 0.0, ALU.mult, ALU.add,
                                                   ssq[:, c:c + 1]))

            for c in range(3) if b == 0 else (b + 2,):
                if c < B:
                    normalise(c)
            src = high(s)
            t = slice(b * S, (b + 1) * S)
            dve.tensor_tensor(xT[1][:, :, t], src[:, 0:2 * S].rearrange("p (k q) -> p k q", k=2),
                              xT[0][:, :, t].bitcast(F32), ALU.subtract).then_inc(split_done, 1)

        def queries_low(s):
            src = high(s)
            _, l, half, rt = s
            t = slice(half * HALF, (half + 1) * HALF)
            if l == 0:
                dve.tensor_tensor(qT[1][:, rt, t], src[:, 0:HALF], qT[0][:, rt, t].bitcast(F32), ALU.subtract)\
                    .then_inc(split_done, 1)
            else:
                dve.scalar_tensor_tensor(qT[1][:, rt, t], src[:, 0:HALF], colT[:, 8 + rt:9 + rt],
                                         qT[0][:, rt, t].bitcast(F32), ALU.add, ALU.subtract).then_inc(split_done, 1)

        def context_low(s):
            src = high(s)
            k = s[2]
            dve.tensor_tensor(cT[1][:, k, 0:NK], src[:, 0:NK], cT[0][:, k, 0:NK].bitcast(F32), ALU.subtract)\
                .then_inc(split_done, 1)

        def keys_low(s):
            src = high(s)
            _, n, rt = s
            hi, lo = kT[0][:, rt].bitcast(F32), kT[1][:, rt]
            if n < B:
                dve.tensor_tensor(lo, src[:, 0:NK + 1], hi, ALU.subtract).then_inc(split_done, 1)
            else:
                dve.scalar_tensor_tensor(lo, src[:, 0:NK + 1], colT[:, 10 + rt:11 + rt], hi, ALU.add, ALU.subtract)\
                    .then_inc(split_done, 1)

        def values_out(s):
            src = begin(s)
            _, n, t = s
            if n == 0 and t == 0:
                dve.wait_ge(pool_const, 1)
            dst = vA[n % 3][0:KT[t], t, :, 0:DH]
            v = src[0:KT[t], 0:D].rearrange("p (h d) -> p h d", h=H)
            if n < B:
                dve.tensor_copy(dst, v).then_inc(split_done, 1)
            else:
                dve.tensor_tensor(dst, v, bvb[0:KT[t], :].rearrange("p (h d) -> p h d", h=H), ALU.add)\
                    .then_inc(split_done, 1)

        def maxima(s):
            _, n, h = s
            x_ = H * n + h
            dve.wait_ge(sn_ready, x_ + 1)
            if n >= B and h == 0:
                dve.wait_ge(mrow_ready, n - B + 1)
            if x_ >= 2:
                dve.wait_ge(max_done, x_ - 1)
            add = fnat[:] if n < B else mrow[:, n % 2]
            dve.tensor_tensor_reduce(junk[:, x_ % 2], bank[2 + x_ % 3][0:S, 0:NK], add, 1.0, -3.0e38, ALU.add, ALU.max,
                                     mx[:, n % 2, h:h + 1]).then_inc(max_done, 1)
            if h == H - 1:
                dve.wait_ge(max_done, x_ + 1)
                dve.tensor_copy(mx[:, n % 2, 32:48], mx[:, n % 2, 0:16]).then_inc(max_twice, 1)

        def max_low(s):
            src = high(s)
            dve.scalar_tensor_tensor(nm[32:48], src[32:48, 0:S], -1.0, nm[32:48].bitcast(F32), ALU.mult, ALU.subtract)\
                .then_inc(split_done, 1)

        def normalise_heads(s):
            src = begin(s)
            v = src[0:S, 0:512].rearrange("p (h c) -> p h c", c=32)
            after(dve.reciprocal(rden[:], v[:, :, DH]))
            dve.tensor_tensor(an[:].rearrange("p (h d) -> p h d", h=H), v[:, :, 0:DH],
                              rden[:].unsqueeze(2).to_broadcast((S, H, DH)), ALU.mult).then_inc(split_done, 1)

        def out_low(s):
            src = high(s)
            dve.tensor_tensor(aT[1][:], src[:, 0:2 * S].rearrange("p (k q) -> p k q", k=2), aT[0][:].bitcast(F32),
                              ALU.subtract).then_inc(split_done, 1)

        def add_attention(s):
            src = begin(s)
            n = s[1]
            l, b = n // B, n % B
            dve.scalar_tensor_tensor(xres[:, b], src[0:S, 0:D], tg[0:S, l:l + 1], xres[:, b], ALU.mult, ALU.add)\
                .then_inc(split_done, 1)
            dve.wait_ge(split_done, job[s] + 1)
            if l == 1:
                after(dve.tensor_tensor(xres[:, b], xres[:, b], bob[:], ALU.add))
            after(dve.bn_stats(stats[:, b], xres[:, b]))
            after(dve.bn_aggr(mv[:, b], stats[:, b]))
            if b == B - 1:
                dve.tensor_copy(rs[:, 3], rs[:, 2]).then_inc(attn_done, 1)

        def prep_out(s):
            src = begin(s)
            if s[0] == "PB":
                after(dve.tensor_copy(colT[:], src[:, 0:12]))
                ins = dve.tensor_scalar(colT[:, 8:10], colT[:, 8:10], 0.25, None, ALU.mult)
            elif s[0] == "PM":
                for t in range(3):
                    ins = dve.tensor_copy(maskT[0:KT[t], t], src[0:KT[t], 8 * t:8 * t + 8])
            else:
                after(dve.tensor_copy(rt_raw[:, :, 0:16], src[:, 0:32].rearrange("p (k c) -> p k c", k=2)))
                after(dve.tensor_copy(rtw[0][:], rt_raw[:]))
                ins = dve.tensor_tensor(rtw[1][:], rt_raw[:], rtw[0][:].bitcast(F32), ALU.subtract)
            ins.then_inc(split_done, 1)

        def experts0_low(s):
            c = s[1]
            p = slice(2 * c, 2 * c + 2)
            dve.wait_ge(v_high, c + 1)
            dve.tensor_tensor(e0[1][:, :, p], e0_raw[:, :, p], e0[0][:, :, p].bitcast(F32), ALU.subtract).then_inc(v_split, 1)

        def router_out(s):
            src = begin(s)
            _, l, half = s
            wide = 16 if l == 0 else 8
            dve.tensor_copy(gT[0:wide, half * HALF:(half + 1) * HALF], src[0:wide, 0:HALF]).then_inc(split_done, 1)

        def choices(s):
            l = s[1]
            src = begin(s)
            wide = 16 if l == 0 else 8
            dve.tensor_copy(lg[:, :, 0:wide], src[0:S, 0:16 * B].rearrange("p (b c) -> p b c", b=B)[:, :, 0:wide])\
                .then_inc(split_done, 1)
            dve.wait_ge(split_done, job[s] + 1)
            z, top, low, _, pick, _, pr = (gw[:, i] for i in range(7))

            def wide_of(a):
                return a.to_broadcast((S, B, E))

            if l == 0:
                dve.tensor_scalar(rs[:, 0], ssq[:], 1e-24, None, ALU.max).then_inc(var_ready, 1)
                inverse_root(rs[:, 0], rs[:, 1], rs[:, 2])
                after(dve.tensor_tensor(z, lg[:, :, 0:8], wide_of(rs[:, 1].unsqueeze(2)), ALU.mult))
                after(dve.tensor_tensor(z, z, lg[:, :, 8:16], ALU.add))
            else:
                after(dve.tensor_tensor(z, lg[:, :, 0:8], wide_of(brb[:].unsqueeze(1)), ALU.add))
            for b in range(B):
                last = dve.max(top[:, b], z[:, b])
            after(last)
            dve.tensor_tensor(low, z, wide_of(top[:, :, 0:1]), ALU.subtract).then_inc(shifted, 1)
            if l == 0:
                after(dve.tensor_tensor(pick, z, wide_of(top[:, :, 1:2]), ALU.is_ge))
            else:
                for b in range(B):
                    last = dve.max_index(idx[:, b], top[:, b], z[:, b])
                after(last)
                after(dve.tensor_copy(pr, idx[:]))
                for c in range(TOP):
                    last = dve.tensor_tensor(pk[:, c], wide_of(iota8[:].unsqueeze(1)), wide_of(pr[:, :, c:c + 1]),
                                             ALU.is_equal)
                after(last)
                after(dve.tensor_tensor(pick, pk[:, 0], pk[:, 1], ALU.add))
                dve.tensor_copy(pkr[:], pick.rearrange("p b e -> p (b e)")).then_inc(counts_in, 1)

        def gates_of_choices(s):
            l = s[1]
            ex, pick, pick2 = (gw[:, i] for i in (3, 4, 5))
            dve.wait_ge(exp_gate, l + 1)
            after(dve.tensor_tensor(pick2, ex, pick, ALU.mult))
            after(dve.tensor_reduce(rs[:, 0], pick2, AX.X, ALU.add))
            after(dve.reciprocal(rs[:, 1], rs[:, 0]))
            after(dve.tensor_tensor(gate[:], pick2, rs[:, 1].unsqueeze(2).to_broadcast((S, B, E)), ALU.mult))
            dve.tensor_scalar(gate[:], gate[:], tg[0:S, 2 + l:3 + l], None, ALU.mult).then_inc(gates_ready, 1)
            dve.wait_ge(gates_ready, l + 1)
            if l == 1:
                scratch = gw[:, 1:3]
                for c in range(TOP):
                    last = dve.tensor_tensor(scratch[:, c], pk[:, c], gate[:], ALU.mult)
                after(last)
                after(dve.tensor_reduce(gk[:], scratch, AX.X, ALU.add))

        def gates_turned(s):
            src = begin(s)
            dve.tensor_copy(gT[0:E, s[2] * HALF:(s[2] + 1) * HALF], src[0:E, 0:HALF]).then_inc(split_done, 1)

        def add_bias(s):
            src = begin(s)
            b = s[2]
            dve.wait_ge(y_added, sum(t[0] == "Y0" for t in order[:order.index(s)]))
            dve.tensor_tensor(xres[:, b], src[0:S, 0:D], xres[:, b], ALU.add).then_inc(split_done, 1)
            dve.wait_ge(split_done, job[s] + 1)

        def add_expert(j, src, e, b):
            dve.wait_ge(y_ready, j + 1)
            if j >= B:
                dve.wait_ge(y_added, j - B + 1)
            dve.scalar_tensor_tensor(xres[:, b], src[0:S, 0:D], gate[:, b, e:e + 1], xres[:, b], ALU.mult, ALU.add)\
                .then_inc(y_added, 1)

        def hidden0_low(s):
            i = 2 * s[1] + s[2]
            dve.wait_ge(h_high, i + 1)
            dve.tensor_tensor(h0s[1][:, i % 2], h0[:, i % 2], h0s[0][:, i % 2].bitcast(F32), ALU.subtract)\
                .then_inc(h_split, 1)

        def output0(s):
            _, e, b = s
            j = 4 * (2 * e + b // 4) + b % 4
            add_expert(j, bank[3 + j % 3], e, b)
            if j == Y0N - 1:
                dve.wait_ge(y_added, Y0N)

        def biases1_low(s):
            dve.wait_ge(b_high, 1)
            dve.tensor_tensor(bsp[1][:], bnat[:], bsp[0][:].bitcast(F32), ALU.subtract).then_inc(b_split, 1)

        def experts1_low(s):
            _, j, c = s
            if c in POOL_PIECES:
                return
            dve.wait_ge(r_high, 6 * j + c + 1)
            dve.tensor_tensor(e1[j % 2][1][:, c], e1_raw[:, c], e1[j % 2][0][:, c].bitcast(F32), ALU.subtract)\
                .then_inc(r_split, 1)

        def place_choices(s):
            src = begin(s)
            dve.tensor_copy(cnt[:].rearrange("p m b e -> p (m b e)"), src[0:S, 0:2 * B * E]).then_inc(split_done, 1)
            dve.memset(off[:, 0], 0.0)
            dve.wait_ge(split_done, job[s] + 1)
            after(dve.tensor_copy(off[:, 1], cnt[:, 1, 0]))
            for b in range(1, B):
                after(dve.tensor_tensor(off[:, b + 1], off[:, b], cnt[:, 1, b], ALU.add))
            after(dve.tensor_tensor(cmp7[:], off[:, B].unsqueeze(2).to_broadcast((S, E, 7)),
                                    mult128[:].unsqueeze(1).to_broadcast((S, E, 7)), ALU.is_gt))
            after(dve.tensor_reduce(tl[:, 0], cmp7[:], AX.X, ALU.add))
            after(dve.tensor_tensor(tri8m[:], tl[:, 0].unsqueeze(1).to_broadcast((S, E, E)), tri8[:], ALU.mult))
            after(dve.tensor_reduce(tl[:, 1], tri8m[:], AX.X, ALU.add))
            after(dve.tensor_tensor(cmpt[:], tl[0:1, 1, 0:E - 1].unsqueeze(1).to_broadcast((1, TILES, E - 1)),
                                    tile_no[:].unsqueeze(2).to_broadcast((1, TILES, E - 1)), ALU.is_le))
            dve.memset(tex[:, 1], 1.0)
            after(dve.tensor_reduce(tex[:, 0], cmpt[:], AX.X, ALU.add))
            after(dve.tensor_tensor(tex[:, 1, 1:TILES], tex[:, 0, 1:TILES], tex[:, 0, 0:TILES - 1], ALU.not_equal))
            dve.tensor_copy(texi[:], tex[:]).then_inc(experts_known, 1)
            after(dve.tensor_tensor(tl[:, 2], tl[:, 1], tl[:, 0], ALU.subtract))
            after(dve.tensor_scalar(tl[:, 3], tl[:, 2], 128.0, None, ALU.mult))
            after(dve.tensor_tensor(pos[:], cnt[:, 0], off[:, 0:B], ALU.add))
            after(dve.tensor_tensor(pos[:], pos[:], tl[:, 3].unsqueeze(1).to_broadcast((S, B, E)), ALU.add))
            scratch = gw[:, 1:3]
            dve.wait_ge(exp_gate, 2)
            for c in range(TOP):
                last = dve.tensor_tensor(scratch[:, c], pk[:, c], pos[:], ALU.mult)
            after(last)
            after(dve.tensor_reduce(posk[:], scratch, AX.X, ALU.add))
            dve.tensor_copy(slot[:], posk[:]).then_inc(slots_ready, 1)
            dve.wait_ge(slots_ready, 1)

        def rows_low(s):
            src = high(s)
            j = s[1]
            dve.tensor_tensor(xst[j % 2][1][:], src[:, 0:D].rearrange("p (k q) -> p k q", k=2),
                              xst[j % 2][0][:].bitcast(F32), ALU.subtract).then_inc(split_done, 1)

        def hidden1(s):
            _, j, m = s
            i = 2 * j + m
            dve.wait_ge(h_act, R16 + i + 1)
            dve.tensor_tensor(h1f[:, m], bank[2 * m + 1][:], h1f[:, m], ALU.mult).then_inc(h_made, 1)

        def hidden_low(s):
            _, j, m = s
            dve.wait_ge(h_high, R16 + 2 * j + m + 1)
            f = slice(4 * m, 4 * m + 4)
            dve.tensor_tensor(h1s[j % 2][1][:, f], bank[4 + m][:].rearrange("p (f q) -> p f q", f=4),
                              h1s[j % 2][0][:, f].bitcast(F32), ALU.subtract).then_inc(h_split, 1)

        def output1(s):
            src = begin(s)
            j = s[1]
            if j >= 2:
                dve.wait_ge(y_stored[j % 2], 16 * (j // 2))
            dve.tensor_copy(yo[:, j % 2], src[:, 0:D]).then_inc(split_done, 1)

        def combine(s):
            for b in range(B):
                dve.wait_ge(gathered[b], 16 * TOP)
                for c in range(TOP):
                    ins = dve.scalar_tensor_tensor(xres[:, b], yk[:, c, b], gk[:, c, b:b + 1], xres[:, b], ALU.mult,
                                                   ALU.add)
                    if c == 0:
                        after(ins)
                ins.then_inc(moe_done, 1)

        what = {"AW": attention_weights, "PR": prepare, "PB": prep_out, "PM": prep_out, "PF": prep_out, "PC": prep_out,
                "LS": norm_stats, "LX": norm_low, "Q": queries_low, "CT": context_low, "KP": keys_low,
                "VP": values_out, "SN": maxima, "MT": max_low, "O1": normalise_heads,
                "O2": out_low, "O3": add_attention, "V": experts0_low, "RL": router_out, "R": choices, "G": gates_of_choices, "GT": gates_turned,
                "GB": add_bias, "HS": hidden0_low, "Y0": output0, "Y1": output1, "W": experts1_low, "HP": hidden1,
                "BB": biases1_low, "PS": place_choices, "XT": rows_low, "HT": hidden_low, "GA": combine}
        for s in order:
            if s[0] in what:
                what[s[0]](s)

    st.close()


_INS = ["x", "ctx_1024", "fside_1x1xSxS2_0", "mask_Bx1x1xS2_ik0", "g_xattn", "g_ffn",
        "L0_xattn_wq", "L0_xattn_wk", "L0_xattn_wv", "L0_xattn_wo",
        "L0_ffn_w1", "L0_ffn_b1", "L0_ffn_w2", "L0_ffn_b2", "L0_ffn_centroids", "L0_ffn_w_route",
        "L1_xattn_wq", "L1_xattn_bq", "L1_xattn_wk", "L1_xattn_bk", "L1_xattn_wv", "L1_xattn_bv",
        "L1_xattn_wo", "L1_xattn_bo",
        "L1_ffn_Wr", "L1_ffn_br", "L1_ffn_W1", "L1_ffn_b1", "L1_ffn_W2", "L1_ffn_b2", "L1_ffn_W3", "L1_ffn_b3"]


def kernel(**inputs):
    import numpy as _np
    import concourse.bacc as _bacc
    from concourse import mybir as _mybir
    from concourse.bass_utils import run_bass_kernel_spmd as _run

    nc = _bacc.Bacc("TRN2", target_bir_lowering=False, num_devices=1)
    arrays, aps = {}, {}
    for name in _INS:
        a = _np.ascontiguousarray(inputs[name])
        if name in ("L0_xattn_wq", "L0_xattn_wk", "L0_xattn_wv", "L0_xattn_wo"):
            a = a.reshape(D, D)
        arrays[f"in_{name}_dram"] = a
        aps[name] = nc.dram_tensor(f"in_{name}_dram", a.shape, _mybir.dt.from_np(a.dtype), kind="ExternalInput").ap()
    out = nc.dram_tensor("out_0_dram", (B, S, D), F32, kind="ExternalOutput").ap()

    def part(prefix):
        return {name[len(prefix):]: ap for name, ap in aps.items() if name.startswith(prefix)}

    gated_layers(nc, aps["x"], aps["ctx_1024"], aps["fside_1x1xSxS2_0"], aps["mask_Bx1x1xS2_ik0"], aps["g_xattn"],
                 aps["g_ffn"], part("L0_xattn_"), part("L0_ffn_"), part("L1_xattn_"), part("L1_ffn_"), out)
    r = _run(nc, [arrays], core_ids=[0])
    return r.results[0]["out_0_dram"]
```
